# Optimizing a Trainium2 kernel written in Bass

```python
import numpy as np
import jax
import jax.numpy as jnp

def _softmax(x, axis=-1):
    return jax.nn.softmax(x, axis=axis)

def _gelu(x):
    return jax.nn.gelu(x, approximate=True)

def _silu(x):
    return jax.nn.silu(x)

def _sigmoid(x):
    return jax.nn.sigmoid(x)

def _layernorm(x, axis=-1, eps=1e-05):
    m = jnp.mean(x, axis=axis, keepdims=True)
    v = jnp.var(x, axis=axis, keepdims=True)
    return (x - m) / jnp.sqrt(v + eps)

def _scatter_add(tgt, idx, src, axis=0):
    return tgt.at[idx].add(src)

def _segment_sum(src, seg, n):
    return jax.ops.segment_sum(src, seg, n)
kernel_name = 'mk_gnn_preln_d4_gnn_r64_d0ae34'

def setup_inputs(seed: int=0):
    np.random.seed(seed)
    _w = jnp.asarray

    def _rec_inputs():
        import jax
        import jax.numpy as jnp
        _gk = jax.random.key(seed)
        x = -0.0005121 + 1.001 * jax.random.normal(jax.random.fold_in(_gk, 1), (50000, 64), jnp.float32)
        src = jax.random.randint(jax.random.fold_in(_gk, 2), (25000,), 0, 50000, jnp.int32)
        dst = jnp.minimum((50000 * jax.random.uniform(jax.random.fold_in(_gk, 3), (25000,)) ** 2.0).astype(jnp.int32), 49999)
        _o = jnp.argsort(dst, stable=True)
        src = src[_o]
        dst = dst[_o]
        edge_attr_32 = -5.3897e-05 + 0.999841 * jax.random.normal(jax.random.fold_in(_gk, 12), (25000, 32), jnp.float32)
        edge_type_32 = jax.random.randint(jax.random.fold_in(_gk, 14), (25000,), 0, 32, jnp.int32)
        return (x, src, dst, edge_attr_32, edge_type_32)
    x, src, dst, edge_attr_32, edge_type_32 = _rec_inputs()

    def _L0_gnn_setup():
        import jax, jax.numpy as jnp
        import numpy as np
        N, E = (50000, 12500)
        NODE_DIM, EDGE_DIM, HIDDEN = (64, 32, 128)

        def _glorot(key, shape):
            fan_in = shape[0]
            bound = 1.0 / np.sqrt(fan_in)
            return jax.random.uniform(key, shape, jnp.float32, -bound, bound)
        key = jax.random.key(seed)
        ks = jax.random.split(key, 12)
        node_feats = jax.random.normal(ks[0], (N, NODE_DIM), jnp.float32)
        edge_feats = jax.random.normal(ks[1], (E, EDGE_DIM), jnp.float32)
        edge_index = jax.random.randint(ks[2], (2, E), 0, N, jnp.int64)
        msg_in = 2 * NODE_DIM + EDGE_DIM
        upd_in = NODE_DIM + HIDDEN
        return {'node_feats': node_feats, 'edge_feats': edge_feats, 'edge_index': edge_index, 'w_m1': _glorot(ks[3], (msg_in, HIDDEN)), 'b_m1': jnp.zeros((HIDDEN,), jnp.float32), 'w_m2': _glorot(ks[4], (HIDDEN, HIDDEN)), 'b_m2': jnp.zeros((HIDDEN,), jnp.float32), 'w_u1': _glorot(ks[5], (upd_in, HIDDEN)), 'b_u1': jnp.zeros((HIDDEN,), jnp.float32), 'w_u2': _glorot(ks[6], (HIDDEN, NODE_DIM)), 'b_u2': jnp.zeros((NODE_DIM,), jnp.float32)}
    _L0_gnn_all = _L0_gnn_setup()
    _L0_gnn_in = {k: v for k, v in _L0_gnn_all.items() if k in ('w_m1', 'b_m1', 'w_m2', 'b_m2', 'w_u1', 'b_u1', 'w_u2', 'b_u2')}
    del _L0_gnn_all

    def _L1_gnn_setup():
        import jax, jax.numpy as jnp
        import numpy as np
        N_NODES = 100000
        N_EDGES = 15625
        IN_F = 64
        OUT_F = 64
        N_REL = 32
        N_BASES = 30
        key = jax.random.key(seed)
        k = jax.random.split(key, 8)
        node_features = jax.random.normal(k[0], (N_NODES, IN_F), dtype=jnp.float32)
        senders = jax.random.randint(k[1], (N_EDGES,), 0, N_NODES, dtype=jnp.int32)
        receivers = jax.random.randint(k[2], (N_EDGES,), 0, N_NODES, dtype=jnp.int32)
        relation_types = jax.random.randint(k[3], (N_EDGES,), 0, N_REL, dtype=jnp.int32)
        basis = jax.random.normal(k[4], (N_BASES, IN_F, OUT_F), dtype=jnp.float32) * 0.01
        coeff = jax.random.normal(k[5], (N_REL, N_BASES), dtype=jnp.float32) * 0.01
        self_weight = jax.random.normal(k[6], (IN_F, OUT_F), dtype=jnp.float32) * 0.01
        bias = jnp.zeros((OUT_F,), dtype=jnp.float32)
        return {'node_features': node_features, 'senders': senders, 'receivers': receivers, 'relation_types': relation_types, 'basis': basis, 'coeff': coeff, 'self_weight': self_weight, 'bias': bias}
    _L1_gnn_all = _L1_gnn_setup()
    _L1_gnn_in = {k: v for k, v in _L1_gnn_all.items() if k in ('basis', 'coeff', 'self_weight', 'bias')}
    del _L1_gnn_all

    def _L2_gnn_setup():
        import jax, jax.numpy as jnp
        import numpy as np
        N = 100000
        E = 25000
        D = 64
        EPS = 1e-12
        key = jax.random.key(seed)
        k1, k2, k3 = jax.random.split(key, 3)
        H = jax.random.normal(k1, (N, D), dtype=jnp.float32)
        row = jnp.sort(jax.random.randint(k2, (E,), 0, N, dtype=jnp.int64))
        col = jax.random.randint(k3, (E,), 0, N, dtype=jnp.int64)
        return {'H': H, 'row': row, 'col': col, 'num_nodes': N}
    _L2_gnn_all = _L2_gnn_setup()
    _L2_gnn_in = {k: v for k, v in _L2_gnn_all.items() if k in ()}
    del _L2_gnn_all

    def _L3_gnn_setup():
        import jax, jax.numpy as jnp
        import numpy as np
        N_CON = 100000
        NUM_VAR = 100000
        E = 1250000
        H = 64
        key = jax.random.key(seed)
        ks = jax.random.split(key, 6)
        x_con = jax.random.normal(ks[0], (N_CON, H), dtype=jnp.float32)
        src = jax.random.randint(ks[1], (E,), 0, N_CON, dtype=jnp.int32)
        dst = jax.random.randint(ks[2], (E,), 0, NUM_VAR, dtype=jnp.int32)
        W = jax.random.normal(ks[3], (H, H), dtype=jnp.float32) * (1.0 / np.sqrt(H))
        b = jax.random.normal(ks[4], (H,), dtype=jnp.float32) * 0.02
        gamma = jnp.ones((H,), dtype=jnp.float32)
        beta = jnp.zeros((H,), dtype=jnp.float32)
        return {'x_con': x_con, 'src': src, 'dst': dst, 'num_var': NUM_VAR, 'W': W, 'b': b, 'gamma': gamma, 'beta': beta}
    _L3_gnn_all = _L3_gnn_setup()
    _L3_gnn_in = {k: v for k, v in _L3_gnn_all.items() if k in ('W', 'b', 'gamma', 'beta')}
    del _L3_gnn_all
    return {'x': x, 'src': src, 'dst': dst, 'edge_attr_32': edge_attr_32, 'edge_type_32': edge_type_32, 'L0_gnn_w_m1': _L0_gnn_in['w_m1'], 'L0_gnn_b_m1': _L0_gnn_in['b_m1'], 'L0_gnn_w_m2': _L0_gnn_in['w_m2'], 'L0_gnn_b_m2': _L0_gnn_in['b_m2'], 'L0_gnn_w_u1': _L0_gnn_in['w_u1'], 'L0_gnn_b_u1': _L0_gnn_in['b_u1'], 'L0_gnn_w_u2': _L0_gnn_in['w_u2'], 'L0_gnn_b_u2': _L0_gnn_in['b_u2'], 'L1_gnn_basis': _L1_gnn_in['basis'], 'L1_gnn_coeff': _L1_gnn_in['coeff'], 'L1_gnn_self_weight': _L1_gnn_in['self_weight'], 'L1_gnn_bias': _L1_gnn_in['bias'], 'L3_gnn_W': _L3_gnn_in['W'], 'L3_gnn_b': _L3_gnn_in['b'], 'L3_gnn_gamma': _L3_gnn_in['gamma'], 'L3_gnn_beta': _L3_gnn_in['beta']}

def reference(x, src, dst, edge_attr_32, edge_type_32, L0_gnn_w_m1, L0_gnn_b_m1, L0_gnn_w_m2, L0_gnn_b_m2, L0_gnn_w_u1, L0_gnn_b_u1, L0_gnn_w_u2, L0_gnn_b_u2, L1_gnn_basis, L1_gnn_coeff, L1_gnn_self_weight, L1_gnn_bias, L3_gnn_W, L3_gnn_b, L3_gnn_gamma, L3_gnn_beta):
    import jax
    import jax.numpy as jnp

    def _L0_gnn_ref(node_feats, edge_feats, edge_index, w_m1, b_m1, w_m2, b_m2, w_u1, b_u1, w_u2, b_u2):
        import jax, jax.numpy as jnp
        import numpy as np
        N, E = (50000, 12500)
        NODE_DIM, EDGE_DIM, HIDDEN = (64, 32, 128)

        def _glorot(key, shape):
            fan_in = shape[0]
            bound = 1.0 / np.sqrt(fan_in)
            return jax.random.uniform(key, shape, jnp.float32, -bound, bound)
        src_idx = edge_index[0]
        tgt_idx = edge_index[1]
        msg_in = jnp.concatenate([node_feats[src_idx], node_feats[tgt_idx], edge_feats], axis=1)
        h = jax.nn.relu(msg_in @ w_m1 + b_m1)
        messages = h @ w_m2 + b_m2
        aggregated = jax.ops.segment_sum(messages, tgt_idx, num_segments=node_feats.shape[0])
        upd_in = jnp.concatenate([node_feats, aggregated], axis=1)
        u = jax.nn.relu(upd_in @ w_u1 + b_u1)
        node_updates = u @ w_u2 + b_u2
        return node_feats + node_updates

    def _L1_gnn_ref(node_features, senders, receivers, relation_types, basis, coeff, self_weight, bias):
        import jax, jax.numpy as jnp
        import numpy as np
        N_NODES = 100000
        N_EDGES = 15625
        IN_F = 64
        OUT_F = 64
        N_REL = 32
        N_BASES = 30
        num_nodes = node_features.shape[0]
        n_edges = senders.shape[0]
        rel_weights = jnp.einsum('rb,bio->rio', coeff, basis)
        src_features = node_features[senders]
        seg_ids = receivers * N_REL + relation_types
        agg = jax.ops.segment_sum(src_features, seg_ids, num_segments=num_nodes * N_REL)
        agg = agg.reshape(num_nodes, N_REL, node_features.shape[1])
        aggregated = jnp.einsum('nri,rio->no', agg, rel_weights)
        ones = jnp.ones((n_edges,), dtype=node_features.dtype)
        in_degree = jax.ops.segment_sum(ones, receivers, num_segments=num_nodes)
        in_degree = jnp.maximum(in_degree, 1.0)
        out = aggregated / in_degree[:, None]
        out = out + node_features @ self_weight
        out = out + bias
        return out

    def _L2_gnn_ref(H, row, col, num_nodes):
        import jax, jax.numpy as jnp
        import numpy as np
        N = 100000
        E = 25000
        D = 64
        EPS = 1e-12
        norm = jnp.sqrt(jnp.sum(H * H, axis=1, keepdims=True))
        Hn = H / jnp.maximum(norm, EPS)
        scores = jnp.sum(Hn[row] * Hn[col], axis=1)
        m = jax.ops.segment_max(scores, row, num_segments=num_nodes)
        e = jnp.exp(scores - m[row])
        s = jax.ops.segment_sum(e, row, num_segments=num_nodes)
        attn = e / s[row]
        out = jax.ops.segment_sum(attn[:, None] * H[col], row, num_segments=num_nodes)
        return out

    def _L3_gnn_ref(x_con, src, dst, num_var, W, b, gamma, beta):
        import jax, jax.numpy as jnp
        import numpy as np
        N_CON = 100000
        NUM_VAR = 100000
        E = 1250000
        H = 64
        msg = x_con[src] @ W.T + b
        deg = jnp.zeros((num_var,), dtype=msg.dtype).at[dst].add(1.0)
        agg = jnp.zeros((num_var, msg.shape[1]), dtype=msg.dtype).at[dst].add(msg)
        agg = agg / (deg[:, None] + 1e-06)
        h = jax.nn.relu(agg)
        mu = jnp.mean(h, axis=-1, keepdims=True)
        var = jnp.mean((h - mu) ** 2, axis=-1, keepdims=True)
        return (h - mu) * jax.lax.rsqrt(var + 1e-05) * gamma + beta
    edge_index = jnp.stack([src, dst])
    h = jnp.maximum(_layernorm(x, axis=-1), 0.0)
    x = x + _L0_gnn_ref(h, edge_attr_32, edge_index, L0_gnn_w_m1, L0_gnn_b_m1, L0_gnn_w_m2, L0_gnn_b_m2, L0_gnn_w_u1, L0_gnn_b_u1, L0_gnn_w_u2, L0_gnn_b_u2)
    h = jnp.maximum(_layernorm(x, axis=-1), 0.0)
    x = x + _L1_gnn_ref(h, src, dst, edge_type_32, L1_gnn_basis, L1_gnn_coeff, L1_gnn_self_weight, L1_gnn_bias)
    h = jnp.maximum(_layernorm(x, axis=-1), 0.0)
    x = x + _L2_gnn_ref(h, src, dst, 50000)
    h = jnp.maximum(_layernorm(x, axis=-1), 0.0)
    x = x + _L3_gnn_ref(h, src, dst, 50000, L3_gnn_W, L3_gnn_b, L3_gnn_gamma, L3_gnn_beta)
    return x

_drawn_inputs = setup_inputs


def setup_inputs(seed=0):
    import zlib

    import numpy as np

    out = dict(_drawn_inputs(seed))
    spreads = {'L0_gnn_b_m1': (0.0, 0.8),
     'L0_gnn_b_m2': (0.0, 0.398),
     'L0_gnn_b_u1': (0.0, 0.269),
     'L0_gnn_b_u2': (0.0, 0.1),
     'L1_gnn_bias': (0.0, 0.1),
     'L3_gnn_gamma': (1.0, 0.2),
     'L3_gnn_beta': (0.0, 0.1)}
    factors = {'edge_attr_32': 6.893,
     'L0_gnn_w_m1': 2.984,
     'L1_gnn_basis': 8.0,
     'L1_gnn_coeff': 8.0,
     'L3_gnn_b': 4.764}
    for name, (base, spread) in spreads.items():
        noise = np.random.default_rng([zlib.crc32(name.encode()), seed]).standard_normal(out[name].shape)
        drawn = base * np.exp(spread * noise) if base else spread * noise
        out[name] = jnp.asarray(drawn.astype(out[name].dtype))
    for name, factor in factors.items():
        out[name] = (out[name] * factor).astype(out[name].dtype)
    return out
```

```python
from contextlib import ExitStack

import concourse.bass as bass
from concourse import mybir
from concourse.alu_op_type import AluOpType as ALU

ACT = mybir.ActivationFunctionType
F32 = mybir.dt.float32
BF16 = mybir.dt.bfloat16
I32 = mybir.dt.int32
AX = mybir.AxisListType

P = 128
NODES = 50000
EDGES = 25000
D = 64
ED = 32
H = 128
RELS = 32
BASES = 30

TG = 4
GS = TG * P
EG = -(-EDGES // GS)
SLOTS = EG * GS
ET = SLOTS // P
PAD = SLOTS - EDGES
ROWS = ET // 2
FAR = 65536

NP = 125
NPP = NODES // NP
NG = 8
DG = NPP // NG
HALF = NG // 2 * NP

SUM_ROWS = -(-(NODES + GS) // P) * P
CLEAR = SUM_ROWS // P * (D + 1) // 25
TINY = 1e-30
LN_EPS = 1e-5
COUNT_CHUNK = SLOTS // 7


class Group:

    def __init__(self, pair, off):
        self.pair, self.off = pair, off

    def __sub__(self, k):
        return Group(self.pair, self.off - k)

    def __add__(self, k):
        return Group(self.pair, self.off + k)

    @property
    def n(self):
        return self.pair * 2 + self.off

    @property
    def half(self):
        return self.pair + self.off // 2

    @property
    def buf(self):
        return self.off % 2

    def within(self, count):
        return not isinstance(self.pair, int) or 0 <= self.off < count

    def from_first(self):
        return not isinstance(self.pair, int) or self.off >= 1

    def from_second(self):
        return not isinstance(self.pair, int) or self.off >= 2


def rounds(eng, groups, skew, step):
    first = (skew + 3) // 2 * 2
    last = groups // 2 * 2
    for r in range(first):
        step(Group(0, r))
    with eng.Fori(first // 2, last // 2) as pair:
        step(Group(pair, 0))
        step(Group(pair, 1))
    for r in range(last, groups + skew):
        step(Group(0, r))


def center_rows(vec, done, n, rows, total, centered):
    vec.tensor_reduce(total, rows, AX.X, ALU.add).then_inc(done, 1)
    vec.wait_ge(done, n + 1)
    vec.scalar_tensor_tensor(out=centered, in0=rows, scalar=float(D),
                             in1=total.unsqueeze(2).to_broadcast(list(centered.shape)),
                             op0=ALU.mult, op1=ALU.subtract).then_inc(done, 1)


def scale_rows(vec, done, centered, inverse, out, relu=True):
    scale = inverse.unsqueeze(2).to_broadcast(list(out.shape))
    if relu:
        vec.scalar_tensor_tensor(out=out, in0=centered, scalar=0.0, in1=scale,
                                 op0=ALU.max, op1=ALU.mult).then_inc(done, 1)
    else:
        vec.tensor_tensor(out, centered, scale, ALU.mult).then_inc(done, 1)


class Shared:
    pass


def build(nc, x, src, dst, attr, etype, w_m1, b_m1, w_m2, b_m2, w_u1, b_u1, w_u2, b_u2,
          basis, coeff_t, w_self, b_rel, w3_t, b3, gamma, beta, out):
    k = Shared()
    k.x, k.src, k.dst, k.attr, k.etype = x, src, dst, attr, etype
    k.w_m1, k.b_m1, k.w_m2, k.b_m2, k.w_u1, k.b_u1, k.w_u2, k.b_u2 = w_m1, b_m1, w_m2, b_m2, w_u1, b_u1, w_u2, b_u2
    k.basis, k.coeff_t, k.w_self, k.b_rel = basis, coeff_t, w_self, b_rel
    k.w3_t, k.b3, k.gamma, k.beta, k.out = w3_t, b3, gamma, beta, out
    k.src_s = nc.dram_tensor("src_s", [SLOTS, 1], I32)
    k.dst_s = nc.dram_tensor("dst_s", [SLOTS + 2, 1], I32)
    k.typ_s = nc.dram_tensor("typ_s", [SLOTS, 1], I32)
    k.attr_s = nc.dram_tensor("attr_s", [SLOTS, ED], F32)
    k.src_r = nc.dram_tensor("src_r", [SLOTS, 1], I32)
    k.dst_r = nc.dram_tensor("dst_r", [SLOTS, 1], I32)
    k.typ_r = nc.dram_tensor("typ_r", [SLOTS, 1], I32)
    k.attr_r = nc.dram_tensor("attr_r", [SLOTS, ED], F32)
    k.same_row = nc.dram_tensor("same_row", [SLOTS], BF16)
    k.type_row = nc.dram_tensor("type_row", [SLOTS], F32)
    k.src_row = nc.dram_tensor("src_row", [SLOTS], F32)
    k.rel_rows = nc.dram_tensor("rel_rows", [RELS, D * D], F32)
    k.x1_table = nc.dram_tensor("x1_table", [NODES, D], F32)
    k.x2_table = nc.dram_tensor("x2_table", [NODES, D], F32)
    k.sum_table = nc.dram_tensor("sum_table", [SUM_ROWS, D + 1], F32)

    with ExitStack() as ctx:
        def sb(name, shape, dt=F32, stack=ctx):
            return stack.enter_context(nc.sbuf_tensor(name, shape, dt))

        def sem(name, stack=ctx):
            return stack.enter_context(nc.semaphore(name))

        def pair_of_sems(name, stack=ctx):
            return [sem(name + "0", stack), sem(name + "1", stack)]

        k.sb, k.sem, k.pair_of_sems = sb, sem, pair_of_sems

        k.bank = [ctx.enter_context(nc.psum_tensor(f"bank{i}", [P, 512], F32)) for i in range(8)]

        k.slots = sb("slots", [P, 2 * ET * D])
        k.x_dst = k.slots[:, 0:ET * D].rearrange("p (t d) -> p t d", d=D)
        k.x_src = k.slots[:, ET * D:2 * ET * D].rearrange("p (t d) -> p t d", d=D)
        k.same = sb("same", [P, SLOTS], BF16)
        k.src_idx = sb("src_idx", [P, ET], I32)
        k.dst_idx = sb("dst_idx", [P, ET], I32)
        k.last_idx = sb("last_idx", [P, ET], I32)
        k.first_idx = sb("first_idx", [P, ET], I32)
        k.src_key = sb("src_key", [P, ET])
        k.degree = sb("degree", [P, ET])
        k.ident = sb("ident", [P, P])
        k.ones_row = sb("ones_row", [1, P])
        k.eps_col = sb("eps_col", [P, 1])
        k.wm1 = sb("wm1", [P, H])
        k.wm1e = sb("wm1e", [ED, H])
        k.wm2 = sb("wm2", [P, H])
        k.wu1x = sb("wu1x", [P, H])
        k.wu1a = sb("wu1a", [P, H])
        k.wu2 = sb("wu2", [P, D])
        k.wself = sb("wself", [D, D])
        k.w3 = sb("w3", [D, D])
        k.relcol = sb("relcol", [P, RELS // 2])
        k.bm1 = sb("bm1", [P, 1])
        k.bm2 = sb("bm2", [P, 1])
        k.bu1 = sb("bu1", [P, 1])
        k.b3c = sb("b3c", [D, 1])
        k.bu2_row = sb("bu2_row", [1, D])
        k.brel_row = sb("brel_row", [1, D])
        k.gamma_b = sb("gamma_b", [P, D])
        k.beta_b = sb("beta_b", [P, D])

        prepare(nc, k)
        dense(nc, k)
        layer0(nc, k)
        layer1(nc, k)
        layer2(nc, k)
        layer3(nc, k)
        write_last(nc, k)


def prepare(nc, k):
    with ExitStack() as ctx:
        def sb(name, shape, dt=F32):
            return k.sb(name, shape, dt, ctx)

        def sem(name):
            return k.sem(name, ctx)

        zero_attr = sb("zero_attr", [PAD, ED])
        zero_pad = sb("zero_pad", [1, PAD], I32)
        src_pad = sb("src_pad", [1, PAD], I32)
        dst_pad = sb("dst_pad", [1, PAD + 2], I32)
        cur_i = sb("cur_i", [ROWS, 2, P], I32)
        prev_i = sb("prev_i", [ROWS, 2, P], I32)
        next_i = sb("next_i", [ROWS, 2, P], I32)
        src_i = sb("src_i", [ROWS, 2, P], I32)
        typ_i = sb("typ_i", [ROWS, 2, P], I32)
        cur = sb("cur", [ROWS, 2, P])
        prev = sb("prev", [ROWS, 2, P])
        nxt = sb("nxt", [ROWS, 2, P])
        srcf = sb("srcf", [ROWS, 2, P])
        typf = sb("typf", [ROWS, 2, P])
        same_t = sb("same_t", [ROWS, 2, P], BF16)
        gath = sb("gath", [ROWS, 2, P])
        src_in = sb("src_in", [ROWS, 2, P])
        scat = sb("scat", [ROWS, 2, P])
        falls = sb("falls", [ROWS, 2 * P])
        falls_sum = sb("falls_sum", [ROWS, 1])
        ones_col = sb("ones_col", [P, 1])
        flag = sb("flag", [1, 1], I32)
        rel_iota = sb("rel_iota", [P, RELS // 2], I32)
        coeff = sb("coeff", [BASES, RELS])
        room = k.same[:, :].bitcast(F32)
        basis_t = room[0:BASES, 0:D * D]
        rel = room[0:RELS, D * D:2 * D * D]
        junk = k.same[:, 4 * D * D:4 * D * D + COUNT_CHUNK]
        tri = sb("tri", [P, P])
        own = sb("own", [P, P])
        counts = sb("counts", [P, SLOTS // COUNT_CHUNK + 1])
        tile_dst_i = sb("tile_dst_i", [P, 1], I32)
        tile_src_i = sb("tile_src_i", [P, 1], I32)
        tile_typ_i = sb("tile_typ_i", [P, 1], I32)
        tile_attr = sb("tile_attr", [P, ED])
        tile_dst = sb("tile_dst", [P, 1])
        tile_half = sb("tile_half", [P, 1])
        rank = sb("rank", [P, 1])
        rank_i = sb("rank_i", [P, 1], I32)

        pads = sem("pads")
        copied = sem("copied")
        order_in = sem("order_in")
        order_v = sem("order_v")
        falls_added = sem("falls_added")
        flag_ready = sem("flag_ready")
        weights_in = sem("weights_in")
        arrays_in = sem("arrays_in")
        arrays_v = sem("arrays_v")
        turned = sem("turned")
        idx_ready = sem("idx_ready")
        rows_out = sem("rows_out")
        same_in = sem("same_in")
        consts = sem("consts")
        coeff_in = sem("coeff_in")
        rel_mm = sem("rel_mm")
        rel_copied = sem("rel_copied")
        rel_out = sem("rel_out")
        wide_in = sem("wide_in")
        wide_v = sem("wide_v")
        tile_in = sem("tile_in")
        rank_v = sem("rank_v")
        ranked_out = sem("ranked_out")
        rank_wait = sem("rank_wait")
        back = sem("back")

        STEPS = SLOTS // COUNT_CHUNK * 2 + 7
        wide = k.slots[:, 0:SLOTS]

        def square(a, first=0):
            return a[first:first + SLOTS, 0].rearrange("(a q f) -> q a f", a=2, f=P)

        with nc.Block() as block:
            @block.sync
            def _(sp):
                sp.dma_start(k.dst_s[1:1 + EDGES, 0].rearrange("(a b) -> a b", a=200),
                             k.dst.rearrange("(a b) -> a b", a=200)).then_inc(copied, 16)
                sp.wait_ge(pads, 5)
                sp.dma_start(k.dst_s[0:1, :].rearrange("a b -> b a"), dst_pad[:, 0:1]).then_inc(copied, 16)
                sp.dma_start(k.dst_s[1 + EDGES:SLOTS + 2, :].rearrange("a b -> b a"),
                             dst_pad[:, 1:PAD + 2]).then_inc(copied, 16)
                sp.dma_start(k.src_s[0:EDGES, 0].rearrange("(a b) -> a b", a=200),
                             k.src.rearrange("(a b) -> a b", a=200)).then_inc(copied, 16)
                sp.dma_start(k.typ_s[0:EDGES, 0].rearrange("(a b) -> a b", a=200),
                             k.etype.rearrange("(a b) -> a b", a=200)).then_inc(copied, 16)
                sp.dma_start(k.src_s[EDGES:SLOTS, :].rearrange("a b -> b a"), src_pad[:, :]).then_inc(copied, 16)
                sp.dma_start(k.typ_s[EDGES:SLOTS, :].rearrange("a b -> b a"), zero_pad[:, :]).then_inc(copied, 16)
                sp.dma_start(k.attr_s[0:EDGES, :].rearrange("(a b) d -> a (b d)", a=200),
                             k.attr.rearrange("(a b) d -> a (b d)", a=200)).then_inc(copied, 16)
                sp.dma_start(k.attr_s[EDGES:SLOTS, :], zero_attr[:, :]).then_inc(copied, 16)
                sp.wait_ge(copied, 9 * 16)
                sp.dma_start(cur_i[:, :, :], square(k.dst_s, 1)).then_inc(order_in, 16)
                sp.dma_start(prev_i[:, :, :], square(k.dst_s, 0)).then_inc(order_in, 16)
                sp.dma_start(coeff[:, :], k.coeff_t[:, :]).then_inc(coeff_in, 16)
                sp.dma_start(basis_t, k.basis.rearrange("b i o -> b (i o)")).then_inc(coeff_in, 16)
                loads = [(k.wm1[:, :], k.w_m1[0:P, :]), (k.wm1e[:, :], k.w_m1[P:P + ED, :]),
                         (k.wm2[:, :], k.w_m2[:, :]), (k.wu1x[0:D, :], k.w_u1[0:D, :]),
                         (k.wu1x[D:P, :], k.w_u1[0:D, :]), (k.wu1a[:, :], k.w_u1[D:D + H, :]),
                         (k.wu2[:, :], k.w_u2[:, :]), (k.wself[:, :], k.w_self[:, :]), (k.w3[:, :], k.w3_t[:, :]),
                         (k.bm1[:, :], k.b_m1.unsqueeze(1)), (k.bm2[:, :], k.b_m2.unsqueeze(1)),
                         (k.bu1[:, :], k.b_u1.unsqueeze(1)), (k.b3c[:, :], k.b3.unsqueeze(1)),
                         (k.bu2_row[:, :], k.b_u2.unsqueeze(0)),
                         (k.brel_row[:, :], k.b_rel.unsqueeze(0)),
                         (k.gamma_b[:, :], k.gamma.partition_broadcast(P)),
                         (k.beta_b[:, :], k.beta.partition_broadcast(P))]
                for to, frm in loads:
                    sp.dma_start(to, frm).then_inc(weights_in, 16)

                sp.wait_ge(flag_ready, 1)
                unsorted = sp.value_load(flag[0:1, 0:1], min_val=0, max_val=SLOTS)
                with sp.If(unsorted > 0):
                    sp.dma_start(wide.bitcast(I32), k.dst_s[1:1 + SLOTS, 0].partition_broadcast(P)).then_inc(wide_in, 16)

                    def load_tile(t):
                        sp.dma_start(tile_dst_i[:, :], k.dst_s[bass.ds(t * P + 1, P), :]).then_inc(tile_in, 16)
                        sp.dma_start(tile_src_i[:, :], k.src_s[bass.ds(t * P, P), :]).then_inc(tile_in, 16)
                        sp.dma_start(tile_typ_i[:, :], k.typ_s[bass.ds(t * P, P), :]).then_inc(tile_in, 16)
                        sp.dma_start(tile_attr[:, :], k.attr_s[bass.ds(t * P, P), :]).then_inc(tile_in, 16)

                    load_tile(0)
                    with sp.Fori(1, ET) as t:
                        sp.wait_ge(ranked_out, t * 64)
                        load_tile(t)
                    sp.wait_ge(ranked_out, ET * 64)
                    sp.dma_start(k.dst_s[1:1 + SLOTS, 0].rearrange("(a b) -> a b", a=P),
                                 k.dst_r[:, 0].rearrange("(a b) -> a b", a=P)).then_inc(back, 16)
                    sp.dma_start(k.src_s[:, 0].rearrange("(a b) -> a b", a=P),
                                 k.src_r[:, 0].rearrange("(a b) -> a b", a=P)).then_inc(back, 16)
                    sp.dma_start(k.typ_s[:, 0].rearrange("(a b) -> a b", a=P),
                                 k.typ_r[:, 0].rearrange("(a b) -> a b", a=P)).then_inc(back, 16)
                    sp.dma_start(k.attr_s[:, :].rearrange("(a b) d -> a (b d)", a=P),
                                 k.attr_r[:, :].rearrange("(a b) d -> a (b d)", a=P)).then_inc(back, 16)
                    sp.wait_ge(back, 64)

                sp.dma_start(cur_i[:, :, :], square(k.dst_s, 1)).then_inc(arrays_in, 16)
                sp.dma_start(prev_i[:, :, :], square(k.dst_s, 0)).then_inc(arrays_in, 16)
                sp.dma_start(next_i[:, :, :], square(k.dst_s, 2)).then_inc(arrays_in, 16)
                sp.dma_start(src_i[:, :, :], square(k.src_s)).then_inc(arrays_in, 16)
                sp.dma_start(typ_i[:, :, :], square(k.typ_s)).then_inc(arrays_in, 16)
                sp.wait_ge(arrays_v, 6)
                sp.dma_start(k.same_row[:].rearrange("(a q f) -> q a f", a=2, f=P), same_t[:, :, :]).then_inc(rows_out, 16)
                sp.dma_start(k.type_row[:].rearrange("(a q f) -> q a f", a=2, f=P), typf[:, :, :]).then_inc(rows_out, 16)
                sp.dma_start(k.src_row[:].rearrange("(a q f) -> q a f", a=2, f=P), srcf[:, :, :]).then_inc(rows_out, 16)
                sp.wait_ge(rel_copied, 8)
                sp.dma_start(k.rel_rows[:, :], rel).then_inc(rel_out, 16)
                sp.wait_ge(rel_out, 16)
                sp.wait_ge(rows_out, 48)
                sp.dma_start(k.same[:, :], k.same_row[:].partition_broadcast(P)).then_inc(same_in, 16)
                sp.wait_ge(weights_in, 16 * len(loads))
                sp.wait_ge(same_in, 16)

            @block.gpsimd
            def _(pool):
                pool.memset(k.ident[:, :], 0.0).then_inc(consts, 1)
                pool.memset(tri[:, :], 1.0).then_inc(consts, 1)
                pool.iota(rel_iota[:, :], pattern=[[2, RELS // 2]], base=0, channel_multiplier=0).then_inc(consts, 1)
                pool.wait_ge(consts, 3)
                pool.affine_select(out=k.ident[:, :], in_=k.ident[:, :], compare_op=ALU.not_equal, fill=1.0,
                                   base=0, pattern=[[-1, P]], channel_multiplier=1).then_inc(consts, 1)
                pool.affine_select(out=tri[:, :], in_=tri[:, :], compare_op=ALU.is_gt, fill=0.0,
                                   base=0, pattern=[[-1, P]], channel_multiplier=1).then_inc(consts, 1)
                pool.wait_ge(flag_ready, 1)
                unsorted = pool.value_load(flag[0:1, 0:1], min_val=0, max_val=SLOTS)
                with pool.If(unsorted > 0):
                    with pool.Fori(0, ET) as t:
                        pool.wait_ge(rank_v, (t + 1) * STEPS)
                        pool.wait_ge(tile_in, (t + 1) * 64)
                        pool.sem_inc(rank_wait, 1)
                        for table, column in ((k.dst_r, tile_dst_i), (k.src_r, tile_src_i),
                                              (k.typ_r, tile_typ_i), (k.attr_r, tile_attr)):
                            pool.indirect_dma_start(table[:, :], bass.IndirectOffsetOnAxis(ap=rank_i[:, 0:1], axis=0),
                                                    column[:, :], None).then_inc(ranked_out, 16)
                    pool.wait_ge(ranked_out, ET * 64)

            @block.tensor
            def _(pe):
                pe.wait_ge(coeff_in, 32)
                for c in range(8):
                    if c >= 4:
                        pe.wait_ge(rel_copied, c - 3)
                    pe.matmul(k.bank[c % 4][0:RELS, :], coeff[:, :], basis_t[:, c * 512:(c + 1) * 512],
                              start=True, stop=True).then_inc(rel_mm, 1)
                pe.wait_ge(order_v, 5)
                pe.matmul(k.bank[4][0:1, 0:1], falls_sum[:, :], ones_col[0:ROWS, :],
                          start=True, stop=True).then_inc(falls_added, 1)
                pe.wait_ge(consts, 5)
                pe.wait_ge(arrays_v, 10)
                for n, a in enumerate((src_in, gath, scat)):
                    for c in range(2):
                        pe.transpose(k.bank[5 + n][:, c * ROWS:(c + 1) * ROWS], a[:, c, :],
                                     k.ident[0:ROWS, 0:ROWS]).then_inc(turned, 1)
                for c in range(2):
                    pe.transpose(k.bank[5][:, (2 + c) * ROWS:(3 + c) * ROWS], srcf[:, c, :],
                                 k.ident[0:ROWS, 0:ROWS]).then_inc(turned, 1)

            @block.scalar
            def _(act):
                for c in range(8):
                    act.wait_ge(rel_mm, c + 1)
                    act.activation(rel[:, c * 512:(c + 1) * 512], k.bank[c % 4][0:RELS, :], ACT.Copy).then_inc(rel_copied, 1)

            @block.vector
            def _(vec):
                vec.memset(zero_attr[:, :], 0.0).then_inc(pads, 1)
                vec.memset(zero_pad[:, :], 0).then_inc(pads, 1)
                vec.memset(src_pad[:, :], NODES).then_inc(pads, 1)
                vec.memset(dst_pad[:, 0:PAD + 2], NODES).then_inc(pads, 1)
                vec.wait_ge(pads, 4)
                vec.memset(dst_pad[:, 0:PAD + 2:PAD + 1], -1).then_inc(pads, 1)
                vec.memset(ones_col[:, :], 1.0).then_inc(order_v, 1)
                vec.memset(k.ones_row[:, :], 1.0)
                vec.memset(k.eps_col[:, :], D * D * LN_EPS)
                vec.wait_ge(consts, 3)
                vec.tensor_copy(k.relcol[:, :], rel_iota[:, :]).then_inc(idx_ready, 1)
                vec.wait_ge(idx_ready, 1)
                vec.tensor_scalar(k.relcol[D:P, :], k.relcol[D:P, :], 1.0, None, ALU.add).then_inc(idx_ready, 1)
                vec.wait_ge(order_in, 32)
                vec.tensor_copy(cur[:, :, :], cur_i[:, :, :]).then_inc(order_v, 1)
                vec.tensor_copy(prev[:, :, :], prev_i[:, :, :]).then_inc(order_v, 1)
                vec.wait_ge(order_v, 3)
                vec.tensor_tensor(falls[:, :].rearrange("q (a f) -> q a f", a=2), prev[:, :, :], cur[:, :, :],
                                  ALU.is_gt).then_inc(order_v, 1)
                vec.wait_ge(order_v, 4)
                vec.tensor_reduce(falls_sum[:, :], falls[:, :], AX.X, ALU.add).then_inc(order_v, 1)
                vec.wait_ge(falls_added, 1)
                vec.tensor_copy(flag[:, :], k.bank[4][0:1, 0:1]).then_inc(flag_ready, 1)
                vec.wait_ge(flag_ready, 1)
                unsorted = vec.value_load(flag[0:1, 0:1], min_val=0, max_val=SLOTS)
                with vec.If(unsorted > 0):
                    vec.wait_ge(wide_in, 16)
                    vec.wait_ge(consts, 5)
                    vec.tensor_scalar(wide, wide.bitcast(I32), 0.5, None, ALU.add).then_inc(wide_v, 1)
                    vec.wait_ge(wide_v, 1)
                    with vec.Fori(0, ET) as t:
                        vec.wait_ge(tile_in, (t + 1) * 64)
                        base = t * STEPS
                        vec.tensor_copy(tile_dst[:, :], tile_dst_i[:, :]).then_inc(rank_v, 1)
                        vec.wait_ge(rank_v, base + 1)
                        vec.tensor_scalar(tile_half[:, :], tile_dst[:, :], 0.5, None, ALU.add).then_inc(rank_v, 1)
                        for c in range(SLOTS // COUNT_CHUNK):
                            if c:
                                vec.wait_ge(rank_v, base + 2 + 2 * c)
                            vec.tensor_scalar(junk, wide[:, c * COUNT_CHUNK:(c + 1) * COUNT_CHUNK],
                                              tile_dst[:, 0:1], None, ALU.is_le).then_inc(rank_v, 1)
                            vec.wait_ge(rank_v, base + 3 + 2 * c)
                            vec.tensor_reduce(counts[:, c:c + 1], junk, AX.X, ALU.add).then_inc(rank_v, 1)
                        n = 2 + 2 * (SLOTS // COUNT_CHUNK)
                        vec.wait_ge(rank_v, base + n)
                        vec.scalar_tensor_tensor(out=own[:, :], in0=wide[:, bass.ds(t * P, P)], scalar=tile_half[:, 0:1],
                                                 in1=tri[:, :], op0=ALU.is_equal, op1=ALU.mult).then_inc(rank_v, 1)
                        vec.wait_ge(rank_v, base + n + 1)
                        vec.tensor_reduce(counts[:, SLOTS // COUNT_CHUNK:], own[:, :], AX.X, ALU.add).then_inc(rank_v, 1)
                        vec.tensor_scalar(wide[:, bass.ds(t * P, P)], wide[:, bass.ds(t * P, P)], -0.5, None,
                                          ALU.add).then_inc(rank_v, 1)
                        vec.wait_ge(rank_v, base + n + 3)
                        vec.tensor_reduce(rank[:, :], counts[:, :], AX.X, ALU.add).then_inc(rank_v, 1)
                        vec.wait_ge(rank_v, base + n + 4)
                        vec.tensor_copy(rank_i[:, :], rank[:, :]).then_inc(rank_v, 1)
                vec.wait_ge(arrays_in, 5 * 16)
                vec.tensor_copy(cur[:, :, :], cur_i[:, :, :]).then_inc(arrays_v, 1)
                vec.tensor_copy(prev[:, :, :], prev_i[:, :, :]).then_inc(arrays_v, 1)
                vec.tensor_copy(nxt[:, :, :], next_i[:, :, :]).then_inc(arrays_v, 1)
                vec.tensor_copy(srcf[:, :, :], src_i[:, :, :]).then_inc(arrays_v, 1)
                vec.tensor_copy(typf[:, :, :], typ_i[:, :, :]).then_inc(arrays_v, 1)
                vec.wait_ge(arrays_v, 5)
                vec.tensor_tensor(same_t[:, :, :], cur[:, :, :], prev[:, :, :], ALU.is_equal).then_inc(arrays_v, 1)
                vec.tensor_tensor(nxt[:, :, :], cur[:, :, :], nxt[:, :, :], ALU.is_equal).then_inc(arrays_v, 1)
                vec.tensor_scalar(gath[:, :, :], cur[:, :, :], float(NODES - 1), None, ALU.min).then_inc(arrays_v, 1)
                vec.tensor_scalar(src_in[:, :, :], srcf[:, :, :], float(NODES - 1), None, ALU.min).then_inc(arrays_v, 1)
                vec.wait_ge(arrays_v, 9)
                vec.scalar_tensor_tensor(out=scat[:, :, :], in0=nxt[:, :, :], scalar=float(FAR), in1=cur[:, :, :],
                                         op0=ALU.mult, op1=ALU.add).then_inc(arrays_v, 1)
                vec.wait_ge(turned, 8)
                for n, a in enumerate((k.src_idx, k.dst_idx, k.last_idx)):
                    vec.tensor_copy(a[:, :], k.bank[5 + n][:, 0:ET]).then_inc(idx_ready, 1)
                vec.tensor_copy(k.src_key[:, :], k.bank[5][:, ET:2 * ET]).then_inc(idx_ready, 1)
                vec.wait_ge(idx_ready, 6)


def stage_index(pool, copied, g, ring, idx):
    pool.tensor_copy(ring[:, g.buf, :], idx[:, bass.ds(g.n * TG, TG)]).then_inc(copied, 1)


def gather_rows(pool, to, table, index):
    return pool.indirect_dma_start(to, None, table[:, :], bass.IndirectOffsetOnAxis(ap=index, axis=0))


def scatter_rows(pool, table, frm, index):
    return pool.indirect_dma_start(table[:, :], bass.IndirectOffsetOnAxis(ap=index, axis=0), frm, None,
                                   bounds_check=NODES - 1, oob_is_err=False)


def gather_group(pool, g, reads, copied, gathered, settled):
    if g.from_second():
        pool.wait_ge(gathered[g.buf], g.half * (len(reads) * TG * 16))
    pool.sem_inc(settled, 1)
    for to, table, idx, ring in reads:
        stage_index(pool, copied, g, ring, idx)
    pool.wait_ge(copied, (g.n + 1) * len(reads))
    pool.sem_inc(settled, 1)
    for t in range(TG):
        for to, table, idx, ring in reads:
            gather_rows(pool, to[:, t], table, ring[:, g.buf, t:t + 1]).then_inc(gathered[g.buf], 16)


def scatter_group(pool, g, rows, ready, count, table, idx, ring, copied, scattered, settled):
    if g.from_second():
        pool.wait_ge(scattered[g.buf], g.half * (TG * 16))
    pool.sem_inc(settled, 1)
    stage_index(pool, copied, g, ring, idx)
    pool.wait_ge(copied, g.n + 1)
    pool.wait_ge(ready, count)
    pool.sem_inc(settled, 1)
    for t in range(TG):
        scatter_rows(pool, table, rows[:, g.buf, t, :], ring[:, g.buf, t:t + 1]).then_inc(scattered[g.buf], 16)


def dense(nc, k):
    with ExitStack() as ctx:
        def two(name, shape, dt=F32):
            return k.sb(name, [shape[0], 2] + shape[1:], dt, ctx)

        def sem(name):
            return k.sem(name, ctx)

        rows = two("rows", [NP, NG, D])
        cen0 = two("cen0", [NP, NG, D])
        res0 = two("res0", [NP, NG, D])
        cen1 = two("cen1", [NP, NG, D])
        res1 = two("res1", [NP, NG, D])
        res2 = two("res2", [NP, NG, D])
        outs = two("outs", [NP, NG, D])
        squares = k.sb("squares", [NP, 2, NG, D], F32, ctx)
        sums = k.sb("sums", [NP, 2, NG], F32, ctx)
        roots = k.sb("roots", [NP, 2, NG], F32, ctx)
        inverse = k.sb("inverse", [NP, 2, NG], F32, ctx)
        h0t = k.sb("h0t", [D, 2, HALF], F32, ctx)
        h1t = k.sb("h1t", [D, 2, HALF], F32, ctx)
        ut = k.sb("ut", [H, 2, HALF], F32, ctx)
        src_ring = k.sb("src_ring", [P, 2, TG], I32, ctx)
        dst_ring = k.sb("dst_ring", [P, 2, TG], I32, ctx)
        xs_ring = k.sb("xs_ring", [P, 2, TG, D], F32, ctx)
        xd_ring = k.sb("xd_ring", [P, 2, TG, D], F32, ctx)

        x_in = k.pair_of_sems("x_in", ctx)
        ln0, ln1, added2 = sem("ln0"), sem("ln1"), sem("added2")
        sq0_done, sq1_done = sem("sq0_done"), sem("sq1_done")
        rooted, inverted = sem("rooted"), sem("inverted")
        t0_done, t1_done = sem("t0_done"), sem("t1_done")
        h0t_done, h1t_done = sem("h0t_done"), sem("h1t_done")
        u1_done, ut_done, u2_done = sem("u1_done"), sem("ut_done"), sem("u2_done")
        self_done = sem("self_done")
        pe_wait = sem("pe_wait")
        x1_out = k.pair_of_sems("x1_out", ctx)
        x2_out = k.pair_of_sems("x2_out", ctx)
        gathered = k.pair_of_sems("gathered", ctx)
        kept = k.pair_of_sems("kept", ctx)
        idx_copied = sem("idx_copied")
        pool_wait = sem("pool_wait")

        def nodes(a, g):
            return a.rearrange("(p j) d -> p j d", p=NP)[:, bass.ds(g.n * NG, NG), :]

        with nc.Block() as block:
            @block.sync
            def _(sp):

                def step(r):
                    g = r
                    if g.within(DG):
                        if g.from_second():
                            sp.wait_ge(ln0, (g - 2).n * 5 + 5)
                        sp.dma_start(rows[:, g.buf], nodes(k.x, g)).then_inc(x_in[g.buf], 16)
                    g = r - 2
                    if g.within(EG):
                        sp.wait_ge(gathered[g.buf], (g.half + 1) * (2 * TG * 16))
                        sp.dma_start(k.x_src[:, bass.ds(g.n * TG, TG), :], xs_ring[:, g.buf]).then_inc(kept[g.buf], 16)
                        sp.dma_start(k.x_dst[:, bass.ds(g.n * TG, TG), :], xd_ring[:, g.buf]).then_inc(kept[g.buf], 16)
                    g = r - 3
                    if g.within(DG):
                        sp.wait_ge(ln1, g.n * 5 + 1)
                        sp.dma_start(nodes(k.x1_table, g), res1[:, g.buf]).then_inc(x1_out[g.buf], 16)
                    g = r - 5
                    if g.within(DG):
                        sp.wait_ge(added2, g.n * 2 + 2)
                        sp.dma_start(nodes(k.x2_table, g), res2[:, g.buf]).then_inc(x2_out[g.buf], 16)
                        sp.dma_start(nodes(k.out, g), outs[:, g.buf]).then_inc(x2_out[g.buf], 16)

                rounds(sp, DG, 5, step)
                for b in range(2):
                    sp.wait_ge(x1_out[b], (DG + 1 - b) // 2 * 16)
                    sp.wait_ge(x2_out[b], (DG + 1 - b) // 2 * 32)
                    sp.wait_ge(kept[b], (EG + 1 - b) // 2 * 32)

            @block.gpsimd
            def _(pool):
                stage_index(pool, idx_copied, Group(0, 0), src_ring, k.src_idx)
                stage_index(pool, idx_copied, Group(0, 0), dst_ring, k.dst_idx)

                def gather(r, j):
                    for ring, index in ((xs_ring, src_ring), (xd_ring, dst_ring)):
                        gather_rows(pool, ring[:, r.buf, j, :], k.x, index[:, r.buf, j:j + 1]).then_inc(gathered[r.buf], 16)

                def step(r):
                    if r.from_second():
                        pool.wait_ge(kept[r.buf], r.half * 32)
                    pool.wait_ge(idx_copied, r.n * 2 + 2)
                    pool.sem_inc(pool_wait, 1)
                    gather(r, 0)
                    gather(r, 1)
                    if (r + 1).within(EG):
                        if r.from_first():
                            pool.wait_ge(gathered[(r + 1).buf], (r + 1).half * (2 * TG * 16))
                            pool.sem_inc(pool_wait, 1)
                        stage_index(pool, idx_copied, r + 1, src_ring, k.src_idx)
                        stage_index(pool, idx_copied, r + 1, dst_ring, k.dst_idx)
                    gather(r, 2)
                    gather(r, 3)

                rounds(pool, EG, 0, step)

            @block.vector
            def _(vec):
                def step(r):
                    g = r
                    if g.within(DG):
                        vec.wait_ge(x_in[g.buf], (g.half + 1) * 16)
                        if g.from_second():
                            vec.wait_ge(t0_done, (g - 2).n * 2 + 2)
                        center_rows(vec, ln0, g.n * 5, rows[:, g.buf], sums[:, 0, :], cen0[:, g.buf])
                    g = r - 4
                    if g.within(DG):
                        vec.wait_ge(self_done, g.n + 1)
                        if g.from_second():
                            vec.wait_ge(x2_out[g.buf], g.half * 32)
                        vec.tensor_tensor(res2[:, g.buf], res1[:, g.buf],
                                          k.bank[7][0:NP, :].rearrange("p (j d) -> p j d", d=D), ALU.add).then_inc(added2, 1)
                        vec.wait_ge(added2, g.n * 2 + 1)
                        vec.tensor_tensor(outs[:, g.buf], res2[:, g.buf],
                                          k.beta_b[0:NP, :].unsqueeze(1).to_broadcast([NP, NG, D]), ALU.add).then_inc(added2, 1)
                    g = r - 2
                    if g.within(DG):
                        vec.wait_ge(u2_done, g.n + 1)
                        if g.from_second():
                            vec.wait_ge(x1_out[g.buf], g.half * 16)
                        vec.tensor_tensor(res1[:, g.buf], res0[:, g.buf],
                                          k.bank[6][0:NP, :].rearrange("p (j d) -> p j d", d=D), ALU.add).then_inc(ln1, 1)
                        vec.wait_ge(ln1, g.n * 5 + 1)
                        if g.from_second():
                            vec.wait_ge(t1_done, (g - 2).n * 2 + 2)
                        center_rows(vec, ln1, g.n * 5 + 1, res1[:, g.buf], sums[:, 1, :], cen1[:, g.buf])
                    live = [m for m in range(2) if (r - 2 * m).within(DG)]
                    if not live:
                        return
                    for m, ln, done in ((0, ln0, sq0_done), (1, ln1, sq1_done)):
                        if m in live:
                            vec.wait_ge(done, (r - 2 * m).n + 1)
                            vec.tensor_reduce(roots[:, m, :], squares[:, m], AX.X, ALU.add).then_inc(ln, 1)
                    vec.wait_ge(rooted, r.n + 1)
                    vec.reciprocal(inverse[:, live[0]:live[-1] + 1, :], roots[:, live[0]:live[-1] + 1, :]).then_inc(inverted, 1)
                    vec.wait_ge(inverted, r.n + 1)
                    g = r - 2
                    if g.within(DG):
                        scale_rows(vec, ln1, cen1[:, g.buf], inverse[:, 1, :], cen1[:, g.buf])
                    g = r
                    if g.within(DG):
                        scale_rows(vec, ln0, cen0[:, g.buf], inverse[:, 0, :], cen0[:, g.buf])
                        vec.wait_ge(ln0, g.n * 5 + 4)
                        vec.tensor_tensor(res0[:, g.buf], rows[:, g.buf], cen0[:, g.buf], ALU.add).then_inc(ln0, 1)

                rounds(vec, DG, 4, step)

            @block.scalar
            def _(act):
                def step(r):
                    g = r - 1
                    if g.within(DG):
                        for c in range(2):
                            act.wait_ge(t0_done, g.n * 2 + c + 1)
                            if g.from_first():
                                act.wait_ge(u1_done, g.n * 2 + c - 1)
                            act.activation(h0t[:, c, :], k.bank[c][0:D, 0:HALF], ACT.Copy).then_inc(h0t_done, 1)
                    g = r - 3
                    if g.within(DG):
                        for c in range(2):
                            act.wait_ge(t1_done, g.n * 2 + c + 1)
                            if g.from_first():
                                act.wait_ge(self_done, g.n)
                            act.activation(h1t[:, c, :], k.bank[2 + c][0:D, 0:HALF], ACT.Copy).then_inc(h1t_done, 1)
                    g = r
                    if g.within(DG):
                        act.wait_ge(ln0, g.n * 5 + 2)
                        act.activation(squares[:, 0], cen0[:, g.buf], ACT.Square, scale=0.125).then_inc(sq0_done, 1)
                    g = r - 2
                    if g.within(DG):
                        act.wait_ge(ln1, g.n * 5 + 3)
                        act.activation(squares[:, 1], cen1[:, g.buf], ACT.Square, scale=0.125).then_inc(sq1_done, 1)
                    g = r - 1
                    if g.within(DG):
                        for c in range(2):
                            act.wait_ge(u1_done, g.n * 2 + c + 1)
                            if g.from_first():
                                act.wait_ge(u2_done, g.n)
                            act.activation(ut[:, c, :], k.bank[4 + c][:, 0:HALF], ACT.Relu, bias=k.bu1[:, 0:1]).then_inc(ut_done, 1)
                    live = [m for m in range(2) if (r - 2 * m).within(DG)]
                    if not live:
                        return
                    if 0 in live:
                        act.wait_ge(ln0, r.n * 5 + 3)
                    if 1 in live:
                        act.wait_ge(ln1, (r - 2).n * 5 + 4)
                    act.activation(roots[:, live[0]:live[-1] + 1, :], roots[:, live[0]:live[-1] + 1, :], ACT.Sqrt,
                                   bias=k.eps_col[0:NP, 0:1]).then_inc(rooted, 1)

                rounds(act, DG, 4, step)

            @block.tensor
            def _(pe):
                def turn(g, rows_in, banks, done):
                    for c in range(2):
                        for j in range(NG // 2):
                            mm = pe.transpose(k.bank[banks + c][0:D, j * NP:(j + 1) * NP],
                                              rows_in[:, g.buf, c * (NG // 2) + j, :], k.ident[0:NP, 0:NP])
                        mm.then_inc(done, 1)

                def back(cols, weights, bias, to, done):
                    pe.matmul(k.bank[to][0:NP, :], k.ones_row[:, 0:NP], bias.unsqueeze(1).to_broadcast([1, NG, D]), start=True, stop=True,
                              skip_group_check=True)
                    for j in range(NG):
                        at = (j % (NG // 2)) * NP
                        mm = pe.matmul(k.bank[to][0:NP, j * D:(j + 1) * D], cols[:, j // (NG // 2), at:at + NP], weights,
                                       start=False, stop=True, skip_group_check=True)
                    mm.then_inc(done, 1)

                def step(r):
                    g = r - 1
                    if g.within(DG):
                        pe.wait_ge(ln0, g.n * 5 + 4)
                        if g.from_first():
                            pe.wait_ge(h0t_done, g.n * 2)
                        pe.sem_inc(pe_wait, 1)
                        turn(g, cen0, 0, t0_done)
                    g = r - 3
                    if g.within(DG):
                        pe.wait_ge(ln1, g.n * 5 + 5)
                        if g.from_first():
                            pe.wait_ge(h1t_done, g.n * 2)
                        pe.sem_inc(pe_wait, 1)
                        turn(g, cen1, 2, t1_done)
                    g = r - 1
                    if g.within(DG):
                        for c in range(2):
                            pe.wait_ge(h0t_done, g.n * 2 + c + 1)
                            if g.from_first():
                                pe.wait_ge(ut_done, g.n * 2 + c - 1)
                            pe.matmul(k.bank[4 + c][:, 0:HALF], k.wu1x[0:D, :], h0t[:, c, :],
                                      start=True, stop=True).then_inc(u1_done, 1)
                    g = r - 3
                    if g.within(DG):
                        pe.wait_ge(h1t_done, g.n * 2 + 2)
                        if g.from_first():
                            pe.wait_ge(added2, g.n * 2 - 1)
                        back(h1t, k.wself[:, :], k.brel_row[:, :], 7, self_done)
                    g = r - 1
                    if g.within(DG):
                        pe.wait_ge(ut_done, g.n * 2 + 2)
                        if g.from_first():
                            pe.wait_ge(ln1, g.n * 5 - 4)
                        back(ut, k.wu2[:, :], k.bu2_row[:, :], 6, u2_done)

                rounds(pe, DG, 4, step)


def layer0(nc, k):
    with ExitStack() as ctx:
        def sb(name, shape, dt=F32):
            return k.sb(name, shape, dt, ctx)

        def sem(name):
            return k.sem(name, ctx)

        attr = sb("l0_attr", [P, 2, TG, ED])
        cen = sb("l0_cen", [P, 2, TG, 2, D])
        squares = sb("l0_squares", [P, 3 * TG * D])
        sq_in = squares[:, 0:2 * TG * D]
        sq_up = squares[:, 2 * TG * D:]
        stats = sb("l0_stats", [P, 3 * TG])
        roots = sb("l0_roots", [P, 3 * TG])
        inverse = sb("l0_inverse", [P, 3 * TG])
        ht = sb("l0_ht", [P, 2, GS])
        at = sb("l0_at", [ED, 2, GS])
        hid = sb("l0_hid", [H, GS])
        msg = sb("l0_msg", [H, 2, GS])
        agg = sb("l0_agg", [H, 2, GS])
        ut = sb("l0_ut", [H, GS])
        x1 = sb("l0_x1", [P, 2, TG, D])
        h1 = sb("l0_h1", [P, 2, TG, D])
        h1t = sb("l0_h1t", [D, GS])
        last_ring = sb("l0_last_ring", [P, 2, TG], I32)
        zeros = sb("l0_zeros", [P, CLEAR])

        attr_in = k.pair_of_sems("l0_attr_in", ctx)
        ln0, ln1 = sem("l0_ln0"), sem("l0_ln1")
        sq_in_done, sq_up_done = sem("l0_sq_in_done"), sem("l0_sq_up_done")
        rooted, inverted = sem("l0_rooted"), sem("l0_inverted")
        turned, ht_done, at_done = sem("l0_turned"), sem("l0_ht_done"), sem("l0_at_done")
        m1_done, hid_done, m2_done, msg_done = sem("l0_m1"), sem("l0_hid_done"), sem("l0_m2"), sem("l0_msg_done")
        scanned = sem("l0_scanned")
        u1_done, ut_done, u2_done = sem("l0_u1"), sem("l0_ut_done"), sem("l0_u2")
        h1_turned, h1t_done, self_done = sem("l0_h1_turned"), sem("l0_h1t_done"), sem("l0_self")
        self_added = sem("l0_self_added")
        pe_wait, pool_wait, idx_copied = sem("l0_pe_wait"), sem("l0_pool_wait"), sem("l0_idx_copied")
        scattered = k.pair_of_sems("l0_scattered", ctx)
        zeroed, cleared = sem("l0_zeroed"), sem("l0_cleared")
        sum_flat = k.sum_table[:, :].rearrange("n d -> (n d)").rearrange("(c p f) -> c p f", p=P, f=CLEAR)

        def x_dst(g):
            return k.x_dst[:, bass.ds(g.n * TG, TG), :]

        def x_src(g):
            return k.x_src[:, bass.ds(g.n * TG, TG), :]

        def spans(r):
            return (0 if r.within(EG) else 2 * TG), (3 * TG if (r - 3).within(EG) else 2 * TG)

        with nc.Block() as block:
            @block.sync
            def _(sp):
                def step(r):
                    if r.from_second():
                        sp.wait_ge(turned, (r - 2).n + 1)
                    sp.dma_start(attr[:, r.buf], k.attr_s[bass.ds(r.n * GS, GS), :].rearrange("(t p) c -> p t c", p=P)
                                 ).then_inc(attr_in[r.buf], 16)

                sp.wait_ge(zeroed, 1)
                for c in range(sum_flat.shape[0]):
                    sp.dma_start(sum_flat[c], zeros[:, :]).then_inc(cleared, 16)
                rounds(sp, EG, 0, step)
                sp.wait_ge(cleared, sum_flat.shape[0] * 16)

            @block.gpsimd
            def _(pool):
                def step(g):
                    scatter_group(pool, g, x1, ln1, g.n * 5 + 1, k.x1_table, k.last_idx, last_ring,
                                  idx_copied, scattered, pool_wait)

                rounds(pool, EG, 0, step)
                for b in range(2):
                    pool.wait_ge(scattered[b], (EG + 1 - b) // 2 * TG * 16)

            @block.vector
            def _(vec):
                vec.memset(zeros[:, :], 0.0).then_inc(zeroed, 1)

                def step(r):
                    g = r - 2
                    if g.within(EG):
                        vec.wait_ge(msg_done, g.n + 1)
                        if g.from_second():
                            vec.wait_ge(u1_done, (g - 2).n + 1)
                        if g.from_first():
                            vec.wait_ge(scanned, g.n)
                        vec.tensor_tensor_scan(agg[:, g.buf, :], k.same[:, bass.ds(g.n * GS, GS)], msg[:, g.buf, :],
                                               agg[:, (g - 1).buf, GS - 1:GS] if g.from_first() else 0.0,
                                               ALU.mult, ALU.add).then_inc(scanned, 1)
                    g = r
                    if g.within(EG):
                        flat = cen[:, g.buf]
                        for side, x in ((0, x_src(g)), (1, x_dst(g))):
                            vec.tensor_reduce(stats[:, side * TG:side * TG + TG], x, AX.X, ALU.add).then_inc(ln0, 1)
                        if g.from_second():
                            vec.wait_ge(turned, (g - 2).n + 1)
                        for side, x in ((0, x_src(g)), (1, x_dst(g))):
                            vec.wait_ge(ln0, g.n * 7 + 1 + side)
                            vec.scalar_tensor_tensor(
                                out=flat[:, :, side, :], in0=x, scalar=float(D),
                                in1=stats[:, side * TG:side * TG + TG].unsqueeze(2).to_broadcast([P, TG, D]),
                                op0=ALU.mult, op1=ALU.subtract).then_inc(ln0, 1)
                    g = r - 5
                    if g.within(EG):
                        vec.wait_ge(self_done, g.n + 1)
                        vec.tensor_tensor(x_dst(g), x1[:, g.buf], k.bank[7][:, 0:TG * D].rearrange("p (t d) -> p t d", d=D),
                                          ALU.add).then_inc(self_added, 1)
                    g = r - 3
                    if g.within(EG):
                        vec.wait_ge(u2_done, g.n + 1)
                        if g.from_second():
                            vec.wait_ge(scattered[g.buf], g.half * (TG * 16))
                            vec.wait_ge(self_added, (g - 2).n + 1)
                        vec.tensor_tensor(x1[:, g.buf], x_dst(g), k.bank[5][:, 0:TG * D].rearrange("p (t d) -> p t d", d=D),
                                          ALU.add).then_inc(ln1, 1)
                        vec.wait_ge(ln1, g.n * 5 + 1)
                        if g.from_second():
                            vec.wait_ge(h1_turned, (g - 2).n + 1)
                        center_rows(vec, ln1, g.n * 5 + 1, x1[:, g.buf], stats[:, 2 * TG:], h1[:, g.buf])
                    lo, hi = spans(r)
                    if lo >= hi:
                        return
                    if r.within(EG):
                        vec.wait_ge(sq_in_done, r.n + 1)
                        vec.tensor_reduce(roots[:, 0:2 * TG], sq_in.rearrange("p (t d) -> p t d", d=D), AX.X, ALU.add).then_inc(ln0, 1)
                    if (r - 3).within(EG):
                        vec.wait_ge(sq_up_done, (r - 3).n + 1)
                        vec.tensor_reduce(roots[:, 2 * TG:], sq_up.rearrange("p (t d) -> p t d", d=D), AX.X, ALU.add).then_inc(ln1, 1)
                    vec.wait_ge(rooted, r.n + 1)
                    vec.reciprocal(inverse[:, lo:hi], roots[:, lo:hi]).then_inc(inverted, 1)
                    vec.wait_ge(inverted, r.n + 1)
                    g = r - 3
                    if g.within(EG):
                        scale_rows(vec, ln1, h1[:, g.buf], inverse[:, 2 * TG:], h1[:, g.buf])
                    g = r
                    if g.within(EG):
                        flat = cen[:, g.buf].rearrange("p t s d -> p (t s) d")
                        scale_rows(vec, ln0, flat, inverse[:, 0:2 * TG], flat)
                        vec.wait_ge(ln0, g.n * 7 + 6)
                        vec.tensor_tensor(x_dst(g), x_dst(g), cen[:, g.buf, :, 1, :], ALU.add).then_inc(ln0, 1)

                rounds(vec, EG, 5, step)

            @block.scalar
            def _(act):
                def step(r):
                    g = r - 1
                    if g.within(EG):
                        act.wait_ge(turned, g.n + 1)
                        if g.from_second():
                            act.wait_ge(u1_done, (g - 2).n + 1)
                        act.activation(ht[:, g.buf, :], k.bank[0][:, :], ACT.Copy).then_inc(ht_done, 1)
                        act.activation(at[:, g.buf, :], k.bank[1][0:ED, :], ACT.Copy).then_inc(at_done, 1)
                    g = r - 4
                    if g.within(EG):
                        act.wait_ge(h1_turned, g.n + 1)
                        if g.from_first():
                            act.wait_ge(self_done, g.n)
                        act.activation(h1t[:, :], k.bank[6][0:D, :], ACT.Copy).then_inc(h1t_done, 1)
                    g = r
                    if g.within(EG):
                        act.wait_ge(ln0, g.n * 7 + 4)
                        act.activation(sq_in.rearrange("p (t d) -> p t d", d=D), cen[:, g.buf].rearrange("p t s d -> p (t s) d"),
                                       ACT.Square, scale=0.125).then_inc(sq_in_done, 1)
                    g = r - 2
                    if g.within(EG):
                        act.wait_ge(u1_done, g.n + 1)
                        if g.from_first():
                            act.wait_ge(u2_done, g.n)
                        act.activation(ut[:, :], k.bank[4][:, :], ACT.Relu, bias=k.bu1[:, 0:1]).then_inc(ut_done, 1)
                    g = r - 3
                    if g.within(EG):
                        act.wait_ge(ln1, g.n * 5 + 3)
                        act.activation(sq_up.rearrange("p (t d) -> p t d", d=D), h1[:, g.buf], ACT.Square, scale=0.125
                                       ).then_inc(sq_up_done, 1)
                    g = r - 1
                    if g.within(EG):
                        act.wait_ge(m1_done, g.n + 1)
                        if g.from_first():
                            act.wait_ge(m2_done, g.n)
                        act.activation(hid[:, :], k.bank[2][:, :], ACT.Relu, bias=k.bm1[:, 0:1]).then_inc(hid_done, 1)
                    lo, hi = spans(r)
                    if lo < hi:
                        if r.within(EG):
                            act.wait_ge(ln0, r.n * 7 + 5)
                        if (r - 3).within(EG):
                            act.wait_ge(ln1, (r - 3).n * 5 + 4)
                        act.activation(roots[:, lo:hi], roots[:, lo:hi], ACT.Sqrt, bias=k.eps_col[:, 0:1]).then_inc(rooted, 1)
                    g = r - 1
                    if g.within(EG):
                        act.wait_ge(m2_done, g.n + 1)
                        if g.from_second():
                            act.wait_ge(scanned, (g - 2).n + 1)
                        act.activation(msg[:, g.buf, :], k.bank[3][:, :], ACT.Identity, bias=k.bm2[:, 0:1]).then_inc(msg_done, 1)

                rounds(act, EG, 4, step)

            @block.tensor
            def _(pe):
                def rows_times(to, cols, weights, bias, done):
                    pe.matmul(k.bank[to][:, 0:TG * D], k.ones_row[:, :], bias[:, :].unsqueeze(1).to_broadcast([1, TG, D]), start=True, stop=True,
                              skip_group_check=True)
                    for t in range(TG):
                        mm = pe.matmul(k.bank[to][:, t * D:(t + 1) * D], cols[:, t * P:(t + 1) * P], weights,
                                       start=False, stop=True, skip_group_check=True)
                    mm.then_inc(done, 1)

                def step(r):
                    g = r - 1
                    if g.within(EG):
                        pe.wait_ge(ln0, g.n * 7 + 6)
                        pe.wait_ge(attr_in[g.buf], (g.half + 1) * 16)
                        if g.from_first():
                            pe.wait_ge(at_done, g.n)
                        pe.sem_inc(pe_wait, 1)
                        for t in range(TG):
                            pe.transpose(k.bank[0][:, t * P:(t + 1) * P], cen[:, g.buf, t].rearrange("p s d -> p (s d)"), k.ident[:, :])
                        for t in range(TG):
                            mm = pe.transpose(k.bank[1][0:ED, t * P:(t + 1) * P], attr[:, g.buf, t, :], k.ident[:, :])
                        mm.then_inc(turned, 1)
                    g = r - 4
                    if g.within(EG):
                        pe.wait_ge(ln1, g.n * 5 + 5)
                        if g.from_first():
                            pe.wait_ge(h1t_done, g.n)
                        pe.sem_inc(pe_wait, 1)
                        for t in range(TG):
                            mm = pe.transpose(k.bank[6][0:D, t * P:(t + 1) * P], h1[:, g.buf, t, :], k.ident[:, :])
                        mm.then_inc(h1_turned, 1)
                    g = r - 2
                    if g.within(EG):
                        pe.wait_ge(scanned, g.n + 1)
                        if g.from_first():
                            pe.wait_ge(ut_done, g.n)
                        pe.matmul(k.bank[4][:, :], k.wu1a[:, :], agg[:, g.buf, :], start=True, stop=False)
                        pe.matmul(k.bank[4][:, :], k.wu1x[D:P, :], ht[D:P, g.buf, :], start=False, stop=True).then_inc(u1_done, 1)
                    g = r - 1
                    if g.within(EG):
                        pe.wait_ge(at_done, g.n + 1)
                        if g.from_first():
                            pe.wait_ge(hid_done, g.n)
                        pe.matmul(k.bank[2][:, :], k.wm1[:, :], ht[:, g.buf, :], start=True, stop=False)
                        pe.matmul(k.bank[2][:, :], k.wm1e[:, :], at[:, g.buf, :], start=False, stop=True).then_inc(m1_done, 1)
                    g = r - 4
                    if g.within(EG):
                        pe.wait_ge(h1t_done, g.n + 1)
                        if g.from_first():
                            pe.wait_ge(self_added, g.n)
                        pe.sem_inc(pe_wait, 1)
                        rows_times(7, h1t, k.wself[:, :], k.brel_row, self_done)
                    g = r - 2
                    if g.within(EG):
                        pe.wait_ge(ut_done, g.n + 1)
                        if g.from_first():
                            pe.wait_ge(ln1, g.n * 5 - 4)
                        pe.sem_inc(pe_wait, 1)
                        rows_times(5, ut, k.wu2[:, :], k.bu2_row, u2_done)
                    g = r - 1
                    if g.within(EG):
                        pe.wait_ge(hid_done, g.n + 1)
                        if g.from_first():
                            pe.wait_ge(msg_done, g.n)
                        pe.matmul(k.bank[3][:, :], k.wm2[:, :], hid[:, :], start=True, stop=True).then_inc(m2_done, 1)

                rounds(pe, EG, 4, step)


def layer1(nc, k):
    with ExitStack() as ctx:
        def sb(name, shape, dt=F32):
            return k.sb(name, shape, dt, ctx)

        def sem(name):
            return k.sem(name, ctx)

        PAIRS = RELS // 2
        NZ = 8
        wrel = sb("l1_wrel", [P, PAIRS, D])
        types = sb("l1_types", [P, 2, GS])
        xs = sb("l1_xs", [P, 2, TG, D])
        cen = sb("l1_cen", [P, TG, D])
        h1 = sb("l1_h1", [P, 2, TG, 2, D])
        squares = sb("l1_squares", [P, TG, D])
        stats = sb("l1_stats", [P, TG])
        roots = sb("l1_roots", [P, TG])
        inverse = sb("l1_inverse", [P, TG])
        ht = sb("l1_ht", [P, 2, GS])
        z = sb("l1_z", [P, NZ, GS])
        msg = sb("l1_msg", [D + 1, 2, GS])
        agg = sb("l1_agg", [D + 1, 2, GS])
        deg = sb("l1_deg", [P, TG])
        part = sb("l1_part", [P, TG, D])
        x2 = sb("l1_x2", [P, 2, TG, D])
        src_ring = sb("l1_src_ring", [P, 2, TG], I32)
        last_ring = sb("l1_last_ring", [P, 2, TG], I32)

        wrel_in, types_in = sem("l1_wrel_in"), k.pair_of_sems("l1_types_in", ctx)
        gathered, scattered = k.pair_of_sems("l1_gathered", ctx), k.pair_of_sems("l1_scattered", ctx)
        ln, sq_done, rooted, inverted = sem("l1_ln"), sem("l1_sq_done"), sem("l1_rooted"), sem("l1_inverted")
        turned, ht_done = sem("l1_turned"), sem("l1_ht_done")
        z_made, z_used, msg_done = sem("l1_z_made"), sem("l1_z_used"), sem("l1_msg_done")
        ones_set, scanned, rows_done, updated = sem("l1_ones"), sem("l1_scanned"), sem("l1_rows"), sem("l1_updated")
        pe_wait, pool_wait = sem("l1_pe_wait"), sem("l1_pool_wait")
        src_copied, last_copied = sem("l1_src_copied"), sem("l1_last_copied")

        with nc.Block() as block:
            @block.sync
            def _(sp):
                sp.dma_start(wrel[:, :, :], k.rel_rows[:, :].rearrange("(k r) (i o) -> (r i) k o", r=2, o=D)).then_inc(wrel_in, 16)

                def step(r):
                    if r.from_second():
                        sp.wait_ge(z_made, (r - 1).n * PAIRS)
                    sp.dma_start(types[:, r.buf, :], k.type_row[bass.ds(r.n * GS, GS)].partition_broadcast(P)
                                 ).then_inc(types_in[r.buf], 16)

                rounds(sp, EG, 0, step)

            @block.gpsimd
            def _(pool):
                def step(r):
                    g = r
                    if g.within(EG):
                        if g.from_second():
                            pool.wait_ge(ln, (g - 2).n * 5 + 2)
                        gather_group(pool, g, ((xs[:, g.buf], k.x1_table, k.src_idx, src_ring),),
                                     src_copied, gathered, pool_wait)
                    g = r - 4
                    if g.within(EG):
                        scatter_group(pool, g, x2, updated, g.n * 5 + 5, k.x2_table, k.last_idx, last_ring,
                                      last_copied, scattered, pool_wait)

                rounds(pool, EG, 4, step)
                for b in range(2):
                    pool.wait_ge(scattered[b], (EG + 1 - b) // 2 * TG * 16)

            @block.vector
            def _(vec):
                vec.memset(msg[D:D + 1, :, :], 1.0).then_inc(ones_set, 1)
                vec.wait_ge(ones_set, 1)

                def mask(g, first, count):
                    if not g.within(EG):
                        return
                    if first == 0:
                        vec.wait_ge(types_in[g.buf], (g.half + 1) * 16)
                        vec.wait_ge(ht_done, g.n + 1)
                    for n in range(first, first + count):
                        if g.from_first() or n >= NZ:
                            vec.wait_ge(z_used, g.n * PAIRS + n - NZ + 1)
                        vec.scalar_tensor_tensor(out=z[:, n % NZ, :], in0=types[:, g.buf, :], scalar=k.relcol[:, n:n + 1],
                                                 in1=ht[:, g.buf, :], op0=ALU.is_equal, op1=ALU.mult).then_inc(z_made, 1)

                def step(r):
                    g = r
                    if g.within(EG):
                        vec.wait_ge(gathered[g.buf], (g.half + 1) * (TG * 16))
                        center_rows(vec, ln, g.n * 5, xs[:, g.buf], stats[:, :], cen[:, :, :])
                    mask(r - 1, 0, 4)
                    g = r
                    if g.within(EG):
                        vec.wait_ge(sq_done, g.n + 1)
                        vec.tensor_reduce(roots[:, :], squares[:, :, :], AX.X, ALU.add).then_inc(ln, 1)
                    mask(r - 1, 4, 2)
                    g = r - 2
                    if g.within(EG):
                        vec.wait_ge(msg_done, g.n + 1)
                        if g.from_second():
                            vec.wait_ge(rows_done, (g - 2).n + 1)
                        if g.from_first():
                            vec.wait_ge(scanned, g.n)
                        vec.tensor_tensor_scan(agg[:, g.buf, :], k.same[0:D + 1, bass.ds(g.n * GS, GS)], msg[:, g.buf, :],
                                               agg[:, (g - 1).buf, GS - 1:GS] if g.from_first() else 0.0,
                                               ALU.mult, ALU.add).then_inc(scanned, 1)
                    mask(r - 1, 6, 2)
                    g = r
                    if g.within(EG):
                        vec.wait_ge(rooted, g.n + 1)
                        vec.reciprocal(inverse[:, :], roots[:, :]).then_inc(inverted, 1)
                        vec.wait_ge(inverted, g.n + 1)
                        if g.from_second():
                            vec.wait_ge(turned, (g - 2).n + 1)
                        for side in range(2):
                            scale_rows(vec, ln, cen[:, :, :], inverse[:, :], h1[:, g.buf, :, side, :])
                    mask(r - 1, 8, 4)
                    g = r - 3
                    if g.within(EG):
                        sums = k.bank[2][:, 0:TG * (D + 1)].rearrange("p (t d) -> p t d", d=D + 1)
                        vec.wait_ge(rows_done, g.n + 1)
                        vec.tensor_scalar(deg[:, :], sums[:, :, D], 1.0, None, ALU.max).then_inc(updated, 1)
                        vec.tensor_copy(k.degree[:, bass.ds(g.n * TG, TG)], sums[:, :, D]).then_inc(updated, 1)
                        vec.wait_ge(updated, g.n * 5 + 1)
                        vec.reciprocal(deg[:, :], deg[:, :]).then_inc(updated, 1)
                        vec.wait_ge(updated, g.n * 5 + 3)
                        vec.tensor_tensor(part[:, :, :], sums[:, :, 0:D], deg[:, :].unsqueeze(2).to_broadcast([P, TG, D]),
                                          ALU.mult).then_inc(updated, 1)
                        vec.wait_ge(updated, g.n * 5 + 4)
                        if g.from_second():
                            vec.wait_ge(scattered[g.buf], g.half * (TG * 16))
                        vec.tensor_tensor(x2[:, g.buf], part[:, :, :], k.x_dst[:, bass.ds(g.n * TG, TG), :], ALU.add).then_inc(updated, 1)
                    mask(r - 1, 12, 4)

                rounds(vec, EG, 3, step)

            @block.scalar
            def _(act):
                def step(r):
                    g = r
                    if g.within(EG):
                        act.wait_ge(ln, g.n * 5 + 2)
                        act.activation(squares[:, :, :], cen[:, :, :], ACT.Square, scale=0.125).then_inc(sq_done, 1)
                    g = r - 2
                    if g.within(EG):
                        act.wait_ge(z_used, (g.n + 1) * PAIRS)
                        if g.from_second():
                            act.wait_ge(scanned, (g - 2).n + 1)
                        act.activation(msg[0:D, g.buf, :], k.bank[3 + g.buf][0:D, :], ACT.Copy).then_inc(msg_done, 1)
                    g = r
                    if g.within(EG):
                        act.wait_ge(ln, g.n * 5 + 3)
                        act.activation(roots[:, :], roots[:, :], ACT.Sqrt, bias=k.eps_col[:, 0:1]).then_inc(rooted, 1)
                        act.wait_ge(turned, g.n + 1)
                        if g.from_second():
                            act.wait_ge(z_made, (g - 1).n * PAIRS)
                        act.activation(ht[:, g.buf, :], k.bank[0][:, :], ACT.Copy).then_inc(ht_done, 1)

                rounds(act, EG, 2, step)

            @block.tensor
            def _(pe):
                pe.wait_ge(wrel_in, 16)
                pe.sem_inc(pe_wait, 1)

                def messages(g, first, count):
                    if not g.within(EG):
                        return
                    if first == 0 and g.from_second():
                        pe.wait_ge(msg_done, (g - 1).n)
                    for n in range(first, first + count):
                        pe.wait_ge(z_made, g.n * PAIRS + n + 1)
                        pe.matmul(k.bank[3 + g.buf][0:D, :], wrel[:, n, :], z[:, n % NZ, :],
                                  start=n == 0, stop=n == PAIRS - 1).then_inc(z_used, 1)

                def step(r):
                    messages(r - 1, 0, 8)
                    g = r - 2
                    if g.within(EG):
                        pe.wait_ge(scanned, g.n + 1)
                        if g.from_first():
                            pe.wait_ge(updated, g.n * 5 - 1)
                        pe.sem_inc(pe_wait, 1)
                        for t in range(TG):
                            mm = pe.transpose(k.bank[2][:, t * (D + 1):(t + 1) * (D + 1)], agg[:, g.buf, t * P:(t + 1) * P],
                                              k.ident[0:D + 1, 0:D + 1])
                        mm.then_inc(rows_done, 1)
                    messages(r - 1, 8, 4)
                    g = r
                    if g.within(EG):
                        pe.wait_ge(ln, g.n * 5 + 5)
                        if g.from_first():
                            pe.wait_ge(ht_done, g.n)
                        pe.sem_inc(pe_wait, 1)
                        for t in range(TG):
                            mm = pe.transpose(k.bank[0][:, t * P:(t + 1) * P], h1[:, g.buf, t].rearrange("p s d -> p (s d)"),
                                              k.ident[:, :])
                        mm.then_inc(turned, 1)
                    messages(r - 1, 12, 4)

                rounds(pe, EG, 2, step)


def layer2(nc, k):
    with ExitStack() as ctx:
        def sb(name, shape, dt=F32):
            return k.sb(name, shape, dt, ctx)

        def sem(name):
            return k.sem(name, ctx)

        SIDES = 2 * TG
        xx = sb("l2_xx", [P, 2, TG, 2, D])
        h = sb("l2_h", [P, 2, TG, 2, D])
        squares = sb("l2_squares", [P, SIDES, D])
        h_squares = sb("l2_h_squares", [P, SIDES, D])
        stats = sb("l2_stats", [P, SIDES])
        roots = sb("l2_roots", [P, SIDES])
        inverse = sb("l2_inverse", [P, SIDES])
        prod = sb("l2_prod", [P, TG, D])
        dot = sb("l2_dot", [P, TG])
        norms = sb("l2_norms", [P, TG, 2])
        scale = sb("l2_scale", [P, TG])
        score = sb("l2_score", [P, TG])
        e = sb("l2_e", [P, 2, TG])
        v = sb("l2_v", [P, TG, D + 1])
        key_row = sb("l2_key_row", [P, 2, GS])
        equal = sb("l2_equal", [P, TG, GS])
        earlier = sb("l2_earlier", [P, TG, GS], BF16)
        junk = sb("l2_junk", [P, TG, GS], BF16)
        before = sb("l2_before", [P, TG])
        away = sb("l2_away", [P, TG])
        drop_i = sb("l2_drop_i", [P, TG], I32)
        drop = sb("l2_drop", [P, TG])
        sums = sb("l2_sums", [P, 2, TG, D + 1])
        src_ring = sb("l2_src_ring", [P, 2, TG], I32)
        dst_ring = sb("l2_dst_ring", [P, 2, TG], I32)
        add_ring = sb("l2_add_ring", [P, 2, TG], I32)

        gathered, kept, key_in = (k.pair_of_sems("l2_" + n, ctx) for n in ("gathered", "kept", "key_in"))
        ln, dots, packed = sem("l2_ln"), sem("l2_dots"), sem("l2_packed")
        sq_done, h_sq_done = sem("l2_sq_done"), sem("l2_h_sq_done")
        rooted, normed, inverted, exped = sem("l2_rooted"), sem("l2_normed"), sem("l2_inverted"), sem("l2_exped")
        summed, sums_out, added = sem("l2_summed"), sem("l2_sums_out"), sem("l2_added")
        consts, indexed = sem("l2_consts"), sem("l2_indexed")
        pe_wait, pool_wait, idx_copied = sem("l2_pe_wait"), sem("l2_pool_wait"), sem("l2_idx_copied")
        PACK = 7 + 2 * TG

        def sides(a, g):
            return a[:, g.buf].rearrange("p t s d -> p (t s) d")

        with nc.Block() as block:
            @block.sync
            def _(sp):
                def step(r):
                    g = r
                    if g.within(EG):
                        if g.from_second():
                            sp.wait_ge(packed, (g - 1).n * PACK)
                        sp.dma_start(key_row[:, g.buf, :], k.src_row[bass.ds(g.n * GS, GS)].partition_broadcast(P)
                                     ).then_inc(key_in[g.buf], 16)
                    g = r - 1
                    if g.within(EG):
                        sp.wait_ge(gathered[g.buf], (g.half + 1) * (2 * TG * 16))
                        sp.dma_start(k.x_src[:, bass.ds(g.n * TG, TG), :], xx[:, g.buf, :, 0, :]).then_inc(kept[g.buf], 16)
                        sp.dma_start(k.x_dst[:, bass.ds(g.n * TG, TG), :], xx[:, g.buf, :, 1, :]).then_inc(kept[g.buf], 16)

                rounds(sp, EG, 1, step)
                for b in range(2):
                    sp.wait_ge(kept[b], (EG + 1 - b) // 2 * 32)

            @block.gpsimd
            def _(pool):
                pool.memset(earlier[:, :, :], 1.0).then_inc(consts, 1)
                pool.iota(drop_i[:, :], pattern=[[P, TG]], base=NODES, channel_multiplier=1).then_inc(consts, 1)
                pool.wait_ge(consts, 2)
                pool.affine_select(out=earlier[:, :, :], in_=earlier[:, :, :], compare_op=ALU.is_gt, fill=0.0,
                                   base=0, pattern=[[P, TG], [-1, GS]], channel_multiplier=1).then_inc(consts, 1)

                def step(r):
                    g = r
                    if g.within(EG):
                        if g.from_second():
                            pool.wait_ge(ln, (g - 2).n * 4 + 2)
                            pool.wait_ge(kept[g.buf], g.half * 32)
                        gather_group(pool, g, ((xx[:, g.buf, :, 0, :], k.x2_table, k.src_idx, src_ring),
                                               (xx[:, g.buf, :, 1, :], k.x2_table, k.dst_idx, dst_ring)),
                                     idx_copied, gathered, pool_wait)
                    g = r - 3
                    if g.within(EG):
                        pool.wait_ge(sums_out, g.n + 1)
                        pool.wait_ge(indexed, g.n + 1)
                        if g.from_first():
                            pool.wait_ge(added, g.n * (TG * 16))
                        pool.sem_inc(pool_wait, 1)
                        for t in range(TG):
                            pool.indirect_dma_start(
                                k.sum_table[:, :], bass.IndirectOffsetOnAxis(ap=add_ring[:, g.buf, t:t + 1], axis=0),
                                sums[:, g.buf, t, :], None, compute_op=ALU.add).then_inc(added, 16)

                rounds(pool, EG, 3, step)
                pool.wait_ge(added, EG * TG * 16)

            @block.vector
            def _(vec):
                vec.wait_ge(consts, 3)
                vec.tensor_copy(drop[:, :], drop_i[:, :]).then_inc(consts, 1)

                def step(r):
                    g = r - 2
                    if g.within(EG):
                        vec.wait_ge(exped, g.n + 1)
                        if g.from_first():
                            vec.wait_ge(summed, g.n)
                        vec.tensor_tensor(v[:, :, 0:D], h[:, g.buf, :, 1, :], e[:, g.buf, :].unsqueeze(2).to_broadcast([P, TG, D]),
                                          ALU.mult).then_inc(packed, 1)
                        vec.tensor_copy(v[:, :, D], e[:, g.buf, :]).then_inc(packed, 1)
                        vec.wait_ge(key_in[g.buf], (g.half + 1) * 16)
                        key = k.src_key[:, bass.ds(g.n * TG, TG)]
                        vec.tensor_copy(away[:, :], key).then_inc(packed, 1)
                        vec.wait_ge(packed, g.n * PACK + 3)
                        for t in range(TG):
                            vec.tensor_scalar(equal[:, t, :], key_row[:, g.buf, :], away[:, t:t + 1], None,
                                              ALU.is_equal).then_inc(packed, 1)
                        for t in range(TG):
                            vec.wait_ge(packed, g.n * PACK + 4 + t)
                            vec.scalar_tensor_tensor(out=junk[:, t, :], in0=equal[:, t, :], scalar=1.0, in1=earlier[:, t, :],
                                                     op0=ALU.mult, op1=ALU.mult, accum_out=before[:, t:t + 1]).then_inc(packed, 1)
                        vec.wait_ge(packed, g.n * PACK + 3 + 2 * TG)
                        vec.tensor_scalar(before[:, :], before[:, :], 0.5, None, ALU.is_gt).then_inc(packed, 1)
                        vec.wait_ge(packed, g.n * PACK + 4 + 2 * TG)
                        vec.scalar_tensor_tensor(out=k.first_idx[:, bass.ds(g.n * TG, TG)], in0=before[:, :], scalar=float(FAR),
                                                 in1=away[:, :], op0=ALU.mult, op1=ALU.add).then_inc(packed, 1)
                        vec.tensor_tensor(away[:, :], drop[:, :], away[:, :], ALU.subtract).then_inc(packed, 1)
                        vec.wait_ge(packed, g.n * PACK + 6 + 2 * TG)
                        vec.tensor_tensor(away[:, :], away[:, :], before[:, :], ALU.mult).then_inc(packed, 1)
                        vec.wait_ge(packed, g.n * PACK + 7 + 2 * TG)
                        if g.from_second():
                            vec.wait_ge(added, (g - 1).n * (TG * 16))
                        vec.tensor_tensor(add_ring[:, g.buf, :], away[:, :], key, ALU.add).then_inc(indexed, 1)
                    g = r
                    if g.within(EG):
                        vec.wait_ge(gathered[g.buf], (g.half + 1) * (2 * TG * 16))
                        center_rows(vec, ln, g.n * 4, sides(xx, g), stats[:, :], sides(h, g))
                    g = r - 1
                    if g.within(EG):
                        vec.tensor_tensor(prod[:, :, :], h[:, g.buf, :, 0, :], h[:, g.buf, :, 1, :], ALU.mult).then_inc(dots, 1)
                        vec.wait_ge(dots, g.n * 7 + 1)
                        vec.tensor_reduce(dot[:, :], prod[:, :, :], AX.X, ALU.add).then_inc(dots, 1)
                    g = r
                    if g.within(EG):
                        vec.wait_ge(sq_done, g.n + 1)
                        vec.tensor_reduce(roots[:, :], squares[:, :, :], AX.X, ALU.add).then_inc(ln, 1)
                    g = r - 1
                    if g.within(EG):
                        vec.wait_ge(h_sq_done, g.n + 1)
                        vec.tensor_reduce(norms[:, :, :].rearrange("p t s -> p (t s)"), h_squares[:, :, :], AX.X, ALU.add).then_inc(dots, 1)
                        vec.wait_ge(dots, g.n * 7 + 3)
                        vec.tensor_scalar(norms[:, :, :], norms[:, :, :], 1e-24, None, ALU.max).then_inc(dots, 1)
                    g = r
                    if g.within(EG):
                        vec.wait_ge(rooted, g.n + 1)
                        vec.reciprocal(inverse[:, :], roots[:, :]).then_inc(inverted, 1)
                        vec.wait_ge(inverted, g.n + 1)
                        scale_rows(vec, ln, sides(h, g), inverse[:, :], sides(h, g))
                    g = r - 1
                    if g.within(EG):
                        vec.wait_ge(normed, g.n + 1)
                        vec.tensor_tensor(scale[:, :], norms[:, :, 0], norms[:, :, 1], ALU.mult).then_inc(dots, 1)
                        vec.wait_ge(dots, g.n * 7 + 5)
                        vec.reciprocal(scale[:, :], scale[:, :]).then_inc(dots, 1)
                        vec.wait_ge(dots, g.n * 7 + 6)
                        if g.from_first():
                            vec.wait_ge(exped, g.n)
                        vec.tensor_tensor(score[:, :], dot[:, :], scale[:, :], ALU.mult).then_inc(dots, 1)

                rounds(vec, EG, 2, step)

            @block.scalar
            def _(act):
                def step(r):
                    g = r
                    if g.within(EG):
                        act.wait_ge(ln, g.n * 4 + 2)
                        act.activation(squares[:, :, :], sides(h, g), ACT.Square, scale=0.125).then_inc(sq_done, 1)
                    g = r - 1
                    if g.within(EG):
                        act.activation(h_squares[:, :, :], sides(h, g), ACT.Square).then_inc(h_sq_done, 1)
                    g = r
                    if g.within(EG):
                        act.wait_ge(ln, g.n * 4 + 3)
                        act.activation(roots[:, :], roots[:, :], ACT.Sqrt, bias=k.eps_col[:, 0:1]).then_inc(rooted, 1)
                    g = r - 1
                    if g.within(EG):
                        act.wait_ge(dots, g.n * 7 + 4)
                        act.activation(norms[:, :, :], norms[:, :, :], ACT.Sqrt).then_inc(normed, 1)
                    g = r - 2
                    if g.within(EG):
                        act.wait_ge(summed, g.n + 1)
                        if g.from_second():
                            act.wait_ge(added, (g - 1).n * (TG * 16))
                        act.activation(sums[:, g.buf], k.bank[0][:, 0:TG * (D + 1)].rearrange("p (t d) -> p t d", d=D + 1),
                                       ACT.Copy).then_inc(sums_out, 1)
                    g = r - 1
                    if g.within(EG):
                        act.wait_ge(dots, g.n * 7 + 7)
                        if g.from_second():
                            act.wait_ge(packed, (g - 1).n * PACK)
                        act.activation(e[:, g.buf, :], score[:, :], ACT.Exp).then_inc(exped, 1)

                rounds(act, EG, 2, step)

            @block.tensor
            def _(pe):
                def step(g):
                    pe.wait_ge(packed, g.n * PACK + 3 + TG)
                    if g.from_first():
                        pe.wait_ge(sums_out, g.n)
                    pe.sem_inc(pe_wait, 1)
                    for t in range(TG):
                        for u in range(TG):
                            mm = pe.matmul(k.bank[0][:, t * (D + 1):(t + 1) * (D + 1)], equal[:, u, t * P:(t + 1) * P],
                                           v[:, u, :], start=u == 0, stop=u == TG - 1)
                    mm.then_inc(summed, 1)

                rounds(pe, EG, 0, step)


def layer3(nc, k):
    with ExitStack() as ctx:
        def sb(name, shape, dt=F32):
            return k.sb(name, shape, dt, ctx)

        def sem(name):
            return k.sem(name, ctx)

        ss = sb("l3_ss", [P, 2, TG, 2, D + 1])
        total = sb("l3_total", [P, TG, 2])
        change = sb("l3_change", [P, TG, 2, D])
        x3 = sb("l3_x3", [P, TG, D])
        outs = sb("l3_outs", [P, 2, TG, D])
        h = sb("l3_h", [P, 2, TG, D])
        squares = sb("l3_squares", [P, 2, TG, D])
        stats = sb("l3_stats", [P, 2, TG])
        roots = sb("l3_roots", [P, 2, TG])
        inverse = sb("l3_inverse", [P, 2, TG])
        ht = sb("l3_ht", [D, GS])
        msg = sb("l3_msg", [D, 2, GS])
        agg = sb("l3_agg", [D, 2, GS])
        deg = sb("l3_deg", [P, TG])
        mean = sb("l3_mean", [P, TG, D])
        y = sb("l3_y", [P, TG, D])
        src_ring = sb("l3_src_ring", [P, 2, TG], I32)
        dst_ring = sb("l3_dst_ring", [P, 2, TG], I32)
        first_ring = sb("l3_first_ring", [P, 2, TG], I32)

        gathered, scattered = k.pair_of_sems("l3_gathered", ctx), k.pair_of_sems("l3_scattered", ctx)
        lna, lnb = sem("l3_lna"), sem("l3_lnb")
        sqa_done, sqb_done, rooted, inverted = sem("l3_sqa_done"), sem("l3_sqb_done"), sem("l3_rooted"), sem("l3_inverted")
        turned, ht_done, m_done, msg_done = sem("l3_turned"), sem("l3_ht_done"), sem("l3_m"), sem("l3_msg_done")
        scanned, rows_done = sem("l3_scanned"), sem("l3_rows")
        pe_wait, pool_wait, idx_copied, first_copied = (sem("l3_" + n) for n in ("pe_wait", "pool_wait", "idx_copied", "first_copied"))

        def x_dst(g):
            return k.x_dst[:, bass.ds(g.n * TG, TG), :]

        def x_src(g):
            return k.x_src[:, bass.ds(g.n * TG, TG), :]

        def live(r):
            return (0 if r.within(EG) else 1), (2 if (r - 3).within(EG) else 1)

        with nc.Block() as block:
            @block.gpsimd
            def _(pool):
                def step(r):
                    g = r
                    if g.within(EG):
                        if g.from_second():
                            pool.wait_ge(lna, (g - 2).n * 10 + 3)
                        gather_group(pool, g, ((ss[:, g.buf, :, 0, :], k.sum_table, k.src_idx, src_ring),
                                               (ss[:, g.buf, :, 1, :], k.sum_table, k.dst_idx, dst_ring)),
                                     idx_copied, gathered, pool_wait)
                    g = r - 1
                    if g.within(EG):
                        if g.from_first():
                            pool.wait_ge(scattered[(g - 1).buf], ((g - 1).half + 1) * (TG * 16))
                        scatter_group(pool, g, outs, lna, g.n * 10 + 6, k.out, k.first_idx, first_ring,
                                      first_copied, scattered, pool_wait)

                rounds(pool, EG, 1, step)
                for b in range(2):
                    pool.wait_ge(scattered[b], (EG + 1 - b) // 2 * TG * 16)

            @block.vector
            def _(vec):
                def step(r):
                    g = r
                    if g.within(EG):
                        n = g.n * 10
                        vec.wait_ge(gathered[g.buf], (g.half + 1) * (2 * TG * 16))
                        vec.tensor_scalar(total[:, :, :], ss[:, g.buf, :, :, D], TINY, None, ALU.max).then_inc(lna, 1)
                        vec.wait_ge(lna, n + 1)
                        vec.reciprocal(total[:, :, :], total[:, :, :]).then_inc(lna, 1)
                        vec.wait_ge(lna, n + 2)
                        vec.tensor_tensor(change[:, :, :, :].rearrange("p t s d -> p (t s) d"),
                                          ss[:, g.buf, :, :, 0:D].rearrange("p t s d -> p (t s) d"),
                                          total[:, :, :].rearrange("p t s -> p (t s)").unsqueeze(2).to_broadcast([P, 2 * TG, D]),
                                          ALU.mult).then_inc(lna, 1)
                        vec.wait_ge(lna, n + 3)
                        vec.tensor_tensor(x3[:, :, :], change[:, :, 0, :], x_src(g), ALU.add).then_inc(lna, 1)
                        vec.tensor_tensor(x_dst(g), change[:, :, 1, :], x_dst(g), ALU.add).then_inc(lna, 1)
                        vec.wait_ge(lna, n + 4)
                        if g.from_second():
                            vec.wait_ge(scattered[g.buf], g.half * (TG * 16))
                        vec.tensor_tensor(outs[:, g.buf], x3[:, :, :], k.beta_b[:, :].unsqueeze(1).to_broadcast([P, TG, D]),
                                          ALU.add).then_inc(lna, 1)
                        if g.from_second():
                            vec.wait_ge(turned, (g - 2).n + 1)
                        center_rows(vec, lna, n + 6, x3[:, :, :], stats[:, 0, :], h[:, g.buf])
                    g = r - 2
                    if g.within(EG):
                        vec.wait_ge(msg_done, g.n + 1)
                        if g.from_second():
                            vec.wait_ge(rows_done, (g - 2).n + 1)
                        if g.from_first():
                            vec.wait_ge(scanned, g.n)
                        vec.tensor_tensor_scan(agg[:, g.buf, :], k.same[0:D, bass.ds(g.n * GS, GS)], msg[:, g.buf, :],
                                               agg[:, (g - 1).buf, GS - 1:GS] if g.from_first() else 0.0,
                                               ALU.mult, ALU.add).then_inc(scanned, 1)
                    g = r - 3
                    if g.within(EG):
                        n = g.n * 10
                        sums = k.bank[2][:, 0:TG * D].rearrange("p (t d) -> p t d", d=D)
                        vec.tensor_scalar(deg[:, :], k.degree[:, bass.ds(g.n * TG, TG)], 1e-6, None, ALU.add).then_inc(lnb, 1)
                        vec.wait_ge(lnb, n + 1)
                        vec.reciprocal(deg[:, :], deg[:, :]).then_inc(lnb, 1)
                        vec.wait_ge(lnb, n + 2)
                        vec.wait_ge(rows_done, g.n + 1)
                        vec.scalar_tensor_tensor(out=mean[:, :, :], in0=sums, scalar=0.0,
                                                 in1=deg[:, :].unsqueeze(2).to_broadcast([P, TG, D]),
                                                 op0=ALU.max, op1=ALU.mult).then_inc(lnb, 1)
                        vec.wait_ge(lnb, n + 3)
                        center_rows(vec, lnb, n + 3, mean[:, :, :], stats[:, 1, :], y[:, :, :])
                    lo, hi = live(r)
                    if lo >= hi:
                        return
                    for m, g, ln, done in ((0, r, lna, sqa_done), (1, r - 3, lnb, sqb_done)):
                        if g.within(EG):
                            vec.wait_ge(done, g.n + 1)
                            vec.tensor_reduce(roots[:, m, :], squares[:, m], AX.X, ALU.add).then_inc(ln, 1)
                    vec.wait_ge(rooted, r.n + 1)
                    vec.reciprocal(inverse[:, lo:hi, :], roots[:, lo:hi, :]).then_inc(inverted, 1)
                    vec.wait_ge(inverted, r.n + 1)
                    g = r
                    if g.within(EG):
                        scale_rows(vec, lna, h[:, g.buf], inverse[:, 0, :], h[:, g.buf])
                    g = r - 3
                    if g.within(EG):
                        n = g.n * 10
                        scale_rows(vec, lnb, y[:, :, :], inverse[:, 1, :], y[:, :, :], relu=False)
                        vec.wait_ge(lnb, n + 7)
                        vec.tensor_tensor(y[:, :, :], y[:, :, :], k.gamma_b[:, :].unsqueeze(1).to_broadcast([P, TG, D]),
                                          ALU.mult).then_inc(lnb, 1)
                        vec.wait_ge(lnb, n + 8)
                        vec.tensor_tensor(y[:, :, :], y[:, :, :], k.beta_b[:, :].unsqueeze(1).to_broadcast([P, TG, D]),
                                          ALU.add).then_inc(lnb, 1)
                        vec.wait_ge(lnb, n + 9)
                        vec.tensor_tensor(x_dst(g), x_dst(g), y[:, :, :], ALU.add).then_inc(lnb, 1)

                rounds(vec, EG, 3, step)

            @block.scalar
            def _(act):
                def step(r):
                    g = r
                    if g.within(EG):
                        act.wait_ge(lna, g.n * 10 + 8)
                        act.activation(squares[:, 0], h[:, g.buf], ACT.Square, scale=0.125).then_inc(sqa_done, 1)
                    g = r - 3
                    if g.within(EG):
                        act.wait_ge(lnb, g.n * 10 + 5)
                        act.activation(squares[:, 1], y[:, :, :], ACT.Square, scale=0.125).then_inc(sqb_done, 1)
                    lo, hi = live(r)
                    if lo < hi:
                        if r.within(EG):
                            act.wait_ge(lna, r.n * 10 + 9)
                        if (r - 3).within(EG):
                            act.wait_ge(lnb, (r - 3).n * 10 + 6)
                        act.activation(roots[:, lo:hi, :], roots[:, lo:hi, :], ACT.Sqrt, bias=k.eps_col[:, 0:1]).then_inc(rooted, 1)
                    g = r
                    if g.within(EG):
                        act.wait_ge(turned, g.n + 1)
                        if g.from_first():
                            act.wait_ge(m_done, g.n)
                        act.activation(ht[:, :], k.bank[0][0:D, :], ACT.Copy).then_inc(ht_done, 1)
                        act.wait_ge(m_done, g.n + 1)
                        if g.from_second():
                            act.wait_ge(scanned, (g - 2).n + 1)
                        act.activation(msg[:, g.buf, :], k.bank[1][0:D, :], ACT.Identity, bias=k.b3c[:, 0:1]).then_inc(msg_done, 1)

                rounds(act, EG, 3, step)

            @block.tensor
            def _(pe):
                def step(r):
                    g = r
                    if g.within(EG):
                        pe.wait_ge(lna, g.n * 10 + 10)
                        if g.from_first():
                            pe.wait_ge(ht_done, g.n)
                        pe.sem_inc(pe_wait, 1)
                        for t in range(TG):
                            mm = pe.transpose(k.bank[0][0:D, t * P:(t + 1) * P], h[:, g.buf, t, :], k.ident[:, :])
                        mm.then_inc(turned, 1)
                    g = r - 2
                    if g.within(EG):
                        pe.wait_ge(scanned, g.n + 1)
                        if g.from_first():
                            pe.wait_ge(lnb, g.n * 10 - 7)
                        pe.sem_inc(pe_wait, 1)
                        for t in range(TG):
                            mm = pe.transpose(k.bank[2][:, t * D:(t + 1) * D], agg[:, g.buf, t * P:(t + 1) * P], k.ident[0:D, 0:D])
                        mm.then_inc(rows_done, 1)
                    g = r
                    if g.within(EG):
                        pe.wait_ge(ht_done, g.n + 1)
                        if g.from_first():
                            pe.wait_ge(msg_done, g.n)
                        pe.sem_inc(pe_wait, 1)
                        pe.matmul(k.bank[1][0:D, :], k.w3[:, :], ht[:, :], start=True, stop=True).then_inc(m_done, 1)

                rounds(pe, EG, 2, step)


def write_last(nc, k):
    with ExitStack() as ctx:
        rows = k.sb("out_rows", [P, 2, TG, D], F32, ctx)
        last_ring = k.sb("out_last_ring", [P, 2, TG], I32, ctx)
        copied, idx_copied, pool_wait, act_wait = (
            k.sem("out_" + n, ctx) for n in ("copied", "idx_copied", "pool_wait", "act_wait"))
        scattered = k.pair_of_sems("out_scattered", ctx)

        with nc.Block() as block:
            @block.scalar
            def _(act):
                def step(g):
                    if g.from_second():
                        act.wait_ge(scattered[g.buf], g.half * (TG * 16))
                        act.sem_inc(act_wait, 1)
                    act.activation(rows[:, g.buf], k.x_dst[:, bass.ds(g.n * TG, TG), :], ACT.Copy).then_inc(copied, 1)

                rounds(act, EG, 0, step)

            @block.gpsimd
            def _(pool):
                def step(g):
                    scatter_group(pool, g, rows, copied, g.n + 1, k.out, k.last_idx, last_ring, idx_copied, scattered, pool_wait)

                rounds(pool, EG, 0, step)
                for b in range(2):
                    pool.wait_ge(scattered[b], (EG + 1 - b) // 2 * TG * 16)


_INS = ["x", "src", "dst", "edge_attr_32", "edge_type_32", "L0_gnn_w_m1", "L0_gnn_b_m1", "L0_gnn_w_m2",
        "L0_gnn_b_m2", "L0_gnn_w_u1", "L0_gnn_b_u1", "L0_gnn_w_u2", "L0_gnn_b_u2", "L1_gnn_basis",
        "L1_gnn_coeff", "L1_gnn_self_weight", "L1_gnn_bias", "L3_gnn_W", "L3_gnn_b", "L3_gnn_gamma",
        "L3_gnn_beta"]
_TURNED = ("L1_gnn_coeff", "L3_gnn_W")


def kernel(**inputs):
    import numpy as _np
    import concourse.bacc as _bacc
    from concourse import mybir as _mybir
    from concourse.bass_utils import run_bass_kernel_spmd as _run

    nc = _bacc.Bacc("TRN2", target_bir_lowering=False, num_devices=1)
    arrays, args = {}, []
    for name in _INS:
        a = _np.asarray(inputs[name])
        a = _np.ascontiguousarray(a.T if name in _TURNED else a)
        arrays[f"in_{name}_dram"] = a
        args.append(nc.dram_tensor(f"in_{name}_dram", a.shape, _mybir.dt.from_np(a.dtype), kind="ExternalInput").ap())
    out = nc.dram_tensor("out_0_dram", (NODES, D), _mybir.dt.float32, kind="ExternalOutput").ap()
    build(nc, *args, out)
    r = _run(nc, [arrays], core_ids=[0])
    return r.results[0]["out_0_dram"]
```

```python
from contextlib import ExitStack

import concourse.bass as bass
from concourse import mybir
from concourse.alu_op_type import AluOpType as ALU

ACT = mybir.ActivationFunctionType
F32 = mybir.dt.float32
BF16 = mybir.dt.bfloat16
I32 = mybir.dt.int32
AX = mybir.AxisListType

P = 128
NODES = 50000
EDGES = 25000
D = 64
ED = 32
H = 128
RELS = 32
BASES = 30

TG = 4
GS = TG * P
EG = -(-EDGES // GS)
SLOTS = EG * GS
ET = SLOTS // P
PAD = SLOTS - EDGES
ROWS = ET // 2
FAR = 65536

NP = 125
NPP = NODES // NP
NG = 8
DG = NPP // NG
HALF = NG // 2 * NP

CLEAR = -(-(NODES + GS) // (P * EG))
SUM_ROWS = CLEAR * P * EG
TINY = 1e-30
LN_EPS = 1e-5
COUNT_CHUNK = SLOTS // 7


BIAS_ROWS = 65


class Group:

    def __init__(self, pair, off):
        self.pair, self.off = pair, off

    def __sub__(self, k):
        return Group(self.pair, self.off - k)

    def __add__(self, k):
        return Group(self.pair, self.off + k)

    @property
    def n(self):
        return self.pair * 2 + self.off

    @property
    def half(self):
        return self.pair + self.off // 2

    @property
    def buf(self):
        return self.off % 2

    def within(self, count):
        return not isinstance(self.pair, int) or 0 <= self.off < count

    def from_first(self):
        return not isinstance(self.pair, int) or self.off >= 1

    def from_second(self):
        return not isinstance(self.pair, int) or self.off >= 2


def rounds(eng, groups, skew, step):
    first = (skew + 3) // 2 * 2
    last = groups // 2 * 2
    for r in range(first):
        step(Group(0, r))
    with eng.Fori(first // 2, last // 2) as pair:
        step(Group(pair, 0))
        step(Group(pair, 1))
    for r in range(last, groups + skew):
        step(Group(0, r))


def center_rows(vec, done, n, rows, total, centered):
    vec.tensor_reduce(total, rows, AX.X, ALU.add).then_inc(done, 1)
    vec.wait_ge(done, n + 1)
    vec.scalar_tensor_tensor(out=centered, in0=rows, scalar=float(D),
                             in1=total.unsqueeze(2).to_broadcast(list(centered.shape)),
                             op0=ALU.mult, op1=ALU.subtract).then_inc(done, 1)


def scale_rows(vec, done, centered, inverse, out, relu=True):
    scale = inverse.unsqueeze(2).to_broadcast(list(out.shape))
    if relu:
        vec.scalar_tensor_tensor(out=out, in0=centered, scalar=0.0, in1=scale,
                                 op0=ALU.max, op1=ALU.mult).then_inc(done, 1)
    else:
        vec.tensor_tensor(out, centered, scale, ALU.mult).then_inc(done, 1)


class Shared:
    pass


def build(nc, x, src, dst, attr, etype, w_m1, b_m1, w_m2, b_m2, w_u1, b_u1, w_u2, b_u2,
          basis, coeff_t, w_self, b_rel, w3_t, b3, gamma, beta, out):
    k = Shared()
    k.x, k.src, k.dst, k.attr, k.etype = x, src, dst, attr, etype
    k.w_m1, k.b_m1, k.w_m2, k.b_m2, k.w_u1, k.b_u1, k.w_u2, k.b_u2 = w_m1, b_m1, w_m2, b_m2, w_u1, b_u1, w_u2, b_u2
    k.basis, k.coeff_t, k.w_self, k.b_rel = basis, coeff_t, w_self, b_rel
    k.w3_t, k.b3, k.gamma, k.beta, k.out = w3_t, b3, gamma, beta, out
    k.src_s = nc.dram_tensor("src_s", [SLOTS, 1], I32)
    k.dst_s = nc.dram_tensor("dst_s", [SLOTS + 2, 1], I32)
    k.typ_s = nc.dram_tensor("typ_s", [SLOTS, 1], I32)
    k.attr_s = nc.dram_tensor("attr_s", [SLOTS, ED], F32)
    k.src_r = nc.dram_tensor("src_r", [SLOTS, 1], I32)
    k.dst_r = nc.dram_tensor("dst_r", [SLOTS, 1], I32)
    k.typ_r = nc.dram_tensor("typ_r", [SLOTS, 1], I32)
    k.attr_r = nc.dram_tensor("attr_r", [SLOTS, ED], F32)
    k.same_row = nc.dram_tensor("same_row", [SLOTS], BF16)
    k.type_row = nc.dram_tensor("type_row", [SLOTS], F32)
    k.src_row = nc.dram_tensor("src_row", [SLOTS], F32)
    k.rel_rows = nc.dram_tensor("rel_rows", [RELS, D * D], F32)
    k.x1_table = nc.dram_tensor("x1_table", [NODES, D], F32)
    k.x2_table = nc.dram_tensor("x2_table", [NODES, D], F32)
    k.sum_table = nc.dram_tensor("sum_table", [SUM_ROWS, D + 1], F32)

    with ExitStack() as ctx:
        def sb(name, shape, dt=F32, stack=ctx):
            return stack.enter_context(nc.sbuf_tensor(name, shape, dt))

        def sem(name, stack=ctx):
            return stack.enter_context(nc.semaphore(name))

        def pair_of_sems(name, stack=ctx):
            return [sem(name + "0", stack), sem(name + "1", stack)]

        k.sb, k.sem, k.pair_of_sems = sb, sem, pair_of_sems

        k.bank = [ctx.enter_context(nc.psum_tensor(f"bank{i}", [P, 512], F32)) for i in range(8)]

        k.slots = sb("slots", [P, 2 * ET * D])
        k.x_dst = k.slots[:, 0:ET * D].rearrange("p (t d) -> p t d", d=D)
        k.x_src = k.slots[:, ET * D:2 * ET * D].rearrange("p (t d) -> p t d", d=D)
        k.same = sb("same", [P, SLOTS], BF16)
        k.src_idx = sb("src_idx", [P, ET], I32)
        k.dst_idx = sb("dst_idx", [P, ET], I32)
        k.last_idx = sb("last_idx", [P, ET], I32)
        k.src_key = sb("src_key", [P, ET])
        k.degree = sb("degree", [P, ET])
        k.ident = sb("ident", [P, P])
        k.ones = sb("ones", [BIAS_ROWS, P], BF16)
        k.eps_col = sb("eps_col", [P, 1])
        k.wm1 = sb("wm1", [P, H])
        k.wm1e = sb("wm1e", [ED, H])
        k.wm2 = sb("wm2", [P, H])
        k.wu1x = sb("wu1x", [P, H])
        k.wu1a = sb("wu1a", [P, H])
        k.wu2 = sb("wu2", [P, D])
        k.wself = sb("wself", [P, P])
        k.w3 = sb("w3", [D, D])
        k.relcol = sb("relcol", [P, RELS // 2])
        k.bm1 = sb("bm1", [P, 1])
        k.bm2 = sb("bm2", [P, 1])
        k.bu1 = sb("bu1", [P, 1])
        k.b3c = sb("b3c", [D, 1])
        k.bu2_parts = sb("bu2_parts", [BIAS_ROWS, D], BF16)
        k.brel_parts = sb("brel_parts", [BIAS_ROWS, D], BF16)
        k.gamma_b = sb("gamma_b", [P, D])
        k.beta_b = sb("beta_b", [P, D])

        prepare(nc, k)
        dense(nc, k)
        layer0(nc, k)
        layer1(nc, k)
        layer2(nc, k)
        layer3(nc, k)
        write_last(nc, k)


def prepare(nc, k):
    with ExitStack() as ctx:
        def sb(name, shape, dt=F32):
            return k.sb(name, shape, dt, ctx)

        def sem(name):
            return k.sem(name, ctx)

        zero_attr = sb("zero_attr", [PAD, ED])
        zero_pad = sb("zero_pad", [1, PAD], I32)
        src_pad = sb("src_pad", [1, PAD], I32)
        dst_pad = sb("dst_pad", [1, PAD + 2], I32)
        cur_i = sb("cur_i", [ROWS, 2, P], I32)
        prev_i = sb("prev_i", [ROWS, 2, P], I32)
        next_i = sb("next_i", [ROWS, 2, P], I32)
        src_i = sb("src_i", [ROWS, 2, P], I32)
        typ_i = sb("typ_i", [ROWS, 2, P], I32)
        cur = sb("cur", [ROWS, 2, P])
        prev = sb("prev", [ROWS, 2, P])
        nxt = sb("nxt", [ROWS, 2, P])
        srcf = sb("srcf", [ROWS, 2, P])
        typf = sb("typf", [ROWS, 2, P])
        same_t = sb("same_t", [ROWS, 2, P], BF16)
        gath = sb("gath", [ROWS, 2, P])
        src_in = sb("src_in", [ROWS, 2, P])
        scat = sb("scat", [ROWS, 2, P])
        falls = sb("falls", [ROWS, 2 * P])
        falls_sum = sb("falls_sum", [ROWS, 1])
        ones_col = sb("ones_col", [P, 1])
        flag = sb("flag", [1, 1], I32)
        bias_left = sb("bias_left", [BIAS_ROWS, 2, D])
        bias_part = sb("bias_part", [BIAS_ROWS, 2, D], BF16)
        rel_iota = sb("rel_iota", [P, RELS // 2], I32)
        coeff = sb("coeff", [BASES, RELS])
        room = k.same[:, :].bitcast(F32)
        basis_t = room[0:BASES, 0:D * D]
        rel = room[0:RELS, D * D:2 * D * D]
        junk = k.same[:, 4 * D * D:4 * D * D + COUNT_CHUNK]
        tri = sb("tri", [P, P])
        own = sb("own", [P, P])
        counts = sb("counts", [P, SLOTS // COUNT_CHUNK + 1])
        tile_dst_i = sb("tile_dst_i", [P, 1], I32)
        tile_src_i = sb("tile_src_i", [P, 1], I32)
        tile_typ_i = sb("tile_typ_i", [P, 1], I32)
        tile_attr = sb("tile_attr", [P, ED])
        tile_dst = sb("tile_dst", [P, 1])
        tile_half = sb("tile_half", [P, 1])
        rank = sb("rank", [P, 1])
        rank_i = sb("rank_i", [P, 1], I32)

        pads = sem("pads")
        copied = sem("copied")
        order_in = sem("order_in")
        order_v = sem("order_v")
        falls_added = sem("falls_added")
        flag_ready = sem("flag_ready")
        weights_in = sem("weights_in")
        arrays_in = sem("arrays_in")
        arrays_v = sem("arrays_v")
        turned = sem("turned")
        idx_ready = sem("idx_ready")
        rows_out = sem("rows_out")
        same_in = sem("same_in")
        consts = sem("consts")
        bias_in, bias_v = sem("bias_in"), sem("bias_v")
        coeff_in = sem("coeff_in")
        rel_mm = sem("rel_mm")
        rel_copied = sem("rel_copied")
        rel_out = sem("rel_out")
        wide_in = sem("wide_in")
        wide_v = sem("wide_v")
        tile_in = sem("tile_in")
        rank_v = sem("rank_v")
        ranked_out = sem("ranked_out")
        rank_wait = sem("rank_wait")
        back = sem("back")

        STEPS = SLOTS // COUNT_CHUNK * 2 + 7
        wide = k.slots[:, 0:SLOTS]

        def square(a, first=0):
            return a[first:first + SLOTS, 0].rearrange("(a q f) -> q a f", a=2, f=P)

        with nc.Block() as block:
            @block.sync
            def _(sp):
                sp.dma_start(k.dst_s[1:1 + EDGES, 0].rearrange("(a b) -> a b", a=200),
                             k.dst.rearrange("(a b) -> a b", a=200)).then_inc(copied, 16)
                sp.wait_ge(pads, 6)
                sp.dma_start(k.dst_s[0:1, :].rearrange("a b -> b a"), dst_pad[:, 0:1]).then_inc(copied, 16)
                sp.dma_start(k.dst_s[1 + EDGES:SLOTS + 2, :].rearrange("a b -> b a"),
                             dst_pad[:, 1:PAD + 2]).then_inc(copied, 16)
                sp.dma_start(k.src_s[0:EDGES, 0].rearrange("(a b) -> a b", a=200),
                             k.src.rearrange("(a b) -> a b", a=200)).then_inc(copied, 16)
                sp.dma_start(k.typ_s[0:EDGES, 0].rearrange("(a b) -> a b", a=200),
                             k.etype.rearrange("(a b) -> a b", a=200)).then_inc(copied, 16)
                sp.dma_start(k.src_s[EDGES:SLOTS, :].rearrange("a b -> b a"), src_pad[:, :]).then_inc(copied, 16)
                sp.dma_start(k.typ_s[EDGES:SLOTS, :].rearrange("a b -> b a"), zero_pad[:, :]).then_inc(copied, 16)
                sp.dma_start(k.attr_s[0:EDGES, :].rearrange("(a b) d -> a (b d)", a=200),
                             k.attr.rearrange("(a b) d -> a (b d)", a=200)).then_inc(copied, 16)
                sp.dma_start(k.attr_s[EDGES:SLOTS, :], zero_attr[:, :]).then_inc(copied, 16)
                sp.wait_ge(copied, 9 * 16)
                sp.dma_start(cur_i[:, :, :], square(k.dst_s, 1)).then_inc(order_in, 16)
                sp.dma_start(prev_i[:, :, :], square(k.dst_s, 0)).then_inc(order_in, 16)
                sp.dma_start(bias_left[:, 0, :], k.b_u2.partition_broadcast(BIAS_ROWS)).then_inc(bias_in, 16)
                sp.dma_start(bias_left[:, 1, :], k.b_rel.partition_broadcast(BIAS_ROWS)).then_inc(bias_in, 16)
                sp.dma_start(coeff[:, :], k.coeff_t[:, :]).then_inc(coeff_in, 16)
                sp.dma_start(basis_t, k.basis.rearrange("b i o -> b (i o)")).then_inc(coeff_in, 16)
                loads = [(k.wm1[:, :], k.w_m1[0:P, :]), (k.wm1e[:, :], k.w_m1[P:P + ED, :]),
                         (k.wm2[:, :], k.w_m2[:, :]), (k.wu1x[0:D, :], k.w_u1[0:D, :]),
                         (k.wu1x[D:P, :], k.w_u1[0:D, :]), (k.wu1a[:, :], k.w_u1[D:D + H, :]),
                         (k.wu2[:, :], k.w_u2[:, :]), (k.wself[0:D, 0:D], k.w_self[:, :]),
                         (k.wself[D:P, D:P], k.w_self[:, :]), (k.w3[:, :], k.w3_t[:, :]),
                         (k.bm1[:, :], k.b_m1.unsqueeze(1)), (k.bm2[:, :], k.b_m2.unsqueeze(1)),
                         (k.bu1[:, :], k.b_u1.unsqueeze(1)), (k.b3c[:, :], k.b3.unsqueeze(1)),
                         (k.gamma_b[:, :], k.gamma.partition_broadcast(P)),
                         (k.beta_b[:, :], k.beta.partition_broadcast(P))]
                for to, frm in loads:
                    sp.dma_start(to, frm).then_inc(weights_in, 16)

                sp.wait_ge(flag_ready, 1)
                unsorted = sp.value_load(flag[0:1, 0:1], min_val=0, max_val=SLOTS)
                with sp.If(unsorted > 0):
                    sp.dma_start(wide.bitcast(I32), k.dst_s[1:1 + SLOTS, 0].partition_broadcast(P)).then_inc(wide_in, 16)

                    def load_tile(t):
                        sp.dma_start(tile_dst_i[:, :], k.dst_s[bass.ds(t * P + 1, P), :]).then_inc(tile_in, 16)
                        sp.dma_start(tile_src_i[:, :], k.src_s[bass.ds(t * P, P), :]).then_inc(tile_in, 16)
                        sp.dma_start(tile_typ_i[:, :], k.typ_s[bass.ds(t * P, P), :]).then_inc(tile_in, 16)
                        sp.dma_start(tile_attr[:, :], k.attr_s[bass.ds(t * P, P), :]).then_inc(tile_in, 16)

                    load_tile(0)
                    with sp.Fori(1, ET) as t:
                        sp.wait_ge(ranked_out, t * 64)
                        load_tile(t)
                    sp.wait_ge(ranked_out, ET * 64)
                    sp.dma_start(k.dst_s[1:1 + SLOTS, 0].rearrange("(a b) -> a b", a=P),
                                 k.dst_r[:, 0].rearrange("(a b) -> a b", a=P)).then_inc(back, 16)
                    sp.dma_start(k.src_s[:, 0].rearrange("(a b) -> a b", a=P),
                                 k.src_r[:, 0].rearrange("(a b) -> a b", a=P)).then_inc(back, 16)
                    sp.dma_start(k.typ_s[:, 0].rearrange("(a b) -> a b", a=P),
                                 k.typ_r[:, 0].rearrange("(a b) -> a b", a=P)).then_inc(back, 16)
                    sp.dma_start(k.attr_s[:, :].rearrange("(a b) d -> a (b d)", a=P),
                                 k.attr_r[:, :].rearrange("(a b) d -> a (b d)", a=P)).then_inc(back, 16)
                    sp.wait_ge(back, 64)

                sp.dma_start(cur_i[:, :, :], square(k.dst_s, 1)).then_inc(arrays_in, 16)
                sp.dma_start(prev_i[:, :, :], square(k.dst_s, 0)).then_inc(arrays_in, 16)
                sp.dma_start(next_i[:, :, :], square(k.dst_s, 2)).then_inc(arrays_in, 16)
                sp.dma_start(src_i[:, :, :], square(k.src_s)).then_inc(arrays_in, 16)
                sp.dma_start(typ_i[:, :, :], square(k.typ_s)).then_inc(arrays_in, 16)
                sp.wait_ge(arrays_v, 6)
                sp.dma_start(k.same_row[:].rearrange("(a q f) -> q a f", a=2, f=P), same_t[:, :, :]).then_inc(rows_out, 16)
                sp.dma_start(k.type_row[:].rearrange("(a q f) -> q a f", a=2, f=P), typf[:, :, :]).then_inc(rows_out, 16)
                sp.dma_start(k.src_row[:].rearrange("(a q f) -> q a f", a=2, f=P), srcf[:, :, :]).then_inc(rows_out, 16)
                sp.wait_ge(rel_copied, 8)
                sp.dma_start(k.rel_rows[:, :], rel).then_inc(rel_out, 16)
                sp.wait_ge(rel_out, 16)
                sp.wait_ge(rows_out, 48)
                sp.dma_start(k.same[:, :], k.same_row[:].partition_broadcast(P)).then_inc(same_in, 16)
                sp.wait_ge(weights_in, 16 * len(loads))
                sp.wait_ge(same_in, 16)

            @block.gpsimd
            def _(pool):
                pool.memset(k.ident[:, :], 0.0).then_inc(consts, 1)
                pool.memset(tri[:, :], 1.0).then_inc(consts, 1)
                pool.iota(rel_iota[:, :], pattern=[[2, RELS // 2]], base=0, channel_multiplier=0).then_inc(consts, 1)
                pool.wait_ge(consts, 3)
                pool.affine_select(out=k.ident[:, :], in_=k.ident[:, :], compare_op=ALU.not_equal, fill=1.0,
                                   base=0, pattern=[[-1, P]], channel_multiplier=1).then_inc(consts, 1)
                pool.affine_select(out=tri[:, :], in_=tri[:, :], compare_op=ALU.is_gt, fill=0.0,
                                   base=0, pattern=[[-1, P]], channel_multiplier=1).then_inc(consts, 1)
                pool.wait_ge(flag_ready, 1)
                unsorted = pool.value_load(flag[0:1, 0:1], min_val=0, max_val=SLOTS)
                with pool.If(unsorted > 0):
                    with pool.Fori(0, ET) as t:
                        pool.wait_ge(rank_v, (t + 1) * STEPS)
                        pool.wait_ge(tile_in, (t + 1) * 64)
                        pool.sem_inc(rank_wait, 1)
                        for table, column in ((k.dst_r, tile_dst_i), (k.src_r, tile_src_i),
                                              (k.typ_r, tile_typ_i), (k.attr_r, tile_attr)):
                            pool.indirect_dma_start(table[:, :], bass.IndirectOffsetOnAxis(ap=rank_i[:, 0:1], axis=0),
                                                    column[:, :], None).then_inc(ranked_out, 16)
                    pool.wait_ge(ranked_out, ET * 64)

            @block.tensor
            def _(pe):
                pe.wait_ge(coeff_in, 32)
                for c in range(8):
                    if c >= 4:
                        pe.wait_ge(rel_copied, c - 3)
                    pe.matmul(k.bank[c % 4][0:RELS, :], coeff[:, :], basis_t[:, c * 512:(c + 1) * 512],
                              start=True, stop=True).then_inc(rel_mm, 1)
                pe.wait_ge(order_v, 5)
                pe.matmul(k.bank[4][0:1, 0:1], falls_sum[:, :], ones_col[0:ROWS, :],
                          start=True, stop=True).then_inc(falls_added, 1)
                pe.wait_ge(consts, 5)
                pe.wait_ge(arrays_v, 10)
                for n, a in enumerate((src_in, gath, scat)):
                    for c in range(2):
                        pe.transpose(k.bank[5 + n][:, c * ROWS:(c + 1) * ROWS], a[:, c, :],
                                     k.ident[0:ROWS, 0:ROWS]).then_inc(turned, 1)
                for c in range(2):
                    pe.transpose(k.bank[5][:, (2 + c) * ROWS:(3 + c) * ROWS], srcf[:, c, :],
                                 k.ident[0:ROWS, 0:ROWS]).then_inc(turned, 1)

            @block.scalar
            def _(act):
                for c in range(8):
                    act.wait_ge(rel_mm, c + 1)
                    act.activation(rel[:, c * 512:(c + 1) * 512], k.bank[c % 4][0:RELS, :], ACT.Copy).then_inc(rel_copied, 1)

            @block.vector
            def _(vec):
                vec.memset(zero_attr[:, :], 0.0).then_inc(pads, 1)
                vec.memset(zero_pad[:, :], 0).then_inc(pads, 1)
                vec.memset(src_pad[:, :], NODES).then_inc(pads, 1)
                vec.memset(dst_pad[:, 0:PAD + 2], NODES).then_inc(pads, 1)
                vec.memset(k.wself[:, :], 0.0).then_inc(pads, 1)
                vec.wait_ge(pads, 5)
                vec.memset(dst_pad[:, 0:PAD + 2:PAD + 1], -1).then_inc(pads, 1)
                vec.memset(ones_col[:, :], 1.0).then_inc(order_v, 1)
                vec.memset(k.ones[:, :], 1.0)
                vec.memset(k.bu2_parts[:, :], 0.0).then_inc(bias_v, 1)
                vec.memset(k.brel_parts[:, :], 0.0).then_inc(bias_v, 1)
                vec.memset(k.eps_col[:, :], D * D * LN_EPS)
                vec.wait_ge(consts, 3)
                vec.tensor_copy(k.relcol[:, :], rel_iota[:, :]).then_inc(idx_ready, 1)
                vec.wait_ge(idx_ready, 1)
                vec.tensor_scalar(k.relcol[D:P, :], k.relcol[D:P, :], 1.0, None, ALU.add).then_inc(idx_ready, 1)
                vec.wait_ge(bias_in, 32)
                for n in range(3):
                    vec.wait_ge(bias_v, 2 + 4 * n)
                    vec.tensor_copy(bias_part[:, :, :], bias_left[:, :, :]).then_inc(bias_v, 1)
                    vec.wait_ge(bias_v, 3 + 4 * n)
                    row = slice(32 * n, 32 * n + 1)
                    vec.tensor_copy(k.bu2_parts[row, :], bias_part[row, 0, :]).then_inc(bias_v, 1)
                    vec.tensor_copy(k.brel_parts[row, :], bias_part[row, 1, :]).then_inc(bias_v, 1)
                    vec.tensor_tensor(bias_left[:, :, :], bias_left[:, :, :], bias_part[:, :, :], ALU.subtract).then_inc(bias_v, 1)
                vec.wait_ge(order_in, 32)
                vec.tensor_copy(cur[:, :, :], cur_i[:, :, :]).then_inc(order_v, 1)
                vec.tensor_copy(prev[:, :, :], prev_i[:, :, :]).then_inc(order_v, 1)
                vec.wait_ge(order_v, 3)
                vec.tensor_tensor(falls[:, :].rearrange("q (a f) -> q a f", a=2), prev[:, :, :], cur[:, :, :],
                                  ALU.is_gt).then_inc(order_v, 1)
                vec.wait_ge(order_v, 4)
                vec.tensor_reduce(falls_sum[:, :], falls[:, :], AX.X, ALU.add).then_inc(order_v, 1)
                vec.wait_ge(falls_added, 1)
                vec.tensor_copy(flag[:, :], k.bank[4][0:1, 0:1]).then_inc(flag_ready, 1)
                vec.wait_ge(flag_ready, 1)
                unsorted = vec.value_load(flag[0:1, 0:1], min_val=0, max_val=SLOTS)
                with vec.If(unsorted > 0):
                    vec.wait_ge(wide_in, 16)
                    vec.wait_ge(consts, 5)
                    vec.tensor_scalar(wide, wide.bitcast(I32), 0.5, None, ALU.add).then_inc(wide_v, 1)
                    vec.wait_ge(wide_v, 1)
                    with vec.Fori(0, ET) as t:
                        vec.wait_ge(tile_in, (t + 1) * 64)
                        base = t * STEPS
                        vec.tensor_copy(tile_dst[:, :], tile_dst_i[:, :]).then_inc(rank_v, 1)
                        vec.wait_ge(rank_v, base + 1)
                        vec.tensor_scalar(tile_half[:, :], tile_dst[:, :], 0.5, None, ALU.add).then_inc(rank_v, 1)
                        for c in range(SLOTS // COUNT_CHUNK):
                            if c:
                                vec.wait_ge(rank_v, base + 2 + 2 * c)
                            vec.tensor_scalar(junk, wide[:, c * COUNT_CHUNK:(c + 1) * COUNT_CHUNK],
                                              tile_dst[:, 0:1], None, ALU.is_le).then_inc(rank_v, 1)
                            vec.wait_ge(rank_v, base + 3 + 2 * c)
                            vec.tensor_reduce(counts[:, c:c + 1], junk, AX.X, ALU.add).then_inc(rank_v, 1)
                        n = 2 + 2 * (SLOTS // COUNT_CHUNK)
                        vec.wait_ge(rank_v, base + n)
                        vec.scalar_tensor_tensor(out=own[:, :], in0=wide[:, bass.ds(t * P, P)], scalar=tile_half[:, 0:1],
                                                 in1=tri[:, :], op0=ALU.is_equal, op1=ALU.mult).then_inc(rank_v, 1)
                        vec.wait_ge(rank_v, base + n + 1)
                        vec.tensor_reduce(counts[:, SLOTS // COUNT_CHUNK:], own[:, :], AX.X, ALU.add).then_inc(rank_v, 1)
                        vec.tensor_scalar(wide[:, bass.ds(t * P, P)], wide[:, bass.ds(t * P, P)], -0.5, None,
                                          ALU.add).then_inc(rank_v, 1)
                        vec.wait_ge(rank_v, base + n + 3)
                        vec.tensor_reduce(rank[:, :], counts[:, :], AX.X, ALU.add).then_inc(rank_v, 1)
                        vec.wait_ge(rank_v, base + n + 4)
                        vec.tensor_copy(rank_i[:, :], rank[:, :]).then_inc(rank_v, 1)
                vec.wait_ge(arrays_in, 5 * 16)
                vec.tensor_copy(cur[:, :, :], cur_i[:, :, :]).then_inc(arrays_v, 1)
                vec.tensor_copy(prev[:, :, :], prev_i[:, :, :]).then_inc(arrays_v, 1)
                vec.tensor_copy(nxt[:, :, :], next_i[:, :, :]).then_inc(arrays_v, 1)
                vec.tensor_copy(srcf[:, :, :], src_i[:, :, :]).then_inc(arrays_v, 1)
                vec.tensor_copy(typf[:, :, :], typ_i[:, :, :]).then_inc(arrays_v, 1)
                vec.wait_ge(arrays_v, 5)
                vec.tensor_tensor(same_t[:, :, :], cur[:, :, :], prev[:, :, :], ALU.is_equal).then_inc(arrays_v, 1)
                vec.tensor_tensor(nxt[:, :, :], cur[:, :, :], nxt[:, :, :], ALU.is_equal).then_inc(arrays_v, 1)
                vec.tensor_scalar(gath[:, :, :], cur[:, :, :], float(NODES - 1), None, ALU.min).then_inc(arrays_v, 1)
                vec.tensor_scalar(src_in[:, :, :], srcf[:, :, :], float(NODES - 1), None, ALU.min).then_inc(arrays_v, 1)
                vec.wait_ge(arrays_v, 9)
                vec.scalar_tensor_tensor(out=scat[:, :, :], in0=nxt[:, :, :], scalar=float(FAR), in1=cur[:, :, :],
                                         op0=ALU.mult, op1=ALU.add).then_inc(arrays_v, 1)
                vec.wait_ge(turned, 8)
                for n, a in enumerate((k.src_idx, k.dst_idx, k.last_idx)):
                    vec.tensor_copy(a[:, :], k.bank[5 + n][:, 0:ET]).then_inc(idx_ready, 1)
                vec.tensor_copy(k.src_key[:, :], k.bank[5][:, ET:2 * ET]).then_inc(idx_ready, 1)
                vec.wait_ge(idx_ready, 6)
                vec.wait_ge(bias_v, 14)


def stage_index(pool, copied, g, ring, idx):
    pool.tensor_copy(ring[:, g.buf, :], idx[:, bass.ds(g.n * TG, TG)]).then_inc(copied, 1)


def gather_rows(pool, to, table, index):
    return pool.indirect_dma_start(to, None, table[:, :], bass.IndirectOffsetOnAxis(ap=index, axis=0))


def scatter_rows(pool, table, frm, index, **how):
    return pool.indirect_dma_start(table[:, :], bass.IndirectOffsetOnAxis(ap=index, axis=0), frm, None,
                                   bounds_check=NODES - 1, oob_is_err=False, **how)


def gather_group(pool, g, reads, copied, gathered, settled):
    if g.from_second():
        pool.wait_ge(gathered[g.buf], g.half * (len(reads) * TG * 16))
    pool.sem_inc(settled, 1)
    for to, table, idx, ring in reads:
        stage_index(pool, copied, g, ring, idx)
    pool.wait_ge(copied, (g.n + 1) * len(reads))
    pool.sem_inc(settled, 1)
    for t in range(TG):
        for to, table, idx, ring in reads:
            gather_rows(pool, to[:, t], table, ring[:, g.buf, t:t + 1]).then_inc(gathered[g.buf], 16)


def scatter_group(pool, g, rows, ready, count, table, idx, ring, copied, scattered, settled, **how):
    if g.from_second():
        pool.wait_ge(scattered[g.buf], g.half * (TG * 16))
    pool.sem_inc(settled, 1)
    stage_index(pool, copied, g, ring, idx)
    pool.wait_ge(copied, g.n + 1)
    pool.wait_ge(ready, count)
    pool.sem_inc(settled, 1)
    for t in range(TG):
        scatter_rows(pool, table, rows[:, g.buf, t, :], ring[:, g.buf, t:t + 1], **how).then_inc(scattered[g.buf], 16)


def dense(nc, k):
    with ExitStack() as ctx:
        def two(name, shape, dt=F32):
            return k.sb(name, [shape[0], 2] + shape[1:], dt, ctx)

        def sem(name):
            return k.sem(name, ctx)

        rows = two("rows", [NP, NG, D])
        cen0 = two("cen0", [NP, NG, D])
        res0 = two("res0", [NP, NG, D])
        cen1 = two("cen1", [NP, NG, D])
        res1 = two("res1", [NP, NG, D])
        res2 = two("res2", [NP, NG, D])
        squares = k.sb("squares", [NP, 2, NG, D], F32, ctx)
        sums = k.sb("sums", [NP, 2, NG], F32, ctx)
        roots = k.sb("roots", [NP, 2, NG], F32, ctx)
        inverse = k.sb("inverse", [NP, 2, NG], F32, ctx)
        h0t = k.sb("h0t", [P, HALF], F32, ctx)
        h1t = k.sb("h1t", [P, HALF], F32, ctx)
        ut = k.sb("ut", [H, 2, HALF], F32, ctx)
        src_ring = k.sb("src_ring", [P, 2, TG], I32, ctx)
        dst_ring = k.sb("dst_ring", [P, 2, TG], I32, ctx)
        xs_ring = k.sb("xs_ring", [P, 2, TG, D], F32, ctx)
        xd_ring = k.sb("xd_ring", [P, 2, TG, D], F32, ctx)

        x_in = k.pair_of_sems("x_in", ctx)
        ln0, ln1, added2 = sem("ln0"), sem("ln1"), sem("added2")
        sq0_done, sq1_done = sem("sq0_done"), sem("sq1_done")
        rooted, inverted = sem("rooted"), sem("inverted")
        t0_done, t1_done = sem("t0_done"), sem("t1_done")
        h0t_done, h1t_done = sem("h0t_done"), sem("h1t_done")
        u1_done, ut_done, u2_done = sem("u1_done"), sem("ut_done"), sem("u2_done")
        self_done = sem("self_done")
        pe_wait = sem("pe_wait")
        x1_out = k.pair_of_sems("x1_out", ctx)
        x2_out = k.pair_of_sems("x2_out", ctx)
        gathered = k.pair_of_sems("gathered", ctx)
        kept = k.pair_of_sems("kept", ctx)
        idx_copied = sem("idx_copied")
        pool_wait = sem("pool_wait")

        def nodes(a, g):
            return a.rearrange("(p j) d -> p j d", p=NP)[:, bass.ds(g.n * NG, NG), :]

        with nc.Block() as block:
            @block.sync
            def _(sp):

                def step(r):
                    g = r
                    if g.within(DG):
                        if g.from_second():
                            sp.wait_ge(ln0, (g - 2).n * 5 + 5)
                        sp.dma_start(rows[:, g.buf], nodes(k.x, g)).then_inc(x_in[g.buf], 16)
                    g = r - 2
                    if g.within(EG):
                        sp.wait_ge(gathered[g.buf], (g.half + 1) * (2 * TG * 16))
                        sp.dma_start(k.x_src[:, bass.ds(g.n * TG, TG), :], xs_ring[:, g.buf]).then_inc(kept[g.buf], 16)
                        sp.dma_start(k.x_dst[:, bass.ds(g.n * TG, TG), :], xd_ring[:, g.buf]).then_inc(kept[g.buf], 16)
                    g = r - 3
                    if g.within(DG):
                        sp.wait_ge(ln1, g.n * 5 + 1)
                        sp.dma_start(nodes(k.x1_table, g), res1[:, g.buf]).then_inc(x1_out[g.buf], 16)
                    g = r - 5
                    if g.within(DG):
                        sp.wait_ge(added2, g.n + 1)
                        sp.dma_start(nodes(k.x2_table, g), res2[:, g.buf]).then_inc(x2_out[g.buf], 16)

                rounds(sp, DG, 5, step)
                for b in range(2):
                    sp.wait_ge(x1_out[b], (DG + 1 - b) // 2 * 16)
                    sp.wait_ge(x2_out[b], (DG + 1 - b) // 2 * 16)
                    sp.wait_ge(kept[b], (EG + 1 - b) // 2 * 32)

            @block.gpsimd
            def _(pool):
                stage_index(pool, idx_copied, Group(0, 0), src_ring, k.src_idx)
                stage_index(pool, idx_copied, Group(0, 0), dst_ring, k.dst_idx)

                def gather(r, j):
                    for ring, index in ((xs_ring, src_ring), (xd_ring, dst_ring)):
                        gather_rows(pool, ring[:, r.buf, j, :], k.x, index[:, r.buf, j:j + 1]).then_inc(gathered[r.buf], 16)

                def step(r):
                    if r.from_second():
                        pool.wait_ge(kept[r.buf], r.half * 32)
                    pool.wait_ge(idx_copied, r.n * 2 + 2)
                    pool.sem_inc(pool_wait, 1)
                    gather(r, 0)
                    gather(r, 1)
                    if (r + 1).within(EG):
                        if r.from_first():
                            pool.wait_ge(gathered[(r + 1).buf], (r + 1).half * (2 * TG * 16))
                            pool.sem_inc(pool_wait, 1)
                        stage_index(pool, idx_copied, r + 1, src_ring, k.src_idx)
                        stage_index(pool, idx_copied, r + 1, dst_ring, k.dst_idx)
                    gather(r, 2)
                    gather(r, 3)

                rounds(pool, EG, 0, step)

            @block.vector
            def _(vec):
                def step(r):
                    g = r
                    if g.within(DG):
                        vec.wait_ge(x_in[g.buf], (g.half + 1) * 16)
                        if g.from_second():
                            vec.wait_ge(t0_done, (g - 2).n + 1)
                        center_rows(vec, ln0, g.n * 5, rows[:, g.buf], sums[:, 0, :], cen0[:, g.buf])
                    g = r - 4
                    if g.within(DG):
                        vec.wait_ge(self_done, g.n + 1)
                        if g.from_second():
                            vec.wait_ge(x2_out[g.buf], g.half * 16)
                        vec.tensor_tensor(res2[:, g.buf], res1[:, g.buf],
                                          k.bank[7][0:NP, :].rearrange("p (j d) -> p j d", d=D), ALU.add).then_inc(added2, 1)
                    g = r - 2
                    if g.within(DG):
                        vec.wait_ge(u2_done, g.n + 1)
                        if g.from_second():
                            vec.wait_ge(x1_out[g.buf], g.half * 16)
                            vec.wait_ge(added2, (g - 2).n + 1)
                        vec.tensor_tensor(res1[:, g.buf], res0[:, g.buf],
                                          k.bank[6][0:NP, :].rearrange("p (j d) -> p j d", d=D), ALU.add).then_inc(ln1, 1)
                        vec.wait_ge(ln1, g.n * 5 + 1)
                        if g.from_second():
                            vec.wait_ge(t1_done, (g - 2).n + 1)
                        center_rows(vec, ln1, g.n * 5 + 1, res1[:, g.buf], sums[:, 1, :], cen1[:, g.buf])
                    live = [m for m in range(2) if (r - 2 * m).within(DG)]
                    if not live:
                        return
                    for m, ln, done in ((0, ln0, sq0_done), (1, ln1, sq1_done)):
                        if m in live:
                            vec.wait_ge(done, (r - 2 * m).n + 1)
                            vec.tensor_reduce(roots[:, m, :], squares[:, m], AX.X, ALU.add).then_inc(ln, 1)
                    vec.wait_ge(rooted, r.n + 1)
                    vec.reciprocal(inverse[:, live[0]:live[-1] + 1, :], roots[:, live[0]:live[-1] + 1, :]).then_inc(inverted, 1)
                    vec.wait_ge(inverted, r.n + 1)
                    g = r - 2
                    if g.within(DG):
                        scale_rows(vec, ln1, cen1[:, g.buf], inverse[:, 1, :], cen1[:, g.buf])
                    g = r
                    if g.within(DG):
                        scale_rows(vec, ln0, cen0[:, g.buf], inverse[:, 0, :], cen0[:, g.buf])
                        vec.wait_ge(ln0, g.n * 5 + 4)
                        vec.tensor_tensor(res0[:, g.buf], rows[:, g.buf], cen0[:, g.buf], ALU.add).then_inc(ln0, 1)

                rounds(vec, DG, 4, step)

            @block.scalar
            def _(act):
                def step(r):
                    g = r - 1
                    if g.within(DG):
                        act.wait_ge(t0_done, g.n + 1)
                        if g.from_first():
                            act.wait_ge(u1_done, g.n * 2)
                        act.activation(h0t[:, :], k.bank[0][:, 0:HALF], ACT.Copy).then_inc(h0t_done, 1)
                    g = r - 3
                    if g.within(DG):
                        act.wait_ge(t1_done, g.n + 1)
                        if g.from_first():
                            act.wait_ge(self_done, g.n)
                        act.activation(h1t[:, :], k.bank[2][:, 0:HALF], ACT.Copy).then_inc(h1t_done, 1)
                    g = r
                    if g.within(DG):
                        act.wait_ge(ln0, g.n * 5 + 2)
                        act.activation(squares[:, 0], cen0[:, g.buf], ACT.Square, scale=0.125).then_inc(sq0_done, 1)
                    g = r - 2
                    if g.within(DG):
                        act.wait_ge(ln1, g.n * 5 + 3)
                        act.activation(squares[:, 1], cen1[:, g.buf], ACT.Square, scale=0.125).then_inc(sq1_done, 1)
                    g = r - 1
                    if g.within(DG):
                        for c in range(2):
                            act.wait_ge(u1_done, g.n * 2 + c + 1)
                            if g.from_first():
                                act.wait_ge(u2_done, g.n)
                            act.activation(ut[:, c, :], k.bank[4 + c][:, 0:HALF], ACT.Relu, bias=k.bu1[:, 0:1]).then_inc(ut_done, 1)
                    live = [m for m in range(2) if (r - 2 * m).within(DG)]
                    if not live:
                        return
                    if 0 in live:
                        act.wait_ge(ln0, r.n * 5 + 3)
                    if 1 in live:
                        act.wait_ge(ln1, (r - 2).n * 5 + 4)
                    act.activation(roots[:, live[0]:live[-1] + 1, :], roots[:, live[0]:live[-1] + 1, :], ACT.Sqrt,
                                   bias=k.eps_col[0:NP, 0:1]).then_inc(rooted, 1)

                rounds(act, DG, 4, step)

            @block.tensor
            def _(pe):
                def turn(g, rows_in, to, done):
                    for j in range(NG // 2):
                        mm = pe.transpose(k.bank[to][:, j * NP:(j + 1) * NP],
                                          rows_in[:, g.buf, 2 * j:2 * j + 2, :].rearrange("p j d -> p (j d)"),
                                          k.ident[0:NP, 0:NP])
                    mm.then_inc(done, 1)

                def bias_first(to, bias):
                    pe.matmul(k.bank[to][0:NP, :], k.ones[:, 0:NP], bias.unsqueeze(1).to_broadcast([BIAS_ROWS, NG, D]),
                              start=True, stop=True, skip_group_check=True)

                def step(r):
                    g = r - 1
                    if g.within(DG):
                        pe.wait_ge(ln0, g.n * 5 + 4)
                        if g.from_first():
                            pe.wait_ge(h0t_done, g.n)
                        pe.sem_inc(pe_wait, 1)
                        turn(g, cen0, 0, t0_done)
                    g = r - 3
                    if g.within(DG):
                        pe.wait_ge(ln1, g.n * 5 + 5)
                        if g.from_first():
                            pe.wait_ge(h1t_done, g.n)
                        pe.sem_inc(pe_wait, 1)
                        turn(g, cen1, 2, t1_done)
                    g = r - 1
                    if g.within(DG):
                        pe.wait_ge(h0t_done, g.n + 1)
                        for c in range(2):
                            if g.from_first():
                                pe.wait_ge(ut_done, g.n * 2 + c - 1)
                            pe.matmul(k.bank[4 + c][:, 0:HALF], k.wu1x[c * D:(c + 1) * D, :], h0t[c * D:(c + 1) * D, :],
                                      start=True, stop=True).then_inc(u1_done, 1)
                    g = r - 3
                    if g.within(DG):
                        pe.wait_ge(h1t_done, g.n + 1)
                        if g.from_first():
                            pe.wait_ge(added2, g.n)
                        bias_first(7, k.brel_parts[:, :])
                        for j in range(NG // 2):
                            mm = pe.matmul(k.bank[7][0:NP, j * P:(j + 1) * P], h1t[:, j * NP:(j + 1) * NP], k.wself[:, :],
                                           start=False, stop=True, skip_group_check=True)
                        mm.then_inc(self_done, 1)
                    g = r - 1
                    if g.within(DG):
                        pe.wait_ge(ut_done, g.n * 2 + 2)
                        if g.from_first():
                            pe.wait_ge(ln1, g.n * 5 - 4)
                        bias_first(6, k.bu2_parts[:, :])
                        for j in range(NG):
                            at = j // 2 * NP
                            mm = pe.matmul(k.bank[6][0:NP, j * D:(j + 1) * D], ut[:, j % 2, at:at + NP], k.wu2[:, :],
                                           start=False, stop=True, skip_group_check=True)
                        mm.then_inc(u2_done, 1)

                rounds(pe, DG, 4, step)


def layer0(nc, k):
    with ExitStack() as ctx:
        def sb(name, shape, dt=F32):
            return k.sb(name, shape, dt, ctx)

        def sem(name):
            return k.sem(name, ctx)

        attr = sb("l0_attr", [P, 2, TG, ED])
        cen = sb("l0_cen", [P, 2, TG, 2, D])
        squares = sb("l0_squares", [P, 3 * TG * D])
        sq_in = squares[:, 0:2 * TG * D]
        sq_up = squares[:, 2 * TG * D:]
        stats = sb("l0_stats", [P, 3 * TG])
        roots = sb("l0_roots", [P, 3 * TG])
        inverse = sb("l0_inverse", [P, 3 * TG])
        ht = sb("l0_ht", [P, 2, GS])
        at = sb("l0_at", [ED, 2, GS])
        hid = sb("l0_hid", [H, GS])
        msg = sb("l0_msg", [H, 2, GS])
        agg = sb("l0_agg", [H, 2, GS])
        ut = sb("l0_ut", [H, GS])
        x1 = sb("l0_x1", [P, 2, TG, D])
        h1 = sb("l0_h1", [P, 2, TG, D])
        h1t = sb("l0_h1t", [P, GS // 2])
        last_ring = sb("l0_last_ring", [P, 2, TG], I32)
        zeros = sb("l0_zeros", [P, CLEAR, D + 1])

        attr_in = k.pair_of_sems("l0_attr_in", ctx)
        ln0, ln1 = sem("l0_ln0"), sem("l0_ln1")
        sq_in_done, sq_up_done = sem("l0_sq_in_done"), sem("l0_sq_up_done")
        rooted, inverted = sem("l0_rooted"), sem("l0_inverted")
        turned, ht_done, at_done = sem("l0_turned"), sem("l0_ht_done"), sem("l0_at_done")
        m1_done, hid_done, m2_done, msg_done = sem("l0_m1"), sem("l0_hid_done"), sem("l0_m2"), sem("l0_msg_done")
        scanned = sem("l0_scanned")
        u1_done, ut_done, u2_done = sem("l0_u1"), sem("l0_ut_done"), sem("l0_u2")
        h1_turned, h1t_done, self_done = sem("l0_h1_turned"), sem("l0_h1t_done"), sem("l0_self")
        self_added = sem("l0_self_added")
        pe_wait, pool_wait, idx_copied = sem("l0_pe_wait"), sem("l0_pool_wait"), sem("l0_idx_copied")
        scattered = k.pair_of_sems("l0_scattered", ctx)
        zeroed, cleared = sem("l0_zeroed"), sem("l0_cleared")

        def x_dst(g):
            return k.x_dst[:, bass.ds(g.n * TG, TG), :]

        def x_src(g):
            return k.x_src[:, bass.ds(g.n * TG, TG), :]

        def spans(r):
            return (0 if r.within(EG) else 2 * TG), (3 * TG if (r - 3).within(EG) else 2 * TG)

        with nc.Block() as block:
            @block.sync
            def _(sp):
                def step(r):
                    if r.from_second():
                        sp.wait_ge(turned, (r - 2).n + 1)
                    sp.dma_start(attr[:, r.buf], k.attr_s[bass.ds(r.n * GS, GS), :].rearrange("(t p) c -> p t c", p=P)
                                 ).then_inc(attr_in[r.buf], 16)
                    sp.dma_start(k.sum_table[bass.ds(r.n * (P * CLEAR), P * CLEAR), :].rearrange("(p c) d -> p c d", p=P),
                                 zeros[:, :, :]).then_inc(cleared, 16)

                sp.wait_ge(zeroed, 1)
                rounds(sp, EG, 0, step)
                sp.wait_ge(cleared, EG * 16)

            @block.gpsimd
            def _(pool):
                def step(g):
                    scatter_group(pool, g, x1, ln1, g.n * 5 + 1, k.x1_table, k.last_idx, last_ring,
                                  idx_copied, scattered, pool_wait)

                rounds(pool, EG, 0, step)
                for b in range(2):
                    pool.wait_ge(scattered[b], (EG + 1 - b) // 2 * TG * 16)

            @block.vector
            def _(vec):
                vec.memset(zeros[:, :, :], 0.0).then_inc(zeroed, 1)

                def step(r):
                    g = r - 2
                    if g.within(EG):
                        vec.wait_ge(msg_done, g.n + 1)
                        if g.from_second():
                            vec.wait_ge(u1_done, (g - 2).n + 1)
                        if g.from_first():
                            vec.wait_ge(scanned, g.n)
                        vec.tensor_tensor_scan(agg[:, g.buf, :], k.same[:, bass.ds(g.n * GS, GS)], msg[:, g.buf, :],
                                               agg[:, (g - 1).buf, GS - 1:GS] if g.from_first() else 0.0,
                                               ALU.mult, ALU.add).then_inc(scanned, 1)
                    g = r
                    if g.within(EG):
                        flat = cen[:, g.buf]
                        for side, x in ((0, x_src(g)), (1, x_dst(g))):
                            vec.tensor_reduce(stats[:, side * TG:side * TG + TG], x, AX.X, ALU.add).then_inc(ln0, 1)
                        if g.from_second():
                            vec.wait_ge(turned, (g - 2).n + 1)
                        for side, x in ((0, x_src(g)), (1, x_dst(g))):
                            vec.wait_ge(ln0, g.n * 7 + 1 + side)
                            vec.scalar_tensor_tensor(
                                out=flat[:, :, side, :], in0=x, scalar=float(D),
                                in1=stats[:, side * TG:side * TG + TG].unsqueeze(2).to_broadcast([P, TG, D]),
                                op0=ALU.mult, op1=ALU.subtract).then_inc(ln0, 1)
                    g = r - 5
                    if g.within(EG):
                        vec.wait_ge(self_done, g.n + 1)
                        vec.tensor_tensor(x_dst(g), x1[:, g.buf], k.bank[7][:, 0:TG * D].rearrange("p (t d) -> p t d", d=D),
                                          ALU.add).then_inc(self_added, 1)
                    g = r - 3
                    if g.within(EG):
                        vec.wait_ge(u2_done, g.n + 1)
                        if g.from_second():
                            vec.wait_ge(scattered[g.buf], g.half * (TG * 16))
                            vec.wait_ge(self_added, (g - 2).n + 1)
                        vec.tensor_tensor(x1[:, g.buf], x_dst(g), k.bank[5][:, 0:TG * D].rearrange("p (t d) -> p t d", d=D),
                                          ALU.add).then_inc(ln1, 1)
                        vec.wait_ge(ln1, g.n * 5 + 1)
                        if g.from_second():
                            vec.wait_ge(h1_turned, (g - 2).n + 1)
                        center_rows(vec, ln1, g.n * 5 + 1, x1[:, g.buf], stats[:, 2 * TG:], h1[:, g.buf])
                    lo, hi = spans(r)
                    if lo >= hi:
                        return
                    if r.within(EG):
                        vec.wait_ge(sq_in_done, r.n + 1)
                        vec.tensor_reduce(roots[:, 0:2 * TG], sq_in.rearrange("p (t d) -> p t d", d=D), AX.X, ALU.add).then_inc(ln0, 1)
                    if (r - 3).within(EG):
                        vec.wait_ge(sq_up_done, (r - 3).n + 1)
                        vec.tensor_reduce(roots[:, 2 * TG:], sq_up.rearrange("p (t d) -> p t d", d=D), AX.X, ALU.add).then_inc(ln1, 1)
                    vec.wait_ge(rooted, r.n + 1)
                    vec.reciprocal(inverse[:, lo:hi], roots[:, lo:hi]).then_inc(inverted, 1)
                    vec.wait_ge(inverted, r.n + 1)
                    g = r - 3
                    if g.within(EG):
                        scale_rows(vec, ln1, h1[:, g.buf], inverse[:, 2 * TG:], h1[:, g.buf])
                    g = r
                    if g.within(EG):
                        flat = cen[:, g.buf].rearrange("p t s d -> p (t s) d")
                        scale_rows(vec, ln0, flat, inverse[:, 0:2 * TG], flat)
                        vec.wait_ge(ln0, g.n * 7 + 6)
                        vec.tensor_tensor(x_dst(g), x_dst(g), cen[:, g.buf, :, 1, :], ALU.add).then_inc(ln0, 1)

                rounds(vec, EG, 5, step)

            @block.scalar
            def _(act):
                def step(r):
                    g = r - 1
                    if g.within(EG):
                        act.wait_ge(turned, g.n + 1)
                        if g.from_second():
                            act.wait_ge(u1_done, (g - 2).n + 1)
                        act.activation(ht[:, g.buf, :], k.bank[0][:, :], ACT.Copy).then_inc(ht_done, 1)
                        act.activation(at[:, g.buf, :], k.bank[1][0:ED, :], ACT.Copy).then_inc(at_done, 1)
                    g = r - 4
                    if g.within(EG):
                        act.wait_ge(h1_turned, g.n + 1)
                        if g.from_first():
                            act.wait_ge(self_done, g.n)
                        act.activation(h1t[:, :], k.bank[6][:, 0:GS // 2], ACT.Copy).then_inc(h1t_done, 1)
                    g = r
                    if g.within(EG):
                        act.wait_ge(ln0, g.n * 7 + 4)
                        act.activation(sq_in.rearrange("p (t d) -> p t d", d=D), cen[:, g.buf].rearrange("p t s d -> p (t s) d"),
                                       ACT.Square, scale=0.125).then_inc(sq_in_done, 1)
                    g = r - 2
                    if g.within(EG):
                        act.wait_ge(u1_done, g.n + 1)
                        if g.from_first():
                            act.wait_ge(u2_done, g.n)
                        act.activation(ut[:, :], k.bank[4][:, :], ACT.Relu, bias=k.bu1[:, 0:1]).then_inc(ut_done, 1)
                    g = r - 3
                    if g.within(EG):
                        act.wait_ge(ln1, g.n * 5 + 3)
                        act.activation(sq_up.rearrange("p (t d) -> p t d", d=D), h1[:, g.buf], ACT.Square, scale=0.125
                                       ).then_inc(sq_up_done, 1)
                    g = r - 1
                    if g.within(EG):
                        act.wait_ge(m1_done, g.n + 1)
                        if g.from_first():
                            act.wait_ge(m2_done, g.n)
                        act.activation(hid[:, :], k.bank[2][:, :], ACT.Relu, bias=k.bm1[:, 0:1]).then_inc(hid_done, 1)
                    lo, hi = spans(r)
                    if lo < hi:
                        if r.within(EG):
                            act.wait_ge(ln0, r.n * 7 + 5)
                        if (r - 3).within(EG):
                            act.wait_ge(ln1, (r - 3).n * 5 + 4)
                        act.activation(roots[:, lo:hi], roots[:, lo:hi], ACT.Sqrt, bias=k.eps_col[:, 0:1]).then_inc(rooted, 1)
                    g = r - 1
                    if g.within(EG):
                        act.wait_ge(m2_done, g.n + 1)
                        if g.from_second():
                            act.wait_ge(scanned, (g - 2).n + 1)
                        act.activation(msg[:, g.buf, :], k.bank[3][:, :], ACT.Identity, bias=k.bm2[:, 0:1]).then_inc(msg_done, 1)

                rounds(act, EG, 4, step)

            @block.tensor
            def _(pe):
                def rows_times(to, cols, weights, bias, done):
                    pe.matmul(k.bank[to][:, 0:TG * D], k.ones[:, :], bias[:, :].unsqueeze(1).to_broadcast([BIAS_ROWS, TG, D]),
                              start=True, stop=True, skip_group_check=True)
                    width = weights.shape[-1]
                    for t in range(TG * D // width):
                        mm = pe.matmul(k.bank[to][:, t * width:(t + 1) * width], cols[:, t * P:(t + 1) * P], weights,
                                       start=False, stop=True, skip_group_check=True)
                    mm.then_inc(done, 1)

                def step(r):
                    g = r - 1
                    if g.within(EG):
                        pe.wait_ge(ln0, g.n * 7 + 6)
                        pe.wait_ge(attr_in[g.buf], (g.half + 1) * 16)
                        if g.from_first():
                            pe.wait_ge(at_done, g.n)
                        pe.sem_inc(pe_wait, 1)
                        for t in range(TG):
                            pe.transpose(k.bank[0][:, t * P:(t + 1) * P], cen[:, g.buf, t].rearrange("p s d -> p (s d)"), k.ident[:, :])
                        for t in range(TG):
                            mm = pe.transpose(k.bank[1][0:ED, t * P:(t + 1) * P], attr[:, g.buf, t, :], k.ident[:, :])
                        mm.then_inc(turned, 1)
                    g = r - 4
                    if g.within(EG):
                        pe.wait_ge(ln1, g.n * 5 + 5)
                        if g.from_first():
                            pe.wait_ge(h1t_done, g.n)
                        pe.sem_inc(pe_wait, 1)
                        for t in range(TG // 2):
                            mm = pe.transpose(k.bank[6][:, t * P:(t + 1) * P],
                                              h1[:, g.buf, 2 * t:2 * t + 2, :].rearrange("p t d -> p (t d)"), k.ident[:, :])
                        mm.then_inc(h1_turned, 1)
                    g = r - 2
                    if g.within(EG):
                        pe.wait_ge(scanned, g.n + 1)
                        if g.from_first():
                            pe.wait_ge(ut_done, g.n)
                        pe.matmul(k.bank[4][:, :], k.wu1a[:, :], agg[:, g.buf, :], start=True, stop=False)
                        pe.matmul(k.bank[4][:, :], k.wu1x[D:P, :], ht[D:P, g.buf, :], start=False, stop=True).then_inc(u1_done, 1)
                    g = r - 1
                    if g.within(EG):
                        pe.wait_ge(at_done, g.n + 1)
                        if g.from_first():
                            pe.wait_ge(hid_done, g.n)
                        pe.matmul(k.bank[2][:, :], k.wm1[:, :], ht[:, g.buf, :], start=True, stop=False)
                        pe.matmul(k.bank[2][:, :], k.wm1e[:, :], at[:, g.buf, :], start=False, stop=True).then_inc(m1_done, 1)
                    g = r - 4
                    if g.within(EG):
                        pe.wait_ge(h1t_done, g.n + 1)
                        if g.from_first():
                            pe.wait_ge(self_added, g.n)
                        pe.sem_inc(pe_wait, 1)
                        rows_times(7, h1t, k.wself[:, :], k.brel_parts, self_done)
                    g = r - 2
                    if g.within(EG):
                        pe.wait_ge(ut_done, g.n + 1)
                        if g.from_first():
                            pe.wait_ge(ln1, g.n * 5 - 4)
                        pe.sem_inc(pe_wait, 1)
                        rows_times(5, ut, k.wu2[:, :], k.bu2_parts, u2_done)
                    g = r - 1
                    if g.within(EG):
                        pe.wait_ge(hid_done, g.n + 1)
                        if g.from_first():
                            pe.wait_ge(msg_done, g.n)
                        pe.matmul(k.bank[3][:, :], k.wm2[:, :], hid[:, :], start=True, stop=True).then_inc(m2_done, 1)

                rounds(pe, EG, 4, step)


def layer1(nc, k):
    with ExitStack() as ctx:
        def sb(name, shape, dt=F32):
            return k.sb(name, shape, dt, ctx)

        def sem(name):
            return k.sem(name, ctx)

        PAIRS = RELS // 2
        NZ = 8
        wrel = sb("l1_wrel", [P, PAIRS, D])
        types = sb("l1_types", [P, 2, GS])
        xs = sb("l1_xs", [P, 2, TG, D])
        cen = sb("l1_cen", [P, TG, D])
        h1 = sb("l1_h1", [P, 2, TG, 2, D])
        squares = sb("l1_squares", [P, TG, D])
        stats = sb("l1_stats", [P, TG])
        roots = sb("l1_roots", [P, TG])
        inverse = sb("l1_inverse", [P, TG])
        ht = sb("l1_ht", [P, 2, GS])
        z = sb("l1_z", [P, NZ, GS])
        msg = sb("l1_msg", [D + 1, 2, GS])
        agg = sb("l1_agg", [D + 1, 2, GS])
        deg = sb("l1_deg", [P, TG])
        part = sb("l1_part", [P, TG, D])
        x2 = sb("l1_x2", [P, 2, TG, D])
        src_ring = sb("l1_src_ring", [P, 2, TG], I32)
        last_ring = sb("l1_last_ring", [P, 2, TG], I32)

        wrel_in, types_in = sem("l1_wrel_in"), k.pair_of_sems("l1_types_in", ctx)
        gathered, scattered = k.pair_of_sems("l1_gathered", ctx), k.pair_of_sems("l1_scattered", ctx)
        ln, sq_done, rooted, inverted = sem("l1_ln"), sem("l1_sq_done"), sem("l1_rooted"), sem("l1_inverted")
        turned, ht_done = sem("l1_turned"), sem("l1_ht_done")
        z_made, z_used, msg_done = sem("l1_z_made"), sem("l1_z_used"), sem("l1_msg_done")
        ones_set, scanned, rows_done, updated = sem("l1_ones"), sem("l1_scanned"), sem("l1_rows"), sem("l1_updated")
        pe_wait, pool_wait = sem("l1_pe_wait"), sem("l1_pool_wait")
        src_copied, last_copied = sem("l1_src_copied"), sem("l1_last_copied")

        with nc.Block() as block:
            @block.sync
            def _(sp):
                sp.dma_start(wrel[:, :, :], k.rel_rows[:, :].rearrange("(k r) (i o) -> (r i) k o", r=2, o=D)).then_inc(wrel_in, 16)

                def step(r):
                    if r.from_second():
                        sp.wait_ge(z_made, (r - 1).n * PAIRS)
                    sp.dma_start(types[:, r.buf, :], k.type_row[bass.ds(r.n * GS, GS)].partition_broadcast(P)
                                 ).then_inc(types_in[r.buf], 16)

                rounds(sp, EG, 0, step)

            @block.gpsimd
            def _(pool):
                def step(r):
                    g = r
                    if g.within(EG):
                        if g.from_second():
                            pool.wait_ge(ln, (g - 2).n * 5 + 2)
                        gather_group(pool, g, ((xs[:, g.buf], k.x1_table, k.src_idx, src_ring),),
                                     src_copied, gathered, pool_wait)
                    g = r - 4
                    if g.within(EG):
                        scatter_group(pool, g, x2, updated, g.n * 5 + 5, k.x2_table, k.last_idx, last_ring,
                                      last_copied, scattered, pool_wait)

                rounds(pool, EG, 4, step)
                for b in range(2):
                    pool.wait_ge(scattered[b], (EG + 1 - b) // 2 * TG * 16)

            @block.vector
            def _(vec):
                vec.memset(msg[D:D + 1, :, :], 1.0).then_inc(ones_set, 1)
                vec.wait_ge(ones_set, 1)

                def mask(g, first, count):
                    if not g.within(EG):
                        return
                    if first == 0:
                        vec.wait_ge(types_in[g.buf], (g.half + 1) * 16)
                        vec.wait_ge(ht_done, g.n + 1)
                    for n in range(first, first + count):
                        if g.from_first() or n >= NZ:
                            vec.wait_ge(z_used, g.n * PAIRS + n - NZ + 1)
                        vec.scalar_tensor_tensor(out=z[:, n % NZ, :], in0=types[:, g.buf, :], scalar=k.relcol[:, n:n + 1],
                                                 in1=ht[:, g.buf, :], op0=ALU.is_equal, op1=ALU.mult).then_inc(z_made, 1)

                def step(r):
                    now, done = r.within(EG), (r - 3).within(EG)
                    g = r
                    n = g.n * 5
                    if now:
                        vec.wait_ge(gathered[g.buf], (g.half + 1) * (TG * 16))
                        vec.tensor_reduce(stats[:, :], xs[:, g.buf], AX.X, ALU.add).then_inc(ln, 1)
                    mask(r - 1, 0, 1)
                    if now:
                        vec.wait_ge(ln, n + 1)
                        vec.scalar_tensor_tensor(out=cen[:, :, :], in0=xs[:, g.buf], scalar=float(D),
                                                 in1=stats[:, :].unsqueeze(2).to_broadcast([P, TG, D]),
                                                 op0=ALU.mult, op1=ALU.subtract).then_inc(ln, 1)
                    mask(r - 1, 1, 3)
                    if now:
                        vec.wait_ge(sq_done, g.n + 1)
                        vec.tensor_reduce(roots[:, :], squares[:, :, :], AX.X, ALU.add).then_inc(ln, 1)
                    g = r - 3
                    m = g.n * 5
                    sums = k.bank[2][:, 0:TG * (D + 1)].rearrange("p (t d) -> p t d", d=D + 1)
                    if done:
                        vec.wait_ge(rows_done, g.n + 1)
                        vec.tensor_scalar(deg[:, :], sums[:, :, D], 1.0, None, ALU.max).then_inc(updated, 1)
                        vec.tensor_copy(k.degree[:, bass.ds(g.n * TG, TG)], sums[:, :, D]).then_inc(updated, 1)
                    mask(r - 1, 4, 1)
                    if done:
                        vec.wait_ge(updated, m + 1)
                        vec.reciprocal(deg[:, :], deg[:, :]).then_inc(updated, 1)
                    mask(r - 1, 5, 1)
                    if done:
                        vec.wait_ge(updated, m + 3)
                        vec.tensor_tensor(part[:, :, :], sums[:, :, 0:D], deg[:, :].unsqueeze(2).to_broadcast([P, TG, D]),
                                          ALU.mult).then_inc(updated, 1)
                    if now:
                        vec.wait_ge(rooted, r.n + 1)
                        vec.reciprocal(inverse[:, :], roots[:, :]).then_inc(inverted, 1)
                    mask(r - 1, 6, 1)
                    if done:
                        vec.wait_ge(updated, m + 4)
                        if g.from_second():
                            vec.wait_ge(scattered[g.buf], g.half * (TG * 16))
                        vec.tensor_tensor(x2[:, g.buf], part[:, :, :], k.x_dst[:, bass.ds(g.n * TG, TG), :], ALU.add).then_inc(updated, 1)
                    if now:
                        vec.wait_ge(inverted, r.n + 1)
                        if r.from_second():
                            vec.wait_ge(turned, (r - 2).n + 1)
                        for side in range(2):
                            scale_rows(vec, ln, cen[:, :, :], inverse[:, :], h1[:, r.buf, :, side, :])
                    g = r - 2
                    if g.within(EG):
                        vec.wait_ge(msg_done, g.n + 1)
                        if g.from_second():
                            vec.wait_ge(rows_done, (g - 2).n + 1)
                        if g.from_first():
                            vec.wait_ge(scanned, g.n)
                        vec.tensor_tensor_scan(agg[:, g.buf, :], k.same[0:D + 1, bass.ds(g.n * GS, GS)], msg[:, g.buf, :],
                                               agg[:, (g - 1).buf, GS - 1:GS] if g.from_first() else 0.0,
                                               ALU.mult, ALU.add).then_inc(scanned, 1)
                    mask(r - 1, 7, 9)

                rounds(vec, EG, 3, step)

            @block.scalar
            def _(act):
                def step(r):
                    g = r
                    if g.within(EG):
                        act.wait_ge(ln, g.n * 5 + 2)
                        act.activation(squares[:, :, :], cen[:, :, :], ACT.Square, scale=0.125).then_inc(sq_done, 1)
                    g = r - 2
                    if g.within(EG):
                        act.wait_ge(z_used, (g.n + 1) * PAIRS)
                        if g.from_second():
                            act.wait_ge(scanned, (g - 2).n + 1)
                        act.activation(msg[0:D, g.buf, :], k.bank[3 + g.buf][0:D, :], ACT.Copy).then_inc(msg_done, 1)
                    g = r
                    if g.within(EG):
                        act.wait_ge(ln, g.n * 5 + 3)
                        act.activation(roots[:, :], roots[:, :], ACT.Sqrt, bias=k.eps_col[:, 0:1]).then_inc(rooted, 1)
                        act.wait_ge(turned, g.n + 1)
                        if g.from_second():
                            act.wait_ge(z_made, (g - 1).n * PAIRS)
                        act.activation(ht[:, g.buf, :], k.bank[0][:, :], ACT.Copy).then_inc(ht_done, 1)

                rounds(act, EG, 2, step)

            @block.tensor
            def _(pe):
                pe.wait_ge(wrel_in, 16)
                pe.sem_inc(pe_wait, 1)

                def messages(g, first, count):
                    if not g.within(EG):
                        return
                    if first == 0 and g.from_second():
                        pe.wait_ge(msg_done, (g - 1).n)
                    for n in range(first, first + count):
                        pe.wait_ge(z_made, g.n * PAIRS + n + 1)
                        pe.matmul(k.bank[3 + g.buf][0:D, :], wrel[:, n, :], z[:, n % NZ, :],
                                  start=n == 0, stop=n == PAIRS - 1).then_inc(z_used, 1)

                def step(r):
                    messages(r - 1, 0, 8)
                    g = r - 2
                    if g.within(EG):
                        pe.wait_ge(scanned, g.n + 1)
                        if g.from_first():
                            pe.wait_ge(updated, g.n * 5 - 1)
                        pe.sem_inc(pe_wait, 1)
                        for t in range(TG):
                            mm = pe.transpose(k.bank[2][:, t * (D + 1):(t + 1) * (D + 1)], agg[:, g.buf, t * P:(t + 1) * P],
                                              k.ident[0:D + 1, 0:D + 1])
                        mm.then_inc(rows_done, 1)
                    messages(r - 1, 8, 4)
                    g = r
                    if g.within(EG):
                        pe.wait_ge(ln, g.n * 5 + 5)
                        if g.from_first():
                            pe.wait_ge(ht_done, g.n)
                        pe.sem_inc(pe_wait, 1)
                        for t in range(TG):
                            mm = pe.transpose(k.bank[0][:, t * P:(t + 1) * P], h1[:, g.buf, t].rearrange("p s d -> p (s d)"),
                                              k.ident[:, :])
                        mm.then_inc(turned, 1)
                    messages(r - 1, 12, 4)

                rounds(pe, EG, 2, step)


def layer2(nc, k):
    with ExitStack() as ctx:
        def sb(name, shape, dt=F32):
            return k.sb(name, shape, dt, ctx)

        def sem(name):
            return k.sem(name, ctx)

        SIDES = 2 * TG
        xx = sb("l2_xx", [P, 2, TG, 2, D])
        h = sb("l2_h", [P, 2, TG, 2, D])
        squares = sb("l2_squares", [P, SIDES, D])
        h_squares = sb("l2_h_squares", [P, SIDES, D])
        stats = sb("l2_stats", [P, SIDES])
        roots = sb("l2_roots", [P, SIDES])
        inverse = sb("l2_inverse", [P, SIDES])
        prod = sb("l2_prod", [P, TG, D])
        dot = sb("l2_dot", [P, TG])
        norms = sb("l2_norms", [P, TG, 2])
        scale = sb("l2_scale", [P, TG])
        score = sb("l2_score", [P, TG])
        e = sb("l2_e", [P, 2, TG])
        v = sb("l2_v", [P, TG, D + 1])
        key_row = sb("l2_key_row", [P, 2, GS])
        equal = sb("l2_equal", [P, TG, GS])
        earlier = sb("l2_earlier", [P, TG, GS], BF16)
        junk = sb("l2_junk", [P, TG, GS], BF16)
        before = sb("l2_before", [P, TG])
        away = sb("l2_away", [P, TG])
        drop_i = sb("l2_drop_i", [P, TG], I32)
        drop = sb("l2_drop", [P, TG])
        sums = sb("l2_sums", [P, 2, TG, D + 1])
        src_ring = sb("l2_src_ring", [P, 2, TG], I32)
        dst_ring = sb("l2_dst_ring", [P, 2, TG], I32)
        add_ring = sb("l2_add_ring", [P, 2, TG], I32)

        gathered, kept, key_in = (k.pair_of_sems("l2_" + n, ctx) for n in ("gathered", "kept", "key_in"))
        ln, dots, packed = sem("l2_ln"), sem("l2_dots"), sem("l2_packed")
        sq_done, h_sq_done = sem("l2_sq_done"), sem("l2_h_sq_done")
        rooted, normed, inverted, exped = sem("l2_rooted"), sem("l2_normed"), sem("l2_inverted"), sem("l2_exped")
        summed, sums_out, added = sem("l2_summed"), sem("l2_sums_out"), sem("l2_added")
        consts, indexed = sem("l2_consts"), sem("l2_indexed")
        pe_wait, pool_wait, idx_copied = sem("l2_pe_wait"), sem("l2_pool_wait"), sem("l2_idx_copied")
        PACK = 6 + 2 * TG

        def sides(a, g):
            return a[:, g.buf].rearrange("p t s d -> p (t s) d")

        with nc.Block() as block:
            @block.sync
            def _(sp):
                def step(r):
                    g = r
                    if g.within(EG):
                        if g.from_second():
                            sp.wait_ge(packed, (g - 1).n * PACK)
                        sp.dma_start(key_row[:, g.buf, :], k.src_row[bass.ds(g.n * GS, GS)].partition_broadcast(P)
                                     ).then_inc(key_in[g.buf], 16)
                    g = r - 1
                    if g.within(EG):
                        sp.wait_ge(gathered[g.buf], (g.half + 1) * (2 * TG * 16))
                        sp.dma_start(k.x_src[:, bass.ds(g.n * TG, TG), :], xx[:, g.buf, :, 0, :]).then_inc(kept[g.buf], 16)

                rounds(sp, EG, 1, step)
                for b in range(2):
                    sp.wait_ge(kept[b], (EG + 1 - b) // 2 * 16)

            @block.gpsimd
            def _(pool):
                pool.memset(earlier[:, :, :], 1.0).then_inc(consts, 1)
                pool.iota(drop_i[:, :], pattern=[[P, TG]], base=NODES, channel_multiplier=1).then_inc(consts, 1)
                pool.wait_ge(consts, 2)
                pool.affine_select(out=earlier[:, :, :], in_=earlier[:, :, :], compare_op=ALU.is_gt, fill=0.0,
                                   base=0, pattern=[[P, TG], [-1, GS]], channel_multiplier=1).then_inc(consts, 1)

                def step(r):
                    g = r
                    if g.within(EG):
                        if g.from_second():
                            pool.wait_ge(ln, (g - 2).n * 4 + 2)
                            pool.wait_ge(kept[g.buf], g.half * 16)
                        gather_group(pool, g, ((xx[:, g.buf, :, 0, :], k.x2_table, k.src_idx, src_ring),
                                               (xx[:, g.buf, :, 1, :], k.x2_table, k.dst_idx, dst_ring)),
                                     idx_copied, gathered, pool_wait)
                    g = r - 3
                    if g.within(EG):
                        pool.wait_ge(sums_out, g.n + 1)
                        pool.wait_ge(indexed, g.n + 1)
                        if g.from_first():
                            pool.wait_ge(added, g.n * (TG * 16))
                        pool.sem_inc(pool_wait, 1)
                        for t in range(TG):
                            pool.indirect_dma_start(
                                k.sum_table[:, :], bass.IndirectOffsetOnAxis(ap=add_ring[:, g.buf, t:t + 1], axis=0),
                                sums[:, g.buf, t, :], None, compute_op=ALU.add).then_inc(added, 16)

                rounds(pool, EG, 3, step)
                pool.wait_ge(added, EG * TG * 16)

            @block.vector
            def _(vec):
                vec.wait_ge(consts, 3)
                vec.tensor_copy(drop[:, :], drop_i[:, :]).then_inc(consts, 1)

                def step(r):
                    g = r - 2
                    if g.within(EG):
                        vec.wait_ge(exped, g.n + 1)
                        if g.from_first():
                            vec.wait_ge(summed, g.n)
                        vec.tensor_tensor(v[:, :, 0:D], h[:, g.buf, :, 1, :], e[:, g.buf, :].unsqueeze(2).to_broadcast([P, TG, D]),
                                          ALU.mult).then_inc(packed, 1)
                        vec.tensor_copy(v[:, :, D], e[:, g.buf, :]).then_inc(packed, 1)
                        vec.wait_ge(key_in[g.buf], (g.half + 1) * 16)
                        key = k.src_key[:, bass.ds(g.n * TG, TG)]
                        vec.tensor_copy(away[:, :], key).then_inc(packed, 1)
                        vec.wait_ge(packed, g.n * PACK + 3)
                        for t in range(TG):
                            vec.tensor_scalar(equal[:, t, :], key_row[:, g.buf, :], away[:, t:t + 1], None,
                                              ALU.is_equal).then_inc(packed, 1)
                        for t in range(TG):
                            vec.wait_ge(packed, g.n * PACK + 4 + t)
                            vec.scalar_tensor_tensor(out=junk[:, t, :], in0=equal[:, t, :], scalar=1.0, in1=earlier[:, t, :],
                                                     op0=ALU.mult, op1=ALU.mult, accum_out=before[:, t:t + 1]).then_inc(packed, 1)
                        vec.wait_ge(packed, g.n * PACK + 3 + 2 * TG)
                        vec.tensor_scalar(before[:, :], before[:, :], 0.5, None, ALU.is_gt).then_inc(packed, 1)
                        vec.wait_ge(packed, g.n * PACK + 4 + 2 * TG)
                        vec.tensor_tensor(away[:, :], drop[:, :], away[:, :], ALU.subtract).then_inc(packed, 1)
                        vec.wait_ge(packed, g.n * PACK + 5 + 2 * TG)
                        vec.tensor_tensor(away[:, :], away[:, :], before[:, :], ALU.mult).then_inc(packed, 1)
                        vec.wait_ge(packed, g.n * PACK + 6 + 2 * TG)
                        if g.from_second():
                            vec.wait_ge(added, (g - 1).n * (TG * 16))
                        vec.tensor_tensor(add_ring[:, g.buf, :], away[:, :], key, ALU.add).then_inc(indexed, 1)
                    g = r
                    if g.within(EG):
                        vec.wait_ge(gathered[g.buf], (g.half + 1) * (2 * TG * 16))
                        center_rows(vec, ln, g.n * 4, sides(xx, g), stats[:, :], sides(h, g))
                    g = r - 1
                    if g.within(EG):
                        vec.tensor_tensor(prod[:, :, :], h[:, g.buf, :, 0, :], h[:, g.buf, :, 1, :], ALU.mult).then_inc(dots, 1)
                        vec.wait_ge(dots, g.n * 7 + 1)
                        vec.tensor_reduce(dot[:, :], prod[:, :, :], AX.X, ALU.add).then_inc(dots, 1)
                    g = r
                    if g.within(EG):
                        vec.wait_ge(sq_done, g.n + 1)
                        vec.tensor_reduce(roots[:, :], squares[:, :, :], AX.X, ALU.add).then_inc(ln, 1)
                    g = r - 1
                    if g.within(EG):
                        vec.wait_ge(h_sq_done, g.n + 1)
                        vec.tensor_reduce(norms[:, :, :].rearrange("p t s -> p (t s)"), h_squares[:, :, :], AX.X, ALU.add).then_inc(dots, 1)
                        vec.wait_ge(dots, g.n * 7 + 3)
                        vec.tensor_scalar(norms[:, :, :], norms[:, :, :], 1e-24, None, ALU.max).then_inc(dots, 1)
                    g = r
                    if g.within(EG):
                        vec.wait_ge(rooted, g.n + 1)
                        vec.reciprocal(inverse[:, :], roots[:, :]).then_inc(inverted, 1)
                        vec.wait_ge(inverted, g.n + 1)
                        scale_rows(vec, ln, sides(h, g), inverse[:, :], sides(h, g))
                    g = r - 1
                    if g.within(EG):
                        vec.wait_ge(normed, g.n + 1)
                        vec.tensor_tensor(scale[:, :], norms[:, :, 0], norms[:, :, 1], ALU.mult).then_inc(dots, 1)
                        vec.wait_ge(dots, g.n * 7 + 5)
                        vec.reciprocal(scale[:, :], scale[:, :]).then_inc(dots, 1)
                        vec.wait_ge(dots, g.n * 7 + 6)
                        if g.from_first():
                            vec.wait_ge(exped, g.n)
                        vec.tensor_tensor(score[:, :], dot[:, :], scale[:, :], ALU.mult).then_inc(dots, 1)

                rounds(vec, EG, 2, step)

            @block.scalar
            def _(act):
                def step(r):
                    g = r
                    if g.within(EG):
                        act.wait_ge(ln, g.n * 4 + 2)
                        act.activation(squares[:, :, :], sides(h, g), ACT.Square, scale=0.125).then_inc(sq_done, 1)
                    g = r - 1
                    if g.within(EG):
                        act.activation(h_squares[:, :, :], sides(h, g), ACT.Square).then_inc(h_sq_done, 1)
                    g = r
                    if g.within(EG):
                        act.wait_ge(ln, g.n * 4 + 3)
                        act.activation(roots[:, :], roots[:, :], ACT.Sqrt, bias=k.eps_col[:, 0:1]).then_inc(rooted, 1)
                    g = r - 1
                    if g.within(EG):
                        act.wait_ge(dots, g.n * 7 + 4)
                        act.activation(norms[:, :, :], norms[:, :, :], ACT.Sqrt).then_inc(normed, 1)
                    g = r - 2
                    if g.within(EG):
                        act.wait_ge(summed, g.n + 1)
                        if g.from_second():
                            act.wait_ge(added, (g - 1).n * (TG * 16))
                        act.activation(sums[:, g.buf], k.bank[0][:, 0:TG * (D + 1)].rearrange("p (t d) -> p t d", d=D + 1),
                                       ACT.Copy).then_inc(sums_out, 1)
                    g = r - 1
                    if g.within(EG):
                        act.wait_ge(dots, g.n * 7 + 7)
                        if g.from_second():
                            act.wait_ge(packed, (g - 1).n * PACK)
                        act.activation(e[:, g.buf, :], score[:, :], ACT.Exp).then_inc(exped, 1)

                rounds(act, EG, 2, step)

            @block.tensor
            def _(pe):
                def step(g):
                    pe.wait_ge(packed, g.n * PACK + 3 + TG)
                    if g.from_first():
                        pe.wait_ge(sums_out, g.n)
                    pe.sem_inc(pe_wait, 1)
                    for t in range(TG):
                        for u in range(TG):
                            mm = pe.matmul(k.bank[0][:, t * (D + 1):(t + 1) * (D + 1)], equal[:, u, t * P:(t + 1) * P],
                                           v[:, u, :], start=u == 0, stop=u == TG - 1)
                    mm.then_inc(summed, 1)

                rounds(pe, EG, 0, step)


def layer3(nc, k):
    with ExitStack() as ctx:
        def sb(name, shape, dt=F32):
            return k.sb(name, shape, dt, ctx)

        def sem(name):
            return k.sem(name, ctx)

        ss = sb("l3_ss", [P, 2, TG, D + 1])
        total = sb("l3_total", [P, TG])
        change = sb("l3_change", [P, TG, D])
        x3 = sb("l3_x3", [P, TG, D])
        x2 = sb("l3_x2", [NP, 2, NG, D])
        node_sums = sb("l3_node_sums", [NP, 2, NG, D + 1])
        node_total = sb("l3_node_total", [NP, NG])
        outs = sb("l3_outs", [NP, 2, NG, D])
        h = sb("l3_h", [P, 2, TG, D])
        squares = sb("l3_squares", [P, 2, TG, D])
        stats = sb("l3_stats", [P, 2, TG])
        roots = sb("l3_roots", [P, 2, TG])
        inverse = sb("l3_inverse", [P, 2, TG])
        ht = sb("l3_ht", [D, GS])
        msg = sb("l3_msg", [D, 2, GS])
        agg = sb("l3_agg", [D, 2, GS])
        deg = sb("l3_deg", [P, TG])
        mean = sb("l3_mean", [P, TG, D])
        y = sb("l3_y", [P, TG, D])
        src_ring = sb("l3_src_ring", [P, 2, TG], I32)

        gathered = k.pair_of_sems("l3_gathered", ctx)
        nodes_in, out_stored, outed = k.pair_of_sems("l3_nodes_in", ctx), k.pair_of_sems("l3_out_stored", ctx), sem("l3_outed")
        lna, lnb = sem("l3_lna"), sem("l3_lnb")
        sqa_done, sqb_done, rooted, inverted = sem("l3_sqa_done"), sem("l3_sqb_done"), sem("l3_rooted"), sem("l3_inverted")
        turned, ht_done, m_done, msg_done = sem("l3_turned"), sem("l3_ht_done"), sem("l3_m"), sem("l3_msg_done")
        scanned, rows_done = sem("l3_scanned"), sem("l3_rows")
        pe_wait, pool_wait, idx_copied = (sem("l3_" + n) for n in ("pe_wait", "pool_wait", "idx_copied"))

        def x_dst(g):
            return k.x_dst[:, bass.ds(g.n * TG, TG), :]

        def x_src(g):
            return k.x_src[:, bass.ds(g.n * TG, TG), :]

        def live(r):
            return (0 if r.within(EG) else 1), (2 if (r - 3).within(EG) else 1)

        def nodes(a, g):
            return a[0:NODES, :].rearrange("(p j) d -> p j d", p=NP)[:, bass.ds(g.n * NG, NG), :]

        with nc.Block() as block:
            @block.sync
            def _(sp):
                def step(r):
                    g = r
                    if g.within(DG):
                        if g.from_second():
                            sp.wait_ge(outed, (g - 2).n * 5 + 5)
                        sp.dma_start(x2[:, g.buf], nodes(k.x2_table, g)).then_inc(nodes_in[g.buf], 16)
                        sp.dma_start(node_sums[:, g.buf], nodes(k.sum_table, g)).then_inc(nodes_in[g.buf], 16)
                    g = r - 1
                    if g.within(DG):
                        sp.wait_ge(outed, g.n * 5 + 5)
                        sp.dma_start(nodes(k.out, g), outs[:, g.buf]).then_inc(out_stored[g.buf], 16)

                rounds(sp, DG, 1, step)
                for b in range(2):
                    sp.wait_ge(out_stored[b], (DG + 1 - b) // 2 * 16)

            @block.gpsimd
            def _(pool):
                def step(r):
                    g = r
                    if g.within(EG):
                        if g.from_second():
                            pool.wait_ge(lna, (g - 2).n * 8 + 3)
                        gather_group(pool, g, ((ss[:, g.buf], k.sum_table, k.src_idx, src_ring),),
                                     idx_copied, gathered, pool_wait)

                rounds(pool, EG, 0, step)

            @block.vector
            def _(vec):
                def step(r):
                    edges, of_nodes = r.within(EG), r.within(DG)
                    g = r
                    n, m = g.n * 8, g.n * 5
                    if edges:
                        vec.wait_ge(gathered[g.buf], (g.half + 1) * (TG * 16))
                        vec.tensor_scalar(total[:, :], ss[:, g.buf, :, D], TINY, None, ALU.max).then_inc(lna, 1)
                    if of_nodes:
                        vec.wait_ge(nodes_in[g.buf], (g.half + 1) * 32)
                        vec.tensor_scalar(node_total[:, :], node_sums[:, g.buf, :, D], TINY, None, ALU.max).then_inc(outed, 1)
                    if edges:
                        vec.wait_ge(lna, n + 1)
                        vec.reciprocal(total[:, :], total[:, :]).then_inc(lna, 1)
                    if of_nodes:
                        vec.wait_ge(outed, m + 1)
                        vec.reciprocal(node_total[:, :], node_total[:, :]).then_inc(outed, 1)
                    if edges:
                        vec.wait_ge(lna, n + 2)
                        vec.tensor_tensor(change[:, :, :], ss[:, g.buf, :, 0:D],
                                          total[:, :].unsqueeze(2).to_broadcast([P, TG, D]), ALU.mult).then_inc(lna, 1)
                    if of_nodes:
                        vec.wait_ge(outed, m + 2)
                        if g.from_second():
                            vec.wait_ge(out_stored[g.buf], g.half * 16)
                        vec.tensor_tensor(outs[:, g.buf], node_sums[:, g.buf, :, 0:D],
                                          node_total[:, :].unsqueeze(2).to_broadcast([NP, NG, D]), ALU.mult).then_inc(outed, 1)
                    if edges:
                        vec.wait_ge(lna, n + 3)
                        vec.tensor_tensor(x3[:, :, :], change[:, :, :], x_src(g), ALU.add).then_inc(lna, 1)
                        vec.wait_ge(lna, n + 4)
                        if g.from_second():
                            vec.wait_ge(turned, (g - 2).n + 1)
                        center_rows(vec, lna, n + 4, x3[:, :, :], stats[:, 0, :], h[:, g.buf])
                    g = r - 3
                    k3 = g.n * 8
                    if g.within(EG):
                        sums = k.bank[2][:, 0:TG * D].rearrange("p (t d) -> p t d", d=D)
                        vec.tensor_scalar(deg[:, :], k.degree[:, bass.ds(g.n * TG, TG)], 1e-6, None, ALU.add).then_inc(lnb, 1)
                        vec.wait_ge(lnb, k3 + 1)
                        vec.reciprocal(deg[:, :], deg[:, :]).then_inc(lnb, 1)
                        vec.wait_ge(lnb, k3 + 2)
                        vec.wait_ge(rows_done, g.n + 1)
                        vec.scalar_tensor_tensor(out=mean[:, :, :], in0=sums, scalar=0.0,
                                                 in1=deg[:, :].unsqueeze(2).to_broadcast([P, TG, D]),
                                                 op0=ALU.max, op1=ALU.mult).then_inc(lnb, 1)
                        vec.wait_ge(lnb, k3 + 3)
                        center_rows(vec, lnb, k3 + 3, mean[:, :, :], stats[:, 1, :], y[:, :, :])
                    if of_nodes:
                        vec.wait_ge(outed, m + 3)
                        vec.tensor_tensor(outs[:, r.buf], outs[:, r.buf], x2[:, r.buf], ALU.add).then_inc(outed, 1)
                    for j, g, ln, done in ((0, r, lna, sqa_done), (1, r - 3, lnb, sqb_done)):
                        if g.within(EG):
                            vec.wait_ge(done, g.n + 1)
                            vec.tensor_reduce(roots[:, j, :], squares[:, j], AX.X, ALU.add).then_inc(ln, 1)
                    g = r - 2
                    if g.within(EG):
                        vec.wait_ge(msg_done, g.n + 1)
                        if g.from_second():
                            vec.wait_ge(rows_done, (g - 2).n + 1)
                        if g.from_first():
                            vec.wait_ge(scanned, g.n)
                        vec.tensor_tensor_scan(agg[:, g.buf, :], k.same[0:D, bass.ds(g.n * GS, GS)], msg[:, g.buf, :],
                                               agg[:, (g - 1).buf, GS - 1:GS] if g.from_first() else 0.0,
                                               ALU.mult, ALU.add).then_inc(scanned, 1)
                    lo, hi = live(r)
                    if lo < hi:
                        vec.wait_ge(rooted, r.n + 1)
                        vec.reciprocal(inverse[:, lo:hi, :], roots[:, lo:hi, :]).then_inc(inverted, 1)
                    if of_nodes:
                        vec.wait_ge(outed, m + 4)
                        vec.tensor_tensor(outs[:, r.buf], outs[:, r.buf],
                                          k.beta_b[0:NP, :].unsqueeze(1).to_broadcast([NP, NG, D]), ALU.add).then_inc(outed, 1)
                    if lo < hi:
                        vec.wait_ge(inverted, r.n + 1)
                    if edges:
                        scale_rows(vec, lna, h[:, r.buf], inverse[:, 0, :], h[:, r.buf])
                    g = r - 3
                    if g.within(EG):
                        scale_rows(vec, lnb, y[:, :, :], inverse[:, 1, :], y[:, :, :], relu=False)
                        vec.wait_ge(lnb, k3 + 7)
                        vec.tensor_tensor(x_dst(g), y[:, :, :], k.gamma_b[:, :].unsqueeze(1).to_broadcast([P, TG, D]),
                                          ALU.mult).then_inc(lnb, 1)

                rounds(vec, EG, 3, step)

            @block.scalar
            def _(act):
                def step(r):
                    g = r
                    if g.within(EG):
                        act.wait_ge(lna, g.n * 8 + 6)
                        act.activation(squares[:, 0], h[:, g.buf], ACT.Square, scale=0.125).then_inc(sqa_done, 1)
                    g = r - 3
                    if g.within(EG):
                        act.wait_ge(lnb, g.n * 8 + 5)
                        act.activation(squares[:, 1], y[:, :, :], ACT.Square, scale=0.125).then_inc(sqb_done, 1)
                    lo, hi = live(r)
                    if lo < hi:
                        if r.within(EG):
                            act.wait_ge(lna, r.n * 8 + 7)
                        if (r - 3).within(EG):
                            act.wait_ge(lnb, (r - 3).n * 8 + 6)
                        act.activation(roots[:, lo:hi, :], roots[:, lo:hi, :], ACT.Sqrt, bias=k.eps_col[:, 0:1]).then_inc(rooted, 1)
                    g = r
                    if g.within(EG):
                        act.wait_ge(turned, g.n + 1)
                        if g.from_first():
                            act.wait_ge(m_done, g.n)
                        act.activation(ht[:, :], k.bank[0][0:D, :], ACT.Copy).then_inc(ht_done, 1)
                        act.wait_ge(m_done, g.n + 1)
                        if g.from_second():
                            act.wait_ge(scanned, (g - 2).n + 1)
                        act.activation(msg[:, g.buf, :], k.bank[1][0:D, :], ACT.Identity, bias=k.b3c[:, 0:1]).then_inc(msg_done, 1)

                rounds(act, EG, 3, step)

            @block.tensor
            def _(pe):
                def step(r):
                    g = r
                    if g.within(EG):
                        pe.wait_ge(lna, g.n * 8 + 8)
                        if g.from_first():
                            pe.wait_ge(ht_done, g.n)
                        pe.sem_inc(pe_wait, 1)
                        for t in range(TG):
                            mm = pe.transpose(k.bank[0][0:D, t * P:(t + 1) * P], h[:, g.buf, t, :], k.ident[:, :])
                        mm.then_inc(turned, 1)
                    g = r - 2
                    if g.within(EG):
                        pe.wait_ge(scanned, g.n + 1)
                        if g.from_first():
                            pe.wait_ge(lnb, g.n * 8 - 5)
                        pe.sem_inc(pe_wait, 1)
                        for t in range(TG):
                            mm = pe.transpose(k.bank[2][:, t * D:(t + 1) * D], agg[:, g.buf, t * P:(t + 1) * P], k.ident[0:D, 0:D])
                        mm.then_inc(rows_done, 1)
                    g = r
                    if g.within(EG):
                        pe.wait_ge(ht_done, g.n + 1)
                        if g.from_first():
                            pe.wait_ge(msg_done, g.n)
                        pe.sem_inc(pe_wait, 1)
                        pe.matmul(k.bank[1][0:D, :], k.w3[:, :], ht[:, :], start=True, stop=True).then_inc(m_done, 1)

                rounds(pe, EG, 2, step)


def write_last(nc, k):
    with ExitStack() as ctx:
        rows = k.sb("out_rows", [P, 2, TG, D], F32, ctx)
        last_ring = k.sb("out_last_ring", [P, 2, TG], I32, ctx)
        copied, idx_copied, pool_wait, act_wait = (
            k.sem("out_" + n, ctx) for n in ("copied", "idx_copied", "pool_wait", "act_wait"))
        scattered = k.pair_of_sems("out_scattered", ctx)

        with nc.Block() as block:
            @block.scalar
            def _(act):
                def step(g):
                    if g.from_second():
                        act.wait_ge(scattered[g.buf], g.half * (TG * 16))
                        act.sem_inc(act_wait, 1)
                    act.activation(rows[:, g.buf], k.x_dst[:, bass.ds(g.n * TG, TG), :], ACT.Copy).then_inc(copied, 1)

                rounds(act, EG, 0, step)

            @block.gpsimd
            def _(pool):
                def step(g):
                    scatter_group(pool, g, rows, copied, g.n + 1, k.out, k.last_idx, last_ring, idx_copied, scattered, pool_wait,
                                  compute_op=ALU.add)

                rounds(pool, EG, 0, step)
                for b in range(2):
                    pool.wait_ge(scattered[b], (EG + 1 - b) // 2 * TG * 16)


_INS = ["x", "src", "dst", "edge_attr_32", "edge_type_32", "L0_gnn_w_m1", "L0_gnn_b_m1", "L0_gnn_w_m2",
        "L0_gnn_b_m2", "L0_gnn_w_u1", "L0_gnn_b_u1", "L0_gnn_w_u2", "L0_gnn_b_u2", "L1_gnn_basis",
        "L1_gnn_coeff", "L1_gnn_self_weight", "L1_gnn_bias", "L3_gnn_W", "L3_gnn_b", "L3_gnn_gamma",
        "L3_gnn_beta"]
_TURNED = ("L1_gnn_coeff", "L3_gnn_W")


def kernel(**inputs):
    import numpy as _np
    import concourse.bacc as _bacc
    from concourse import mybir as _mybir
    from concourse.bass_utils import run_bass_kernel_spmd as _run

    nc = _bacc.Bacc("TRN2", target_bir_lowering=False, num_devices=1)
    arrays, args = {}, []
    for name in _INS:
        a = _np.asarray(inputs[name])
        a = _np.ascontiguousarray(a.T if name in _TURNED else a)
        arrays[f"in_{name}_dram"] = a
        args.append(nc.dram_tensor(f"in_{name}_dram", a.shape, _mybir.dt.from_np(a.dtype), kind="ExternalInput").ap())
    out = nc.dram_tensor("out_0_dram", (NODES, D), _mybir.dt.float32, kind="ExternalOutput").ap()
    build(nc, *args, out)
    r = _run(nc, [arrays], core_ids=[0])
    return r.results[0]["out_0_dram"]
```

```python
from contextlib import ExitStack

import concourse.bass as bass
from concourse import mybir
from concourse.alu_op_type import AluOpType as ALU

ACT = mybir.ActivationFunctionType
F32 = mybir.dt.float32
BF16 = mybir.dt.bfloat16
I32 = mybir.dt.int32
AX = mybir.AxisListType

P = 128
NODES = 50000
EDGES = 25000
D = 64
ED = 32
H = 128
RELS = 32
BASES = 30

TG = 4
GS = TG * P
EG = -(-EDGES // GS)
SLOTS = EG * GS
ET = SLOTS // P
PAD = SLOTS - EDGES
ROWS = ET // 2
FAR = 65536

NP = 125
NPP = NODES // NP
NG = 8
DG = NPP // NG
HALF = NG // 2 * NP

CLEAR = -(-(NODES + GS) // (P * EG))
SUM_ROWS = CLEAR * P * EG
TINY = 1e-30
LN_EPS = 1e-5
COUNT_CHUNK = SLOTS // 7


BIAS_ROWS = 65


class Group:

    def __init__(self, pair, off):
        self.pair, self.off = pair, off

    def __sub__(self, k):
        return Group(self.pair, self.off - k)

    def __add__(self, k):
        return Group(self.pair, self.off + k)

    @property
    def n(self):
        return self.pair * 2 + self.off

    @property
    def half(self):
        return self.pair + self.off // 2

    @property
    def buf(self):
        return self.off % 2

    def within(self, count):
        return not isinstance(self.pair, int) or 0 <= self.off < count

    def from_first(self):
        return not isinstance(self.pair, int) or self.off >= 1

    def from_second(self):
        return not isinstance(self.pair, int) or self.off >= 2


def rounds(eng, groups, skew, step):
    first = (skew + 3) // 2 * 2
    last = groups // 2 * 2
    for r in range(first):
        step(Group(0, r))
    with eng.Fori(first // 2, last // 2) as pair:
        step(Group(pair, 0))
        step(Group(pair, 1))
    for r in range(last, groups + skew):
        step(Group(0, r))


def center_rows(vec, done, n, rows, total, centered):
    vec.tensor_reduce(total, rows, AX.X, ALU.add).then_inc(done, 1)
    vec.wait_ge(done, n + 1)
    vec.scalar_tensor_tensor(out=centered, in0=rows, scalar=float(D),
                             in1=total.unsqueeze(2).to_broadcast(list(centered.shape)),
                             op0=ALU.mult, op1=ALU.subtract).then_inc(done, 1)


def scale_rows(vec, done, centered, inverse, out, relu=True):
    scale = inverse.unsqueeze(2).to_broadcast(list(out.shape))
    if relu:
        vec.scalar_tensor_tensor(out=out, in0=centered, scalar=0.0, in1=scale,
                                 op0=ALU.max, op1=ALU.mult).then_inc(done, 1)
    else:
        vec.tensor_tensor(out, centered, scale, ALU.mult).then_inc(done, 1)


class Shared:
    pass


def build(nc, x, src, dst, attr, etype, w_m1, b_m1, w_m2, b_m2, w_u1, b_u1, w_u2, b_u2,
          basis, coeff_t, w_self, b_rel, w3_t, b3, gamma, beta, out):
    k = Shared()
    k.x, k.src, k.dst, k.attr, k.etype = x, src, dst, attr, etype
    k.w_m1, k.b_m1, k.w_m2, k.b_m2, k.w_u1, k.b_u1, k.w_u2, k.b_u2 = w_m1, b_m1, w_m2, b_m2, w_u1, b_u1, w_u2, b_u2
    k.basis, k.coeff_t, k.w_self, k.b_rel = basis, coeff_t, w_self, b_rel
    k.w3_t, k.b3, k.gamma, k.beta, k.out = w3_t, b3, gamma, beta, out
    k.src_s = nc.dram_tensor("src_s", [SLOTS, 1], I32)
    k.dst_s = nc.dram_tensor("dst_s", [SLOTS + 2, 1], I32)
    k.typ_s = nc.dram_tensor("typ_s", [SLOTS, 1], I32)
    k.attr_s = nc.dram_tensor("attr_s", [SLOTS, ED], F32)
    k.src_r = nc.dram_tensor("src_r", [SLOTS, 1], I32)
    k.dst_r = nc.dram_tensor("dst_r", [SLOTS, 1], I32)
    k.typ_r = nc.dram_tensor("typ_r", [SLOTS, 1], I32)
    k.attr_r = nc.dram_tensor("attr_r", [SLOTS, ED], F32)
    k.same_row = nc.dram_tensor("same_row", [SLOTS], BF16)
    k.type_row = nc.dram_tensor("type_row", [SLOTS], F32)
    k.src_row = nc.dram_tensor("src_row", [SLOTS], F32)
    k.rel_rows = nc.dram_tensor("rel_rows", [RELS, D * D], F32)
    k.x1_table = nc.dram_tensor("x1_table", [NODES, D], F32)
    k.x2_table = nc.dram_tensor("x2_table", [NODES, D], F32)
    k.sum_table = nc.dram_tensor("sum_table", [SUM_ROWS, D + 1], F32)

    with ExitStack() as ctx:
        def sb(name, shape, dt=F32, stack=ctx):
            return stack.enter_context(nc.sbuf_tensor(name, shape, dt))

        def sem(name, stack=ctx):
            return stack.enter_context(nc.semaphore(name))

        def pair_of_sems(name, stack=ctx):
            return [sem(name + "0", stack), sem(name + "1", stack)]

        k.sb, k.sem, k.pair_of_sems = sb, sem, pair_of_sems
        k.pe_wait, k.pool_wait, k.act_wait = sem("pe_wait"), sem("pool_wait"), sem("act_wait")

        k.bank = [ctx.enter_context(nc.psum_tensor(f"bank{i}", [P, 512], F32)) for i in range(8)]

        k.slots = sb("slots", [P, 2 * ET * D])
        k.x_dst = k.slots[:, 0:ET * D].rearrange("p (t d) -> p t d", d=D)
        k.x_src = k.slots[:, ET * D:2 * ET * D].rearrange("p (t d) -> p t d", d=D)
        k.same = sb("same", [P, SLOTS], BF16)
        k.src_idx = sb("src_idx", [P, ET], I32)
        k.dst_idx = sb("dst_idx", [P, ET], I32)
        k.last_idx = sb("last_idx", [P, ET], I32)
        k.src_key = sb("src_key", [P, ET])
        k.degree = sb("degree", [P, ET])
        k.ident = sb("ident", [P, P])
        k.ones = sb("ones", [BIAS_ROWS, P], BF16)
        k.eps_col = sb("eps_col", [P, 1])
        k.wm1 = sb("wm1", [P, H])
        k.wm1e = sb("wm1e", [ED, H])
        k.wm2 = sb("wm2", [P, H])
        k.wu1x = sb("wu1x", [P, H])
        k.wu1a = sb("wu1a", [P, H])
        k.wu2 = sb("wu2", [P, D])
        k.wself = sb("wself", [P, P])
        k.w3 = sb("w3", [D, D])
        k.relcol = sb("relcol", [P, RELS // 2])
        k.bm1 = sb("bm1", [P, 1])
        k.bm2 = sb("bm2", [P, 1])
        k.bu1 = sb("bu1", [P, 1])
        k.b3c = sb("b3c", [D, 1])
        k.bu2_parts = sb("bu2_parts", [BIAS_ROWS, D], BF16)
        k.brel_parts = sb("brel_parts", [BIAS_ROWS, D], BF16)
        k.gamma_b = sb("gamma_b", [P, D])
        k.beta_b = sb("beta_b", [P, D])

        prepare(nc, k)
        dense(nc, k)
        layer0(nc, k)
        layer1(nc, k)
        layer2(nc, k)
        layer3(nc, k)
        write_last(nc, k)


def prepare(nc, k):
    with ExitStack() as ctx:
        def sb(name, shape, dt=F32):
            return k.sb(name, shape, dt, ctx)

        def sem(name):
            return k.sem(name, ctx)

        zero_attr = sb("zero_attr", [PAD, ED])
        zero_pad = sb("zero_pad", [1, PAD], I32)
        src_pad = sb("src_pad", [1, PAD], I32)
        dst_pad = sb("dst_pad", [1, PAD + 2], I32)
        cur_i = sb("cur_i", [ROWS, 2, P], I32)
        prev_i = sb("prev_i", [ROWS, 2, P], I32)
        next_i = sb("next_i", [ROWS, 2, P], I32)
        src_i = sb("src_i", [ROWS, 2, P], I32)
        typ_i = sb("typ_i", [ROWS, 2, P], I32)
        cur = sb("cur", [ROWS, 2, P])
        prev = sb("prev", [ROWS, 2, P])
        nxt = sb("nxt", [ROWS, 2, P])
        srcf = sb("srcf", [ROWS, 2, P])
        typf = sb("typf", [ROWS, 2, P])
        same_t = sb("same_t", [ROWS, 2, P], BF16)
        gath = sb("gath", [ROWS, 2, P])
        src_in = sb("src_in", [ROWS, 2, P])
        scat = sb("scat", [ROWS, 2, P])
        falls = sb("falls", [ROWS, 2 * P])
        falls_sum = sb("falls_sum", [ROWS, 1])
        ones_col = sb("ones_col", [P, 1])
        flag = sb("flag", [1, 1], I32)
        bias_left = sb("bias_left", [BIAS_ROWS, 2, D])
        bias_part = sb("bias_part", [BIAS_ROWS, 2, D], BF16)
        rel_iota = sb("rel_iota", [P, RELS // 2], I32)
        coeff = sb("coeff", [BASES, RELS])
        room = k.same[:, :].bitcast(F32)
        basis_t = room[0:BASES, 0:D * D]
        rel = room[0:RELS, D * D:2 * D * D]
        junk = k.same[:, 4 * D * D:4 * D * D + COUNT_CHUNK]
        tri = sb("tri", [P, P])
        own = sb("own", [P, P])
        counts = sb("counts", [P, SLOTS // COUNT_CHUNK + 1])
        tile_dst_i = sb("tile_dst_i", [P, 1], I32)
        tile_src_i = sb("tile_src_i", [P, 1], I32)
        tile_typ_i = sb("tile_typ_i", [P, 1], I32)
        tile_attr = sb("tile_attr", [P, ED])
        tile_dst = sb("tile_dst", [P, 1])
        tile_half = sb("tile_half", [P, 1])
        rank = sb("rank", [P, 1])
        rank_i = sb("rank_i", [P, 1], I32)

        pads = sem("pads")
        copied = sem("copied")
        order_in = sem("order_in")
        order_v = sem("order_v")
        falls_added = sem("falls_added")
        flag_ready = sem("flag_ready")
        weights_in = sem("weights_in")
        arrays_in = sem("arrays_in")
        arrays_v = sem("arrays_v")
        turned = sem("turned")
        idx_ready = sem("idx_ready")
        rows_out = sem("rows_out")
        same_in = sem("same_in")
        consts = sem("consts")
        bias_in, bias_v = sem("bias_in"), sem("bias_v")
        coeff_in = sem("coeff_in")
        rel_mm = sem("rel_mm")
        rel_copied = sem("rel_copied")
        rel_out = sem("rel_out")
        wide_in = sem("wide_in")
        wide_v = sem("wide_v")
        tile_in = sem("tile_in")
        rank_v = sem("rank_v")
        ranked_out = sem("ranked_out")
        back = sem("back")

        STEPS = SLOTS // COUNT_CHUNK * 2 + 7
        wide = k.slots[:, 0:SLOTS]

        def square(a, first=0):
            return a[first:first + SLOTS, 0].rearrange("(a q f) -> q a f", a=2, f=P)

        with nc.Block() as block:
            @block.sync
            def _(sp):
                sp.dma_start(k.dst_s[1:1 + EDGES, 0].rearrange("(a b) -> a b", a=200),
                             k.dst.rearrange("(a b) -> a b", a=200)).then_inc(copied, 16)
                sp.wait_ge(pads, 6)
                sp.dma_start(k.dst_s[0:1, :].rearrange("a b -> b a"), dst_pad[:, 0:1]).then_inc(copied, 16)
                sp.dma_start(k.dst_s[1 + EDGES:SLOTS + 2, :].rearrange("a b -> b a"),
                             dst_pad[:, 1:PAD + 2]).then_inc(copied, 16)
                sp.dma_start(k.src_s[0:EDGES, 0].rearrange("(a b) -> a b", a=200),
                             k.src.rearrange("(a b) -> a b", a=200)).then_inc(copied, 16)
                sp.dma_start(k.typ_s[0:EDGES, 0].rearrange("(a b) -> a b", a=200),
                             k.etype.rearrange("(a b) -> a b", a=200)).then_inc(copied, 16)
                sp.dma_start(k.src_s[EDGES:SLOTS, :].rearrange("a b -> b a"), src_pad[:, :]).then_inc(copied, 16)
                sp.dma_start(k.typ_s[EDGES:SLOTS, :].rearrange("a b -> b a"), zero_pad[:, :]).then_inc(copied, 16)
                sp.dma_start(k.attr_s[0:EDGES, :].rearrange("(a b) d -> a (b d)", a=200),
                             k.attr.rearrange("(a b) d -> a (b d)", a=200)).then_inc(copied, 16)
                sp.dma_start(k.attr_s[EDGES:SLOTS, :], zero_attr[:, :]).then_inc(copied, 16)
                sp.wait_ge(copied, 9 * 16)
                sp.dma_start(cur_i[:, :, :], square(k.dst_s, 1)).then_inc(order_in, 16)
                sp.dma_start(prev_i[:, :, :], square(k.dst_s, 0)).then_inc(order_in, 16)
                sp.dma_start(bias_left[:, 0, :], k.b_u2.partition_broadcast(BIAS_ROWS)).then_inc(bias_in, 16)
                sp.dma_start(bias_left[:, 1, :], k.b_rel.partition_broadcast(BIAS_ROWS)).then_inc(bias_in, 16)
                sp.dma_start(coeff[:, :], k.coeff_t[:, :]).then_inc(coeff_in, 16)
                sp.dma_start(basis_t, k.basis.rearrange("b i o -> b (i o)")).then_inc(coeff_in, 16)
                loads = [(k.wm1[:, :], k.w_m1[0:P, :]), (k.wm1e[:, :], k.w_m1[P:P + ED, :]),
                         (k.wm2[:, :], k.w_m2[:, :]), (k.wu1x[0:D, :], k.w_u1[0:D, :]),
                         (k.wu1x[D:P, :], k.w_u1[0:D, :]), (k.wu1a[:, :], k.w_u1[D:D + H, :]),
                         (k.wu2[:, :], k.w_u2[:, :]), (k.wself[0:D, 0:D], k.w_self[:, :]),
                         (k.wself[D:P, D:P], k.w_self[:, :]), (k.w3[:, :], k.w3_t[:, :]),
                         (k.bm1[:, :], k.b_m1.unsqueeze(1)), (k.bm2[:, :], k.b_m2.unsqueeze(1)),
                         (k.bu1[:, :], k.b_u1.unsqueeze(1)), (k.b3c[:, :], k.b3.unsqueeze(1)),
                         (k.gamma_b[:, :], k.gamma.partition_broadcast(P)),
                         (k.beta_b[:, :], k.beta.partition_broadcast(P))]
                for to, frm in loads:
                    sp.dma_start(to, frm).then_inc(weights_in, 16)

                sp.wait_ge(flag_ready, 1)
                unsorted = sp.value_load(flag[0:1, 0:1], min_val=0, max_val=SLOTS)
                with sp.If(unsorted > 0):
                    sp.dma_start(wide.bitcast(I32), k.dst_s[1:1 + SLOTS, 0].partition_broadcast(P)).then_inc(wide_in, 16)

                    def load_tile(t):
                        sp.dma_start(tile_dst_i[:, :], k.dst_s[bass.ds(t * P + 1, P), :]).then_inc(tile_in, 16)
                        sp.dma_start(tile_src_i[:, :], k.src_s[bass.ds(t * P, P), :]).then_inc(tile_in, 16)
                        sp.dma_start(tile_typ_i[:, :], k.typ_s[bass.ds(t * P, P), :]).then_inc(tile_in, 16)
                        sp.dma_start(tile_attr[:, :], k.attr_s[bass.ds(t * P, P), :]).then_inc(tile_in, 16)

                    load_tile(0)
                    with sp.Fori(1, ET) as t:
                        sp.wait_ge(ranked_out, t * 64)
                        load_tile(t)
                    sp.wait_ge(ranked_out, ET * 64)
                    sp.dma_start(k.dst_s[1:1 + SLOTS, 0].rearrange("(a b) -> a b", a=P),
                                 k.dst_r[:, 0].rearrange("(a b) -> a b", a=P)).then_inc(back, 16)
                    sp.dma_start(k.src_s[:, 0].rearrange("(a b) -> a b", a=P),
                                 k.src_r[:, 0].rearrange("(a b) -> a b", a=P)).then_inc(back, 16)
                    sp.dma_start(k.typ_s[:, 0].rearrange("(a b) -> a b", a=P),
                                 k.typ_r[:, 0].rearrange("(a b) -> a b", a=P)).then_inc(back, 16)
                    sp.dma_start(k.attr_s[:, :].rearrange("(a b) d -> a (b d)", a=P),
                                 k.attr_r[:, :].rearrange("(a b) d -> a (b d)", a=P)).then_inc(back, 16)
                    sp.wait_ge(back, 64)

                sp.dma_start(cur_i[:, :, :], square(k.dst_s, 1)).then_inc(arrays_in, 16)
                sp.dma_start(prev_i[:, :, :], square(k.dst_s, 0)).then_inc(arrays_in, 16)
                sp.dma_start(next_i[:, :, :], square(k.dst_s, 2)).then_inc(arrays_in, 16)
                sp.dma_start(src_i[:, :, :], square(k.src_s)).then_inc(arrays_in, 16)
                sp.dma_start(typ_i[:, :, :], square(k.typ_s)).then_inc(arrays_in, 16)
                sp.wait_ge(arrays_v, 6)
                sp.dma_start(k.same_row[:].rearrange("(a q f) -> q a f", a=2, f=P), same_t[:, :, :]).then_inc(rows_out, 16)
                sp.dma_start(k.type_row[:].rearrange("(a q f) -> q a f", a=2, f=P), typf[:, :, :]).then_inc(rows_out, 16)
                sp.dma_start(k.src_row[:].rearrange("(a q f) -> q a f", a=2, f=P), srcf[:, :, :]).then_inc(rows_out, 16)
                sp.wait_ge(rel_copied, 8)
                sp.dma_start(k.rel_rows[:, :], rel).then_inc(rel_out, 16)
                sp.wait_ge(rel_out, 16)
                sp.wait_ge(rows_out, 48)
                sp.dma_start(k.same[:, :], k.same_row[:].partition_broadcast(P)).then_inc(same_in, 16)
                sp.wait_ge(weights_in, 16 * len(loads))
                sp.wait_ge(same_in, 16)

            @block.gpsimd
            def _(pool):
                pool.memset(k.ident[:, :], 0.0).then_inc(consts, 1)
                pool.memset(tri[:, :], 1.0).then_inc(consts, 1)
                pool.iota(rel_iota[:, :], pattern=[[2, RELS // 2]], base=0, channel_multiplier=0).then_inc(consts, 1)
                pool.wait_ge(consts, 3)
                pool.affine_select(out=k.ident[:, :], in_=k.ident[:, :], compare_op=ALU.not_equal, fill=1.0,
                                   base=0, pattern=[[-1, P]], channel_multiplier=1).then_inc(consts, 1)
                pool.affine_select(out=tri[:, :], in_=tri[:, :], compare_op=ALU.is_gt, fill=0.0,
                                   base=0, pattern=[[-1, P]], channel_multiplier=1).then_inc(consts, 1)
                pool.wait_ge(flag_ready, 1)
                unsorted = pool.value_load(flag[0:1, 0:1], min_val=0, max_val=SLOTS)
                with pool.If(unsorted > 0):
                    with pool.Fori(0, ET) as t:
                        pool.wait_ge(rank_v, (t + 1) * STEPS)
                        pool.wait_ge(tile_in, (t + 1) * 64)
                        pool.sem_inc(k.pool_wait, 1)
                        for table, column in ((k.dst_r, tile_dst_i), (k.src_r, tile_src_i),
                                              (k.typ_r, tile_typ_i), (k.attr_r, tile_attr)):
                            pool.indirect_dma_start(table[:, :], bass.IndirectOffsetOnAxis(ap=rank_i[:, 0:1], axis=0),
                                                    column[:, :], None).then_inc(ranked_out, 16)
                    pool.wait_ge(ranked_out, ET * 64)

            @block.tensor
            def _(pe):
                pe.wait_ge(coeff_in, 32)
                for c in range(8):
                    if c >= 4:
                        pe.wait_ge(rel_copied, c - 3)
                    pe.matmul(k.bank[c % 4][0:RELS, :], coeff[:, :], basis_t[:, c * 512:(c + 1) * 512],
                              start=True, stop=True).then_inc(rel_mm, 1)
                pe.wait_ge(order_v, 5)
                pe.matmul(k.bank[4][0:1, 0:1], falls_sum[:, :], ones_col[0:ROWS, :],
                          start=True, stop=True).then_inc(falls_added, 1)
                pe.wait_ge(consts, 5)
                pe.wait_ge(arrays_v, 10)
                for n, a in enumerate((src_in, gath, scat)):
                    for c in range(2):
                        pe.transpose(k.bank[5 + n][:, c * ROWS:(c + 1) * ROWS], a[:, c, :],
                                     k.ident[0:ROWS, 0:ROWS]).then_inc(turned, 1)
                for c in range(2):
                    pe.transpose(k.bank[5][:, (2 + c) * ROWS:(3 + c) * ROWS], srcf[:, c, :],
                                 k.ident[0:ROWS, 0:ROWS]).then_inc(turned, 1)

            @block.scalar
            def _(act):
                for c in range(8):
                    act.wait_ge(rel_mm, c + 1)
                    act.activation(rel[:, c * 512:(c + 1) * 512], k.bank[c % 4][0:RELS, :], ACT.Copy).then_inc(rel_copied, 1)

            @block.vector
            def _(vec):
                vec.memset(zero_attr[:, :], 0.0).then_inc(pads, 1)
                vec.memset(zero_pad[:, :], 0).then_inc(pads, 1)
                vec.memset(src_pad[:, :], NODES).then_inc(pads, 1)
                vec.memset(dst_pad[:, 0:PAD + 2], NODES).then_inc(pads, 1)
                vec.memset(k.wself[:, :], 0.0).then_inc(pads, 1)
                vec.wait_ge(pads, 5)
                vec.memset(dst_pad[:, 0:PAD + 2:PAD + 1], -1).then_inc(pads, 1)
                vec.memset(ones_col[:, :], 1.0).then_inc(order_v, 1)
                vec.memset(k.ones[:, :], 1.0)
                vec.memset(k.bu2_parts[:, :], 0.0).then_inc(bias_v, 1)
                vec.memset(k.brel_parts[:, :], 0.0).then_inc(bias_v, 1)
                vec.memset(k.eps_col[:, :], D * D * LN_EPS)
                vec.wait_ge(consts, 3)
                vec.tensor_copy(k.relcol[:, :], rel_iota[:, :]).then_inc(idx_ready, 1)
                vec.wait_ge(idx_ready, 1)
                vec.tensor_scalar(k.relcol[D:P, :], k.relcol[D:P, :], 1.0, None, ALU.add).then_inc(idx_ready, 1)
                vec.wait_ge(bias_in, 32)
                for n in range(3):
                    vec.wait_ge(bias_v, 2 + 4 * n)
                    vec.tensor_copy(bias_part[:, :, :], bias_left[:, :, :]).then_inc(bias_v, 1)
                    vec.wait_ge(bias_v, 3 + 4 * n)
                    row = slice(32 * n, 32 * n + 1)
                    vec.tensor_copy(k.bu2_parts[row, :], bias_part[row, 0, :]).then_inc(bias_v, 1)
                    vec.tensor_copy(k.brel_parts[row, :], bias_part[row, 1, :]).then_inc(bias_v, 1)
                    vec.tensor_tensor(bias_left[:, :, :], bias_left[:, :, :], bias_part[:, :, :], ALU.subtract).then_inc(bias_v, 1)
                vec.wait_ge(order_in, 32)
                vec.tensor_copy(cur[:, :, :], cur_i[:, :, :]).then_inc(order_v, 1)
                vec.tensor_copy(prev[:, :, :], prev_i[:, :, :]).then_inc(order_v, 1)
                vec.wait_ge(order_v, 3)
                vec.tensor_tensor(falls[:, :].rearrange("q (a f) -> q a f", a=2), prev[:, :, :], cur[:, :, :],
                                  ALU.is_gt).then_inc(order_v, 1)
                vec.wait_ge(order_v, 4)
                vec.tensor_reduce(falls_sum[:, :], falls[:, :], AX.X, ALU.add).then_inc(order_v, 1)
                vec.wait_ge(falls_added, 1)
                vec.tensor_copy(flag[:, :], k.bank[4][0:1, 0:1]).then_inc(flag_ready, 1)
                vec.wait_ge(flag_ready, 1)
                unsorted = vec.value_load(flag[0:1, 0:1], min_val=0, max_val=SLOTS)
                with vec.If(unsorted > 0):
                    vec.wait_ge(wide_in, 16)
                    vec.wait_ge(consts, 5)
                    vec.tensor_scalar(wide, wide.bitcast(I32), 0.5, None, ALU.add).then_inc(wide_v, 1)
                    vec.wait_ge(wide_v, 1)
                    with vec.Fori(0, ET) as t:
                        vec.wait_ge(tile_in, (t + 1) * 64)
                        base = t * STEPS
                        vec.tensor_copy(tile_dst[:, :], tile_dst_i[:, :]).then_inc(rank_v, 1)
                        vec.wait_ge(rank_v, base + 1)
                        vec.tensor_scalar(tile_half[:, :], tile_dst[:, :], 0.5, None, ALU.add).then_inc(rank_v, 1)
                        for c in range(SLOTS // COUNT_CHUNK):
                            if c:
                                vec.wait_ge(rank_v, base + 2 + 2 * c)
                            vec.tensor_scalar(junk, wide[:, c * COUNT_CHUNK:(c + 1) * COUNT_CHUNK],
                                              tile_dst[:, 0:1], None, ALU.is_le).then_inc(rank_v, 1)
                            vec.wait_ge(rank_v, base + 3 + 2 * c)
                            vec.tensor_reduce(counts[:, c:c + 1], junk, AX.X, ALU.add).then_inc(rank_v, 1)
                        n = 2 + 2 * (SLOTS // COUNT_CHUNK)
                        vec.wait_ge(rank_v, base + n)
                        vec.scalar_tensor_tensor(out=own[:, :], in0=wide[:, bass.ds(t * P, P)], scalar=tile_half[:, 0:1],
                                                 in1=tri[:, :], op0=ALU.is_equal, op1=ALU.mult).then_inc(rank_v, 1)
                        vec.wait_ge(rank_v, base + n + 1)
                        vec.tensor_reduce(counts[:, SLOTS // COUNT_CHUNK:], own[:, :], AX.X, ALU.add).then_inc(rank_v, 1)
                        vec.tensor_scalar(wide[:, bass.ds(t * P, P)], wide[:, bass.ds(t * P, P)], -0.5, None,
                                          ALU.add).then_inc(rank_v, 1)
                        vec.wait_ge(rank_v, base + n + 3)
                        vec.tensor_reduce(rank[:, :], counts[:, :], AX.X, ALU.add).then_inc(rank_v, 1)
                        vec.wait_ge(rank_v, base + n + 4)
                        vec.tensor_copy(rank_i[:, :], rank[:, :]).then_inc(rank_v, 1)
                vec.wait_ge(arrays_in, 5 * 16)
                vec.tensor_copy(cur[:, :, :], cur_i[:, :, :]).then_inc(arrays_v, 1)
                vec.tensor_copy(prev[:, :, :], prev_i[:, :, :]).then_inc(arrays_v, 1)
                vec.tensor_copy(nxt[:, :, :], next_i[:, :, :]).then_inc(arrays_v, 1)
                vec.tensor_copy(srcf[:, :, :], src_i[:, :, :]).then_inc(arrays_v, 1)
                vec.tensor_copy(typf[:, :, :], typ_i[:, :, :]).then_inc(arrays_v, 1)
                vec.wait_ge(arrays_v, 5)
                vec.tensor_tensor(same_t[:, :, :], cur[:, :, :], prev[:, :, :], ALU.is_equal).then_inc(arrays_v, 1)
                vec.tensor_tensor(nxt[:, :, :], cur[:, :, :], nxt[:, :, :], ALU.is_equal).then_inc(arrays_v, 1)
                vec.tensor_scalar(gath[:, :, :], cur[:, :, :], float(NODES - 1), None, ALU.min).then_inc(arrays_v, 1)
                vec.tensor_scalar(src_in[:, :, :], srcf[:, :, :], float(NODES - 1), None, ALU.min).then_inc(arrays_v, 1)
                vec.wait_ge(arrays_v, 9)
                vec.scalar_tensor_tensor(out=scat[:, :, :], in0=nxt[:, :, :], scalar=float(FAR), in1=cur[:, :, :],
                                         op0=ALU.mult, op1=ALU.add).then_inc(arrays_v, 1)
                vec.wait_ge(turned, 8)
                for n, a in enumerate((k.src_idx, k.dst_idx, k.last_idx)):
                    vec.tensor_copy(a[:, :], k.bank[5 + n][:, 0:ET]).then_inc(idx_ready, 1)
                vec.tensor_copy(k.src_key[:, :], k.bank[5][:, ET:2 * ET]).then_inc(idx_ready, 1)
                vec.wait_ge(idx_ready, 6)
                vec.wait_ge(bias_v, 14)


def stage_index(pool, copied, g, ring, idx):
    pool.tensor_copy(ring[:, g.buf, :], idx[:, bass.ds(g.n * TG, TG)]).then_inc(copied, 1)


def gather_rows(pool, to, table, index):
    return pool.indirect_dma_start(to, None, table[:, :], bass.IndirectOffsetOnAxis(ap=index, axis=0))


def scatter_rows(pool, table, frm, index, **how):
    return pool.indirect_dma_start(table[:, :], bass.IndirectOffsetOnAxis(ap=index, axis=0), frm, None,
                                   bounds_check=NODES - 1, oob_is_err=False, **how)


def gather_group(pool, g, reads, copied, gathered, settled):
    if g.from_second():
        pool.wait_ge(gathered[g.buf], g.half * (len(reads) * TG * 16))
    pool.sem_inc(settled, 1)
    for to, table, idx, ring in reads:
        stage_index(pool, copied, g, ring, idx)
    pool.wait_ge(copied, (g.n + 1) * len(reads))
    pool.sem_inc(settled, 1)
    for t in range(TG):
        for to, table, idx, ring in reads:
            gather_rows(pool, to[:, t], table, ring[:, g.buf, t:t + 1]).then_inc(gathered[g.buf], 16)


def scatter_group(pool, g, rows, ready, count, table, idx, ring, copied, scattered, settled, **how):
    if g.from_second():
        pool.wait_ge(scattered[g.buf], g.half * (TG * 16))
    pool.sem_inc(settled, 1)
    stage_index(pool, copied, g, ring, idx)
    pool.wait_ge(copied, g.n + 1)
    pool.wait_ge(ready, count)
    pool.sem_inc(settled, 1)
    for t in range(TG):
        scatter_rows(pool, table, rows[:, g.buf, t, :], ring[:, g.buf, t:t + 1], **how).then_inc(scattered[g.buf], 16)


def dense(nc, k):
    with ExitStack() as ctx:
        def two(name, shape, dt=F32):
            return k.sb(name, [shape[0], 2] + shape[1:], dt, ctx)

        def sem(name):
            return k.sem(name, ctx)

        rows = two("rows", [NP, NG, D])
        cen0 = two("cen0", [NP, NG, D])
        res0 = two("res0", [NP, NG, D])
        cen1 = two("cen1", [NP, NG, D])
        res1 = two("res1", [NP, NG, D])
        res2 = two("res2", [NP, NG, D])
        squares = k.sb("squares", [NP, 2, NG, D], F32, ctx)
        sums = k.sb("sums", [NP, 2, NG], F32, ctx)
        roots = k.sb("roots", [NP, 2, NG], F32, ctx)
        inverse = k.sb("inverse", [NP, 2, NG], F32, ctx)
        h0t = k.sb("h0t", [P, HALF], F32, ctx)
        h1t = k.sb("h1t", [P, HALF], F32, ctx)
        ut = k.sb("ut", [H, 2, HALF], F32, ctx)
        src_ring = k.sb("src_ring", [P, 2, TG], I32, ctx)
        dst_ring = k.sb("dst_ring", [P, 2, TG], I32, ctx)
        xs_ring = k.sb("xs_ring", [P, 2, TG, D], F32, ctx)
        xd_ring = k.sb("xd_ring", [P, 2, TG, D], F32, ctx)

        x_in = k.pair_of_sems("x_in", ctx)
        ln0, ln1, added2 = sem("ln0"), sem("ln1"), sem("added2")
        sq0_done, sq1_done = sem("sq0_done"), sem("sq1_done")
        rooted0, inverted0, rooted1, inverted1 = sem("rooted0"), sem("inverted0"), sem("rooted1"), sem("inverted1")
        t0_done, t1_done = sem("t0_done"), sem("t1_done")
        h0t_done, h1t_done = sem("h0t_done"), sem("h1t_done")
        u1_done, ut_done, u2_done = sem("u1_done"), sem("ut_done"), sem("u2_done")
        self_done = sem("self_done")
        x1_out = k.pair_of_sems("x1_out", ctx)
        x2_out = k.pair_of_sems("x2_out", ctx)
        gathered = k.pair_of_sems("gathered", ctx)
        kept = k.pair_of_sems("kept", ctx)
        idx_copied = sem("idx_copied")

        def nodes(a, g):
            return a.rearrange("(p j) d -> p j d", p=NP)[:, bass.ds(g.n * NG, NG), :]

        with nc.Block() as block:
            @block.sync
            def _(sp):

                def step(r):
                    g = r
                    if g.within(DG):
                        if g.from_second():
                            sp.wait_ge(ln0, (g - 2).n * 5 + 5)
                        sp.dma_start(rows[:, g.buf], nodes(k.x, g)).then_inc(x_in[g.buf], 16)
                    g = r - 2
                    if g.within(EG):
                        sp.wait_ge(gathered[g.buf], (g.half + 1) * (2 * TG * 16))
                        sp.dma_start(k.x_src[:, bass.ds(g.n * TG, TG), :], xs_ring[:, g.buf]).then_inc(kept[g.buf], 16)
                        sp.dma_start(k.x_dst[:, bass.ds(g.n * TG, TG), :], xd_ring[:, g.buf]).then_inc(kept[g.buf], 16)
                    g = r - 3
                    if g.within(DG):
                        sp.wait_ge(ln1, g.n * 5 + 1)
                        sp.dma_start(nodes(k.x1_table, g), res1[:, g.buf]).then_inc(x1_out[g.buf], 16)
                    g = r - 5
                    if g.within(DG):
                        sp.wait_ge(added2, g.n + 1)
                        sp.dma_start(nodes(k.x2_table, g), res2[:, g.buf]).then_inc(x2_out[g.buf], 16)

                rounds(sp, DG, 5, step)
                for b in range(2):
                    sp.wait_ge(x1_out[b], (DG + 1 - b) // 2 * 16)
                    sp.wait_ge(x2_out[b], (DG + 1 - b) // 2 * 16)
                    sp.wait_ge(kept[b], (EG + 1 - b) // 2 * 32)

            @block.gpsimd
            def _(pool):
                stage_index(pool, idx_copied, Group(0, 0), src_ring, k.src_idx)
                stage_index(pool, idx_copied, Group(0, 0), dst_ring, k.dst_idx)

                def gather(r, j):
                    for ring, index in ((xs_ring, src_ring), (xd_ring, dst_ring)):
                        gather_rows(pool, ring[:, r.buf, j, :], k.x, index[:, r.buf, j:j + 1]).then_inc(gathered[r.buf], 16)

                def step(r):
                    if r.from_second():
                        pool.wait_ge(kept[r.buf], r.half * 32)
                    pool.wait_ge(idx_copied, r.n * 2 + 2)
                    pool.sem_inc(k.pool_wait, 1)
                    gather(r, 0)
                    gather(r, 1)
                    if (r + 1).within(EG):
                        if r.from_first():
                            pool.wait_ge(gathered[(r + 1).buf], (r + 1).half * (2 * TG * 16))
                            pool.sem_inc(k.pool_wait, 1)
                        stage_index(pool, idx_copied, r + 1, src_ring, k.src_idx)
                        stage_index(pool, idx_copied, r + 1, dst_ring, k.dst_idx)
                    gather(r, 2)
                    gather(r, 3)

                rounds(pool, EG, 0, step)

            @block.vector
            def _(vec):
                def step(r):
                    g0, g1, g2 = r, r - 2, r - 4
                    n0, n1 = g0.n * 5, g1.n * 5
                    first, second = g0.within(DG), g1.within(DG)
                    if first:
                        vec.wait_ge(x_in[g0.buf], (g0.half + 1) * 16)
                        vec.tensor_reduce(sums[:, 0, :], rows[:, g0.buf], AX.X, ALU.add).then_inc(ln0, 1)
                    if g2.within(DG):
                        vec.wait_ge(self_done, g2.n + 1)
                        if g2.from_second():
                            vec.wait_ge(x2_out[g2.buf], g2.half * 16)
                        vec.tensor_tensor(res2[:, g2.buf], res1[:, g2.buf],
                                          k.bank[7][0:NP, :].rearrange("p (j d) -> p j d", d=D), ALU.add).then_inc(added2, 1)
                    if first:
                        vec.wait_ge(ln0, n0 + 1)
                        if g0.from_second():
                            vec.wait_ge(t0_done, (g0 - 2).n + 1)
                        vec.scalar_tensor_tensor(out=cen0[:, g0.buf], in0=rows[:, g0.buf], scalar=float(D),
                                                 in1=sums[:, 0, :].unsqueeze(2).to_broadcast([NP, NG, D]),
                                                 op0=ALU.mult, op1=ALU.subtract).then_inc(ln0, 1)
                    if second:
                        vec.wait_ge(u2_done, g1.n + 1)
                        if g1.from_second():
                            vec.wait_ge(x1_out[g1.buf], g1.half * 16)
                            vec.wait_ge(added2, (g1 - 2).n + 1)
                        vec.tensor_tensor(res1[:, g1.buf], res0[:, g1.buf],
                                          k.bank[6][0:NP, :].rearrange("p (j d) -> p j d", d=D), ALU.add).then_inc(ln1, 1)
                        vec.wait_ge(ln1, n1 + 1)
                        vec.tensor_reduce(sums[:, 1, :], res1[:, g1.buf], AX.X, ALU.add).then_inc(ln1, 1)
                    if first:
                        vec.wait_ge(sq0_done, g0.n + 1)
                        vec.tensor_reduce(roots[:, 0, :], squares[:, 0], AX.X, ALU.add).then_inc(ln0, 1)
                    if second:
                        vec.wait_ge(ln1, n1 + 2)
                        if g1.from_second():
                            vec.wait_ge(t1_done, (g1 - 2).n + 1)
                        vec.scalar_tensor_tensor(out=cen1[:, g1.buf], in0=res1[:, g1.buf], scalar=float(D),
                                                 in1=sums[:, 1, :].unsqueeze(2).to_broadcast([NP, NG, D]),
                                                 op0=ALU.mult, op1=ALU.subtract).then_inc(ln1, 1)
                    if first:
                        vec.wait_ge(rooted0, g0.n + 1)
                        vec.reciprocal(inverse[:, 0, :], roots[:, 0, :]).then_inc(inverted0, 1)
                        vec.wait_ge(inverted0, g0.n + 1)
                        scale_rows(vec, ln0, cen0[:, g0.buf], inverse[:, 0, :], cen0[:, g0.buf])
                    if second:
                        vec.wait_ge(sq1_done, g1.n + 1)
                        vec.tensor_reduce(roots[:, 1, :], squares[:, 1], AX.X, ALU.add).then_inc(ln1, 1)
                    if first:
                        vec.wait_ge(ln0, n0 + 4)
                        vec.tensor_tensor(res0[:, g0.buf], rows[:, g0.buf], cen0[:, g0.buf], ALU.add).then_inc(ln0, 1)
                    if second:
                        vec.wait_ge(rooted1, g1.n + 1)
                        vec.reciprocal(inverse[:, 1, :], roots[:, 1, :]).then_inc(inverted1, 1)
                        vec.wait_ge(inverted1, g1.n + 1)
                        scale_rows(vec, ln1, cen1[:, g1.buf], inverse[:, 1, :], cen1[:, g1.buf])

                rounds(vec, DG, 4, step)

            @block.scalar
            def _(act):
                def step(r):
                    g = r - 1
                    if g.within(DG):
                        act.wait_ge(t0_done, g.n + 1)
                        if g.from_first():
                            act.wait_ge(u1_done, g.n * 2)
                        act.activation(h0t[:, :], k.bank[0][:, 0:HALF], ACT.Copy).then_inc(h0t_done, 1)
                    g = r - 3
                    if g.within(DG):
                        act.wait_ge(t1_done, g.n + 1)
                        if g.from_first():
                            act.wait_ge(self_done, g.n)
                        act.activation(h1t[:, :], k.bank[2][:, 0:HALF], ACT.Copy).then_inc(h1t_done, 1)
                    def relu(g, c):
                        if g.within(DG):
                            act.wait_ge(u1_done, g.n * 2 + c + 1)
                            if g.from_first():
                                act.wait_ge(u2_done, g.n)
                            act.activation(ut[:, c, :], k.bank[4 + c][:, 0:HALF], ACT.Relu, bias=k.bu1[:, 0:1]).then_inc(ut_done, 1)

                    g = r
                    if g.within(DG):
                        act.wait_ge(ln0, g.n * 5 + 2)
                        act.activation(squares[:, 0], cen0[:, g.buf], ACT.Square, scale=0.125).then_inc(sq0_done, 1)
                        act.wait_ge(ln0, g.n * 5 + 3)
                        act.activation(roots[:, 0, :], roots[:, 0, :], ACT.Sqrt, bias=k.eps_col[0:NP, 0:1]).then_inc(rooted0, 1)
                    relu(r - 1, 0)
                    g = r - 2
                    if g.within(DG):
                        act.wait_ge(ln1, g.n * 5 + 3)
                        act.activation(squares[:, 1], cen1[:, g.buf], ACT.Square, scale=0.125).then_inc(sq1_done, 1)
                    relu(r - 1, 1)
                    if g.within(DG):
                        act.wait_ge(ln1, g.n * 5 + 4)
                        act.activation(roots[:, 1, :], roots[:, 1, :], ACT.Sqrt, bias=k.eps_col[0:NP, 0:1]).then_inc(rooted1, 1)

                rounds(act, DG, 4, step)

            @block.tensor
            def _(pe):
                def turn(g, rows_in, to, done):
                    for j in range(NG // 2):
                        mm = pe.transpose(k.bank[to][:, j * NP:(j + 1) * NP],
                                          rows_in[:, g.buf, 2 * j:2 * j + 2, :].rearrange("p j d -> p (j d)"),
                                          k.ident[0:NP, 0:NP])
                    mm.then_inc(done, 1)

                def bias_first(to, bias):
                    pe.matmul(k.bank[to][0:NP, :], k.ones[:, 0:NP], bias.unsqueeze(1).to_broadcast([BIAS_ROWS, NG, D]),
                              start=True, stop=True, skip_group_check=True)

                def step(r):
                    g = r - 1
                    if g.within(DG):
                        pe.wait_ge(ln0, g.n * 5 + 4)
                        if g.from_first():
                            pe.wait_ge(h0t_done, g.n)
                        pe.sem_inc(k.pe_wait, 1)
                        turn(g, cen0, 0, t0_done)
                    g = r - 3
                    if g.within(DG):
                        pe.wait_ge(ln1, g.n * 5 + 5)
                        if g.from_first():
                            pe.wait_ge(h1t_done, g.n)
                        pe.sem_inc(k.pe_wait, 1)
                        turn(g, cen1, 2, t1_done)
                    g = r - 1
                    if g.within(DG):
                        pe.wait_ge(h0t_done, g.n + 1)
                        for c in range(2):
                            if g.from_first():
                                pe.wait_ge(ut_done, g.n * 2 + c - 1)
                            pe.matmul(k.bank[4 + c][:, 0:HALF], k.wu1x[c * D:(c + 1) * D, :], h0t[c * D:(c + 1) * D, :],
                                      start=True, stop=True).then_inc(u1_done, 1)
                    g = r - 3
                    if g.within(DG):
                        pe.wait_ge(h1t_done, g.n + 1)
                        if g.from_first():
                            pe.wait_ge(added2, g.n)
                        bias_first(7, k.brel_parts[:, :])
                        for j in range(NG // 2):
                            mm = pe.matmul(k.bank[7][0:NP, j * P:(j + 1) * P], h1t[:, j * NP:(j + 1) * NP], k.wself[:, :],
                                           start=False, stop=True, skip_group_check=True)
                        mm.then_inc(self_done, 1)
                    g = r - 1
                    if g.within(DG):
                        pe.wait_ge(ut_done, g.n * 2 + 2)
                        if g.from_first():
                            pe.wait_ge(ln1, g.n * 5 - 4)
                        bias_first(6, k.bu2_parts[:, :])
                        for j in range(NG):
                            at = j // 2 * NP
                            mm = pe.matmul(k.bank[6][0:NP, j * D:(j + 1) * D], ut[:, j % 2, at:at + NP], k.wu2[:, :],
                                           start=False, stop=True, skip_group_check=True)
                        mm.then_inc(u2_done, 1)

                rounds(pe, DG, 4, step)


def layer0(nc, k):
    with ExitStack() as ctx:
        def sb(name, shape, dt=F32):
            return k.sb(name, shape, dt, ctx)

        def sem(name):
            return k.sem(name, ctx)

        attr = sb("l0_attr", [P, 2, TG, ED])
        cen = sb("l0_cen", [P, 2, TG, 2, D])
        squares = sb("l0_squares", [P, 3 * TG * D])
        sq_in = squares[:, 0:2 * TG * D]
        sq_up = squares[:, 2 * TG * D:]
        stats = sb("l0_stats", [P, 3 * TG])
        roots = sb("l0_roots", [P, 3 * TG])
        inverse = sb("l0_inverse", [P, 3 * TG])
        ht = sb("l0_ht", [P, 2, GS])
        at = sb("l0_at", [ED, 2, GS])
        hid = sb("l0_hid", [H, GS])
        msg = sb("l0_msg", [H, 2, GS])
        agg = sb("l0_agg", [H, 2, GS])
        ut = sb("l0_ut", [H, GS])
        x1 = sb("l0_x1", [P, 2, TG, D])
        h1 = sb("l0_h1", [P, 2, TG, D])
        h1t = sb("l0_h1t", [P, GS // 2])
        last_ring = sb("l0_last_ring", [P, 2, TG], I32)
        zeros = sb("l0_zeros", [P, CLEAR, D + 1])

        attr_in = k.pair_of_sems("l0_attr_in", ctx)
        ln0, ln1 = sem("l0_ln0"), sem("l0_ln1")
        sq_in_done, sq_up_done = sem("l0_sq_in_done"), sem("l0_sq_up_done")
        rooted0, inverted0, rooted1, inverted1 = (sem("l0_" + n) for n in ("rooted0", "inverted0", "rooted1", "inverted1"))
        turned, ht_done, at_done = sem("l0_turned"), sem("l0_ht_done"), sem("l0_at_done")
        m1_done, hid_done, m2_done, msg_done = sem("l0_m1"), sem("l0_hid_done"), sem("l0_m2"), sem("l0_msg_done")
        scanned = sem("l0_scanned")
        u1_done, ut_done, u2_done = sem("l0_u1"), sem("l0_ut_done"), sem("l0_u2")
        h1_turned, h1t_done, self_done = sem("l0_h1_turned"), sem("l0_h1t_done"), sem("l0_self")
        self_added = sem("l0_self_added")
        idx_copied = sem("l0_idx_copied")
        scattered = k.pair_of_sems("l0_scattered", ctx)
        zeroed, cleared = sem("l0_zeroed"), sem("l0_cleared")

        def x_dst(g):
            return k.x_dst[:, bass.ds(g.n * TG, TG), :]

        def x_src(g):
            return k.x_src[:, bass.ds(g.n * TG, TG), :]

        with nc.Block() as block:
            @block.sync
            def _(sp):
                def step(r):
                    if r.from_second():
                        sp.wait_ge(turned, (r - 2).n + 1)
                    sp.dma_start(attr[:, r.buf], k.attr_s[bass.ds(r.n * GS, GS), :].rearrange("(t p) c -> p t c", p=P)
                                 ).then_inc(attr_in[r.buf], 16)
                    sp.dma_start(k.sum_table[bass.ds(r.n * (P * CLEAR), P * CLEAR), :].rearrange("(p c) d -> p c d", p=P),
                                 zeros[:, :, :]).then_inc(cleared, 16)

                sp.wait_ge(zeroed, 1)
                rounds(sp, EG, 0, step)
                sp.wait_ge(cleared, EG * 16)

            @block.gpsimd
            def _(pool):
                def step(g):
                    scatter_group(pool, g, x1, ln1, g.n * 5 + 1, k.x1_table, k.last_idx, last_ring,
                                  idx_copied, scattered, k.pool_wait)

                rounds(pool, EG, 0, step)
                for b in range(2):
                    pool.wait_ge(scattered[b], (EG + 1 - b) // 2 * TG * 16)

            @block.vector
            def _(vec):
                vec.memset(zeros[:, :, :], 0.0).then_inc(zeroed, 1)

                def step(r):
                    g0, g1 = r, r - 3
                    n0, n1 = g0.n * 7, g1.n * 5
                    first, second = g0.within(EG), g1.within(EG)
                    if first:
                        flat = cen[:, g0.buf]
                        sides = (0, x_src(g0)), (1, x_dst(g0))
                        for side, x in sides:
                            vec.tensor_reduce(stats[:, side * TG:side * TG + TG], x, AX.X, ALU.add).then_inc(ln0, 1)
                    g = r - 2
                    if g.within(EG):
                        vec.wait_ge(msg_done, g.n + 1)
                        if g.from_second():
                            vec.wait_ge(u1_done, (g - 2).n + 1)
                        if g.from_first():
                            vec.wait_ge(scanned, g.n)
                        vec.tensor_tensor_scan(agg[:, g.buf, :], k.same[:, bass.ds(g.n * GS, GS)], msg[:, g.buf, :],
                                               agg[:, (g - 1).buf, GS - 1:GS] if g.from_first() else 0.0,
                                               ALU.mult, ALU.add).then_inc(scanned, 1)
                    if first:
                        if g0.from_second():
                            vec.wait_ge(turned, (g0 - 2).n + 1)
                        for side, x in sides:
                            vec.wait_ge(ln0, n0 + 1 + side)
                            vec.scalar_tensor_tensor(
                                out=flat[:, :, side, :], in0=x, scalar=float(D),
                                in1=stats[:, side * TG:side * TG + TG].unsqueeze(2).to_broadcast([P, TG, D]),
                                op0=ALU.mult, op1=ALU.subtract).then_inc(ln0, 1)
                    g = r - 5
                    if g.within(EG):
                        vec.wait_ge(self_done, g.n + 1)
                        vec.tensor_tensor(x_dst(g), x1[:, g.buf], k.bank[7][:, 0:TG * D].rearrange("p (t d) -> p t d", d=D),
                                          ALU.add).then_inc(self_added, 1)
                    if second:
                        vec.wait_ge(u2_done, g1.n + 1)
                        if g1.from_second():
                            vec.wait_ge(scattered[g1.buf], g1.half * (TG * 16))
                            vec.wait_ge(self_added, (g1 - 2).n + 1)
                        vec.tensor_tensor(x1[:, g1.buf], x_dst(g1), k.bank[5][:, 0:TG * D].rearrange("p (t d) -> p t d", d=D),
                                          ALU.add).then_inc(ln1, 1)
                    if first:
                        vec.wait_ge(sq_in_done, g0.n + 1)
                        vec.tensor_reduce(roots[:, 0:2 * TG], sq_in.rearrange("p (t d) -> p t d", d=D), AX.X, ALU.add).then_inc(ln0, 1)
                    if second:
                        vec.wait_ge(ln1, n1 + 1)
                        vec.tensor_reduce(stats[:, 2 * TG:], x1[:, g1.buf], AX.X, ALU.add).then_inc(ln1, 1)
                        vec.wait_ge(ln1, n1 + 2)
                        if g1.from_second():
                            vec.wait_ge(h1_turned, (g1 - 2).n + 1)
                        vec.scalar_tensor_tensor(out=h1[:, g1.buf], in0=x1[:, g1.buf], scalar=float(D),
                                                 in1=stats[:, 2 * TG:].unsqueeze(2).to_broadcast([P, TG, D]),
                                                 op0=ALU.mult, op1=ALU.subtract).then_inc(ln1, 1)
                    if first:
                        vec.wait_ge(rooted0, g0.n + 1)
                        vec.reciprocal(inverse[:, 0:2 * TG], roots[:, 0:2 * TG]).then_inc(inverted0, 1)
                        vec.wait_ge(inverted0, g0.n + 1)
                        rows = flat.rearrange("p t s d -> p (t s) d")
                        scale_rows(vec, ln0, rows, inverse[:, 0:2 * TG], rows)
                    if second:
                        vec.wait_ge(sq_up_done, g1.n + 1)
                        vec.tensor_reduce(roots[:, 2 * TG:], sq_up.rearrange("p (t d) -> p t d", d=D), AX.X, ALU.add).then_inc(ln1, 1)
                    if first:
                        vec.wait_ge(ln0, n0 + 6)
                        vec.tensor_tensor(x_dst(g0), x_dst(g0), cen[:, g0.buf, :, 1, :], ALU.add).then_inc(ln0, 1)
                    if second:
                        vec.wait_ge(rooted1, g1.n + 1)
                        vec.reciprocal(inverse[:, 2 * TG:], roots[:, 2 * TG:]).then_inc(inverted1, 1)
                        vec.wait_ge(inverted1, g1.n + 1)
                        scale_rows(vec, ln1, h1[:, g1.buf], inverse[:, 2 * TG:], h1[:, g1.buf])

                rounds(vec, EG, 5, step)

            @block.scalar
            def _(act):
                def step(r):
                    g = r - 1
                    if g.within(EG):
                        act.wait_ge(turned, g.n + 1)
                        if g.from_second():
                            act.wait_ge(u1_done, (g - 2).n + 1)
                        act.activation(ht[:, g.buf, :], k.bank[0][:, :], ACT.Copy).then_inc(ht_done, 1)
                        act.activation(at[:, g.buf, :], k.bank[1][0:ED, :], ACT.Copy).then_inc(at_done, 1)
                    g = r - 4
                    if g.within(EG):
                        act.wait_ge(h1_turned, g.n + 1)
                        if g.from_first():
                            act.wait_ge(self_done, g.n)
                        act.activation(h1t[:, :], k.bank[6][:, 0:GS // 2], ACT.Copy).then_inc(h1t_done, 1)
                    g = r
                    if g.within(EG):
                        act.wait_ge(ln0, g.n * 7 + 4)
                        act.activation(sq_in.rearrange("p (t d) -> p t d", d=D), cen[:, g.buf].rearrange("p t s d -> p (t s) d"),
                                       ACT.Square, scale=0.125).then_inc(sq_in_done, 1)
                    g = r - 2
                    if g.within(EG):
                        act.wait_ge(u1_done, g.n + 1)
                        if g.from_first():
                            act.wait_ge(u2_done, g.n)
                        act.activation(ut[:, :], k.bank[4][:, :], ACT.Relu, bias=k.bu1[:, 0:1]).then_inc(ut_done, 1)
                    if r.within(EG):
                        act.wait_ge(ln0, r.n * 7 + 5)
                        act.activation(roots[:, 0:2 * TG], roots[:, 0:2 * TG], ACT.Sqrt, bias=k.eps_col[:, 0:1]).then_inc(rooted0, 1)
                    g = r - 3
                    if g.within(EG):
                        act.wait_ge(ln1, g.n * 5 + 3)
                        act.activation(sq_up.rearrange("p (t d) -> p t d", d=D), h1[:, g.buf], ACT.Square, scale=0.125
                                       ).then_inc(sq_up_done, 1)
                    g = r - 1
                    if g.within(EG):
                        act.wait_ge(m1_done, g.n + 1)
                        if g.from_first():
                            act.wait_ge(m2_done, g.n)
                        act.activation(hid[:, :], k.bank[2][:, :], ACT.Relu, bias=k.bm1[:, 0:1]).then_inc(hid_done, 1)
                    g = r - 3
                    if g.within(EG):
                        act.wait_ge(ln1, g.n * 5 + 4)
                        act.activation(roots[:, 2 * TG:], roots[:, 2 * TG:], ACT.Sqrt, bias=k.eps_col[:, 0:1]).then_inc(rooted1, 1)
                    g = r - 1
                    if g.within(EG):
                        act.wait_ge(m2_done, g.n + 1)
                        if g.from_second():
                            act.wait_ge(scanned, (g - 2).n + 1)
                        act.activation(msg[:, g.buf, :], k.bank[3][:, :], ACT.Identity, bias=k.bm2[:, 0:1]).then_inc(msg_done, 1)

                rounds(act, EG, 4, step)

            @block.tensor
            def _(pe):
                def rows_times(to, cols, weights, bias, done):
                    pe.matmul(k.bank[to][:, 0:TG * D], k.ones[:, :], bias[:, :].unsqueeze(1).to_broadcast([BIAS_ROWS, TG, D]),
                              start=True, stop=True, skip_group_check=True)
                    width = weights.shape[-1]
                    for t in range(TG * D // width):
                        mm = pe.matmul(k.bank[to][:, t * width:(t + 1) * width], cols[:, t * P:(t + 1) * P], weights,
                                       start=False, stop=True, skip_group_check=True)
                    mm.then_inc(done, 1)

                def step(r):
                    g = r - 1
                    if g.within(EG):
                        pe.wait_ge(ln0, g.n * 7 + 6)
                        pe.wait_ge(attr_in[g.buf], (g.half + 1) * 16)
                        if g.from_first():
                            pe.wait_ge(at_done, g.n)
                        pe.sem_inc(k.pe_wait, 1)
                        for t in range(TG):
                            pe.transpose(k.bank[0][:, t * P:(t + 1) * P], cen[:, g.buf, t].rearrange("p s d -> p (s d)"), k.ident[:, :])
                        for t in range(TG):
                            mm = pe.transpose(k.bank[1][0:ED, t * P:(t + 1) * P], attr[:, g.buf, t, :], k.ident[:, :])
                        mm.then_inc(turned, 1)
                    g = r - 4
                    if g.within(EG):
                        pe.wait_ge(ln1, g.n * 5 + 5)
                        if g.from_first():
                            pe.wait_ge(h1t_done, g.n)
                        pe.sem_inc(k.pe_wait, 1)
                        for t in range(TG // 2):
                            mm = pe.transpose(k.bank[6][:, t * P:(t + 1) * P],
                                              h1[:, g.buf, 2 * t:2 * t + 2, :].rearrange("p t d -> p (t d)"), k.ident[:, :])
                        mm.then_inc(h1_turned, 1)
                    g = r - 2
                    if g.within(EG):
                        pe.wait_ge(scanned, g.n + 1)
                        if g.from_first():
                            pe.wait_ge(ut_done, g.n)
                        pe.matmul(k.bank[4][:, :], k.wu1a[:, :], agg[:, g.buf, :], start=True, stop=False)
                        pe.matmul(k.bank[4][:, :], k.wu1x[D:P, :], ht[D:P, g.buf, :], start=False, stop=True).then_inc(u1_done, 1)
                    g = r - 1
                    if g.within(EG):
                        pe.wait_ge(at_done, g.n + 1)
                        if g.from_first():
                            pe.wait_ge(hid_done, g.n)
                        pe.matmul(k.bank[2][:, :], k.wm1[:, :], ht[:, g.buf, :], start=True, stop=False)
                        pe.matmul(k.bank[2][:, :], k.wm1e[:, :], at[:, g.buf, :], start=False, stop=True).then_inc(m1_done, 1)
                    g = r - 4
                    if g.within(EG):
                        pe.wait_ge(h1t_done, g.n + 1)
                        if g.from_first():
                            pe.wait_ge(self_added, g.n)
                        pe.sem_inc(k.pe_wait, 1)
                        rows_times(7, h1t, k.wself[:, :], k.brel_parts, self_done)
                    g = r - 1
                    if g.within(EG):
                        pe.wait_ge(hid_done, g.n + 1)
                        if g.from_first():
                            pe.wait_ge(msg_done, g.n)
                        pe.matmul(k.bank[3][:, :], k.wm2[:, :], hid[:, :], start=True, stop=True).then_inc(m2_done, 1)
                    g = r - 2
                    if g.within(EG):
                        pe.wait_ge(ut_done, g.n + 1)
                        if g.from_first():
                            pe.wait_ge(ln1, g.n * 5 - 4)
                        pe.sem_inc(k.pe_wait, 1)
                        rows_times(5, ut, k.wu2[:, :], k.bu2_parts, u2_done)

                rounds(pe, EG, 4, step)


def layer1(nc, k):
    with ExitStack() as ctx:
        def sb(name, shape, dt=F32):
            return k.sb(name, shape, dt, ctx)

        def sem(name):
            return k.sem(name, ctx)

        PAIRS = RELS // 2
        NZ = 8
        wrel = sb("l1_wrel", [P, PAIRS, D])
        types = sb("l1_types", [P, 2, GS])
        xs = sb("l1_xs", [P, 2, TG, D])
        cen = sb("l1_cen", [P, TG, D])
        h1 = sb("l1_h1", [P, 2, TG, 2, D])
        squares = sb("l1_squares", [P, TG, D])
        stats = sb("l1_stats", [P, TG])
        roots = sb("l1_roots", [P, TG])
        inverse = sb("l1_inverse", [P, TG])
        ht = sb("l1_ht", [P, 2, GS])
        z = sb("l1_z", [P, NZ, GS])
        msg = sb("l1_msg", [D + 1, 2, GS])
        agg = sb("l1_agg", [D + 1, 2, GS])
        deg = sb("l1_deg", [P, TG])
        part = sb("l1_part", [P, TG, D])
        x2 = sb("l1_x2", [P, 2, TG, D])
        src_ring = sb("l1_src_ring", [P, 2, TG], I32)
        last_ring = sb("l1_last_ring", [P, 2, TG], I32)

        wrel_in, types_in = sem("l1_wrel_in"), k.pair_of_sems("l1_types_in", ctx)
        gathered, scattered = k.pair_of_sems("l1_gathered", ctx), k.pair_of_sems("l1_scattered", ctx)
        ln, sq_done, rooted, inverted = sem("l1_ln"), sem("l1_sq_done"), sem("l1_rooted"), sem("l1_inverted")
        turned, ht_done = sem("l1_turned"), sem("l1_ht_done")
        z_made, z_used, msg_done = sem("l1_z_made"), sem("l1_z_used"), sem("l1_msg_done")
        ones_set, scanned, rows_done, updated = sem("l1_ones"), sem("l1_scanned"), sem("l1_rows"), sem("l1_updated")
        src_copied, last_copied = sem("l1_src_copied"), sem("l1_last_copied")

        with nc.Block() as block:
            @block.sync
            def _(sp):
                sp.dma_start(wrel[:, :, :], k.rel_rows[:, :].rearrange("(k r) (i o) -> (r i) k o", r=2, o=D)).then_inc(wrel_in, 16)

                def step(r):
                    if r.from_second():
                        sp.wait_ge(z_made, (r - 1).n * PAIRS)
                    sp.dma_start(types[:, r.buf, :], k.type_row[bass.ds(r.n * GS, GS)].partition_broadcast(P)
                                 ).then_inc(types_in[r.buf], 16)

                rounds(sp, EG, 0, step)

            @block.gpsimd
            def _(pool):
                def step(r):
                    g = r
                    if g.within(EG):
                        if g.from_second():
                            pool.wait_ge(ln, (g - 2).n * 5 + 2)
                        gather_group(pool, g, ((xs[:, g.buf], k.x1_table, k.src_idx, src_ring),),
                                     src_copied, gathered, k.pool_wait)
                    g = r - 4
                    if g.within(EG):
                        scatter_group(pool, g, x2, updated, g.n * 5 + 5, k.x2_table, k.last_idx, last_ring,
                                      last_copied, scattered, k.pool_wait)

                rounds(pool, EG, 4, step)
                for b in range(2):
                    pool.wait_ge(scattered[b], (EG + 1 - b) // 2 * TG * 16)

            @block.vector
            def _(vec):
                vec.memset(msg[D:D + 1, :, :], 1.0).then_inc(ones_set, 1)
                vec.wait_ge(ones_set, 1)

                def mask(g, first, count):
                    if not g.within(EG):
                        return
                    if first == 0:
                        vec.wait_ge(types_in[g.buf], (g.half + 1) * 16)
                        vec.wait_ge(ht_done, g.n + 1)
                    for n in range(first, first + count):
                        if g.from_first() or n >= NZ:
                            vec.wait_ge(z_used, g.n * PAIRS + n - NZ + 1)
                        vec.scalar_tensor_tensor(out=z[:, n % NZ, :], in0=types[:, g.buf, :], scalar=k.relcol[:, n:n + 1],
                                                 in1=ht[:, g.buf, :], op0=ALU.is_equal, op1=ALU.mult).then_inc(z_made, 1)

                def step(r):
                    now, done = r.within(EG), (r - 3).within(EG)
                    g = r
                    n = g.n * 5
                    if now:
                        vec.wait_ge(gathered[g.buf], (g.half + 1) * (TG * 16))
                        vec.tensor_reduce(stats[:, :], xs[:, g.buf], AX.X, ALU.add).then_inc(ln, 1)
                    mask(r - 1, 0, 1)
                    if now:
                        vec.wait_ge(ln, n + 1)
                        vec.scalar_tensor_tensor(out=cen[:, :, :], in0=xs[:, g.buf], scalar=float(D),
                                                 in1=stats[:, :].unsqueeze(2).to_broadcast([P, TG, D]),
                                                 op0=ALU.mult, op1=ALU.subtract).then_inc(ln, 1)
                    mask(r - 1, 1, 3)
                    if now:
                        vec.wait_ge(sq_done, g.n + 1)
                        vec.tensor_reduce(roots[:, :], squares[:, :, :], AX.X, ALU.add).then_inc(ln, 1)
                    g = r - 3
                    m = g.n * 5
                    sums = k.bank[2][:, 0:TG * (D + 1)].rearrange("p (t d) -> p t d", d=D + 1)
                    if done:
                        vec.wait_ge(rows_done, g.n + 1)
                        vec.tensor_scalar(deg[:, :], sums[:, :, D], 1.0, None, ALU.max).then_inc(updated, 1)
                        vec.tensor_copy(k.degree[:, bass.ds(g.n * TG, TG)], sums[:, :, D]).then_inc(updated, 1)
                    mask(r - 1, 4, 1)
                    if done:
                        vec.wait_ge(updated, m + 1)
                        vec.reciprocal(deg[:, :], deg[:, :]).then_inc(updated, 1)
                    mask(r - 1, 5, 1)
                    if done:
                        vec.wait_ge(updated, m + 3)
                        vec.tensor_tensor(part[:, :, :], sums[:, :, 0:D], deg[:, :].unsqueeze(2).to_broadcast([P, TG, D]),
                                          ALU.mult).then_inc(updated, 1)
                    if now:
                        vec.wait_ge(rooted, r.n + 1)
                        vec.reciprocal(inverse[:, :], roots[:, :]).then_inc(inverted, 1)
                    mask(r - 1, 6, 1)
                    if done:
                        vec.wait_ge(updated, m + 4)
                        if g.from_second():
                            vec.wait_ge(scattered[g.buf], g.half * (TG * 16))
                        vec.tensor_tensor(x2[:, g.buf], part[:, :, :], k.x_dst[:, bass.ds(g.n * TG, TG), :], ALU.add).then_inc(updated, 1)
                    if now:
                        vec.wait_ge(inverted, r.n + 1)
                        if r.from_second():
                            vec.wait_ge(turned, (r - 2).n + 1)
                        for side in range(2):
                            scale_rows(vec, ln, cen[:, :, :], inverse[:, :], h1[:, r.buf, :, side, :])
                    g = r - 2
                    if g.within(EG):
                        vec.wait_ge(msg_done, g.n + 1)
                        if g.from_second():
                            vec.wait_ge(rows_done, (g - 2).n + 1)
                        if g.from_first():
                            vec.wait_ge(scanned, g.n)
                        vec.tensor_tensor_scan(agg[:, g.buf, :], k.same[0:D + 1, bass.ds(g.n * GS, GS)], msg[:, g.buf, :],
                                               agg[:, (g - 1).buf, GS - 1:GS] if g.from_first() else 0.0,
                                               ALU.mult, ALU.add).then_inc(scanned, 1)
                    mask(r - 1, 7, 9)

                rounds(vec, EG, 3, step)

            @block.scalar
            def _(act):
                def step(r):
                    g = r
                    if g.within(EG):
                        act.wait_ge(ln, g.n * 5 + 2)
                        act.activation(squares[:, :, :], cen[:, :, :], ACT.Square, scale=0.125).then_inc(sq_done, 1)
                    g = r - 2
                    if g.within(EG):
                        act.wait_ge(z_used, (g.n + 1) * PAIRS)
                        if g.from_second():
                            act.wait_ge(scanned, (g - 2).n + 1)
                        act.activation(msg[0:D, g.buf, :], k.bank[3 + g.buf][0:D, :], ACT.Copy).then_inc(msg_done, 1)
                    g = r
                    if g.within(EG):
                        act.wait_ge(ln, g.n * 5 + 3)
                        act.activation(roots[:, :], roots[:, :], ACT.Sqrt, bias=k.eps_col[:, 0:1]).then_inc(rooted, 1)
                        act.wait_ge(turned, g.n + 1)
                        if g.from_second():
                            act.wait_ge(z_made, (g - 1).n * PAIRS)
                        act.activation(ht[:, g.buf, :], k.bank[0][:, :], ACT.Copy).then_inc(ht_done, 1)

                rounds(act, EG, 2, step)

            @block.tensor
            def _(pe):
                pe.wait_ge(wrel_in, 16)
                pe.sem_inc(k.pe_wait, 1)

                def messages(g, first, count):
                    if not g.within(EG):
                        return
                    if first == 0 and g.from_second():
                        pe.wait_ge(msg_done, (g - 1).n)
                    for n in range(first, first + count):
                        pe.wait_ge(z_made, g.n * PAIRS + n + 1)
                        pe.matmul(k.bank[3 + g.buf][0:D, :], wrel[:, n, :], z[:, n % NZ, :],
                                  start=n == 0, stop=n == PAIRS - 1).then_inc(z_used, 1)

                def step(r):
                    messages(r - 1, 0, 8)
                    g = r - 2
                    if g.within(EG):
                        pe.wait_ge(scanned, g.n + 1)
                        if g.from_first():
                            pe.wait_ge(updated, g.n * 5 - 1)
                        pe.sem_inc(k.pe_wait, 1)
                        for t in range(TG):
                            mm = pe.transpose(k.bank[2][:, t * (D + 1):(t + 1) * (D + 1)], agg[:, g.buf, t * P:(t + 1) * P],
                                              k.ident[0:D + 1, 0:D + 1])
                        mm.then_inc(rows_done, 1)
                    messages(r - 1, 8, 4)
                    g = r
                    if g.within(EG):
                        pe.wait_ge(ln, g.n * 5 + 5)
                        if g.from_first():
                            pe.wait_ge(ht_done, g.n)
                        pe.sem_inc(k.pe_wait, 1)
                        for t in range(TG):
                            mm = pe.transpose(k.bank[0][:, t * P:(t + 1) * P], h1[:, g.buf, t].rearrange("p s d -> p (s d)"),
                                              k.ident[:, :])
                        mm.then_inc(turned, 1)
                    messages(r - 1, 12, 4)

                rounds(pe, EG, 2, step)


def layer2(nc, k):
    with ExitStack() as ctx:
        def sb(name, shape, dt=F32):
            return k.sb(name, shape, dt, ctx)

        def sem(name):
            return k.sem(name, ctx)

        SIDES = 2 * TG
        xx = sb("l2_xx", [P, 2, TG, 2, D])
        h = sb("l2_h", [P, 2, TG, 2, D])
        squares = sb("l2_squares", [P, SIDES, D])
        h_squares = sb("l2_h_squares", [P, SIDES, D])
        stats = sb("l2_stats", [P, SIDES])
        roots = sb("l2_roots", [P, SIDES])
        inverse = sb("l2_inverse", [P, SIDES])
        prod = sb("l2_prod", [P, TG, D])
        dot = sb("l2_dot", [P, TG])
        norms = sb("l2_norms", [P, TG, 2])
        scale = sb("l2_scale", [P, TG])
        score = sb("l2_score", [P, TG])
        e = sb("l2_e", [P, 2, TG])
        v = sb("l2_v", [P, TG, D + 1])
        key_row = sb("l2_key_row", [P, 2, GS])
        equal = sb("l2_equal", [P, TG, GS])
        earlier = sb("l2_earlier", [P, TG, GS], BF16)
        junk = sb("l2_junk", [P, TG, GS], BF16)
        before = sb("l2_before", [P, TG])
        away = sb("l2_away", [P, TG])
        drop_i = sb("l2_drop_i", [P, TG], I32)
        drop = sb("l2_drop", [P, TG])
        sums = sb("l2_sums", [P, 2, TG, D + 1])
        src_ring = sb("l2_src_ring", [P, 2, TG], I32)
        dst_ring = sb("l2_dst_ring", [P, 2, TG], I32)
        add_ring = sb("l2_add_ring", [P, 2, TG], I32)

        gathered, kept, key_in = (k.pair_of_sems("l2_" + n, ctx) for n in ("gathered", "kept", "key_in"))
        ln, dots, packed = sem("l2_ln"), sem("l2_dots"), sem("l2_packed")
        sq_done, h_sq_done = sem("l2_sq_done"), sem("l2_h_sq_done")
        rooted, normed, inverted, exped = sem("l2_rooted"), sem("l2_normed"), sem("l2_inverted"), sem("l2_exped")
        summed, sums_out, added = sem("l2_summed"), sem("l2_sums_out"), sem("l2_added")
        consts, indexed = sem("l2_consts"), sem("l2_indexed")
        idx_copied = sem("l2_idx_copied")
        PACK = 6 + 2 * TG

        def sides(a, g):
            return a[:, g.buf].rearrange("p t s d -> p (t s) d")

        with nc.Block() as block:
            @block.sync
            def _(sp):
                def step(r):
                    g = r
                    if g.within(EG):
                        if g.from_second():
                            sp.wait_ge(packed, (g - 1).n * PACK)
                        sp.dma_start(key_row[:, g.buf, :], k.src_row[bass.ds(g.n * GS, GS)].partition_broadcast(P)
                                     ).then_inc(key_in[g.buf], 16)
                    g = r - 1
                    if g.within(EG):
                        sp.wait_ge(gathered[g.buf], (g.half + 1) * (2 * TG * 16))
                        sp.dma_start(k.x_src[:, bass.ds(g.n * TG, TG), :], xx[:, g.buf, :, 0, :]).then_inc(kept[g.buf], 16)

                rounds(sp, EG, 1, step)
                for b in range(2):
                    sp.wait_ge(kept[b], (EG + 1 - b) // 2 * 16)

            @block.gpsimd
            def _(pool):
                pool.memset(earlier[:, :, :], 1.0).then_inc(consts, 1)
                pool.iota(drop_i[:, :], pattern=[[P, TG]], base=NODES, channel_multiplier=1).then_inc(consts, 1)
                pool.wait_ge(consts, 2)
                pool.affine_select(out=earlier[:, :, :], in_=earlier[:, :, :], compare_op=ALU.is_gt, fill=0.0,
                                   base=0, pattern=[[P, TG], [-1, GS]], channel_multiplier=1).then_inc(consts, 1)

                def step(r):
                    g = r
                    if g.within(EG):
                        if g.from_second():
                            pool.wait_ge(ln, (g - 2).n * 4 + 2)
                            pool.wait_ge(kept[g.buf], g.half * 16)
                        gather_group(pool, g, ((xx[:, g.buf, :, 0, :], k.x2_table, k.src_idx, src_ring),
                                               (xx[:, g.buf, :, 1, :], k.x2_table, k.dst_idx, dst_ring)),
                                     idx_copied, gathered, k.pool_wait)
                    g = r - 3
                    if g.within(EG):
                        pool.wait_ge(sums_out, g.n + 1)
                        pool.wait_ge(indexed, g.n + 1)
                        if g.from_first():
                            pool.wait_ge(added, g.n * (TG * 16))
                        pool.sem_inc(k.pool_wait, 1)
                        for t in range(TG):
                            pool.indirect_dma_start(
                                k.sum_table[:, :], bass.IndirectOffsetOnAxis(ap=add_ring[:, g.buf, t:t + 1], axis=0),
                                sums[:, g.buf, t, :], None, compute_op=ALU.add).then_inc(added, 16)

                rounds(pool, EG, 3, step)
                pool.wait_ge(added, EG * TG * 16)

            @block.vector
            def _(vec):
                vec.wait_ge(consts, 3)
                vec.tensor_copy(drop[:, :], drop_i[:, :]).then_inc(consts, 1)

                def step(r):
                    g = r - 2
                    if g.within(EG):
                        vec.wait_ge(exped, g.n + 1)
                        if g.from_first():
                            vec.wait_ge(summed, g.n)
                        vec.tensor_tensor(v[:, :, 0:D], h[:, g.buf, :, 1, :], e[:, g.buf, :].unsqueeze(2).to_broadcast([P, TG, D]),
                                          ALU.mult).then_inc(packed, 1)
                        vec.tensor_copy(v[:, :, D], e[:, g.buf, :]).then_inc(packed, 1)
                        vec.wait_ge(key_in[g.buf], (g.half + 1) * 16)
                        key = k.src_key[:, bass.ds(g.n * TG, TG)]
                        vec.tensor_copy(away[:, :], key).then_inc(packed, 1)
                        vec.wait_ge(packed, g.n * PACK + 3)
                        for t in range(TG):
                            vec.tensor_scalar(equal[:, t, :], key_row[:, g.buf, :], away[:, t:t + 1], None,
                                              ALU.is_equal).then_inc(packed, 1)
                        for t in range(TG):
                            vec.wait_ge(packed, g.n * PACK + 4 + t)
                            vec.scalar_tensor_tensor(out=junk[:, t, :], in0=equal[:, t, :], scalar=1.0, in1=earlier[:, t, :],
                                                     op0=ALU.mult, op1=ALU.mult, accum_out=before[:, t:t + 1]).then_inc(packed, 1)
                        vec.wait_ge(packed, g.n * PACK + 3 + 2 * TG)
                        vec.tensor_scalar(before[:, :], before[:, :], 0.5, None, ALU.is_gt).then_inc(packed, 1)
                        vec.wait_ge(packed, g.n * PACK + 4 + 2 * TG)
                        vec.tensor_tensor(away[:, :], drop[:, :], away[:, :], ALU.subtract).then_inc(packed, 1)
                        vec.wait_ge(packed, g.n * PACK + 5 + 2 * TG)
                        vec.tensor_tensor(away[:, :], away[:, :], before[:, :], ALU.mult).then_inc(packed, 1)
                        vec.wait_ge(packed, g.n * PACK + 6 + 2 * TG)
                        if g.from_second():
                            vec.wait_ge(added, (g - 1).n * (TG * 16))
                        vec.tensor_tensor(add_ring[:, g.buf, :], away[:, :], key, ALU.add).then_inc(indexed, 1)
                    g = r
                    if g.within(EG):
                        vec.wait_ge(gathered[g.buf], (g.half + 1) * (2 * TG * 16))
                        center_rows(vec, ln, g.n * 4, sides(xx, g), stats[:, :], sides(h, g))
                    g = r - 1
                    if g.within(EG):
                        vec.tensor_tensor(prod[:, :, :], h[:, g.buf, :, 0, :], h[:, g.buf, :, 1, :], ALU.mult).then_inc(dots, 1)
                        vec.wait_ge(dots, g.n * 7 + 1)
                        vec.tensor_reduce(dot[:, :], prod[:, :, :], AX.X, ALU.add).then_inc(dots, 1)
                    g = r
                    if g.within(EG):
                        vec.wait_ge(sq_done, g.n + 1)
                        vec.tensor_reduce(roots[:, :], squares[:, :, :], AX.X, ALU.add).then_inc(ln, 1)
                    g = r - 1
                    if g.within(EG):
                        vec.wait_ge(h_sq_done, g.n + 1)
                        vec.tensor_reduce(norms[:, :, :].rearrange("p t s -> p (t s)"), h_squares[:, :, :], AX.X, ALU.add).then_inc(dots, 1)
                        vec.wait_ge(dots, g.n * 7 + 3)
                        vec.tensor_scalar(norms[:, :, :], norms[:, :, :], 1e-24, None, ALU.max).then_inc(dots, 1)
                    g = r
                    if g.within(EG):
                        vec.wait_ge(rooted, g.n + 1)
                        vec.reciprocal(inverse[:, :], roots[:, :]).then_inc(inverted, 1)
                        vec.wait_ge(inverted, g.n + 1)
                        scale_rows(vec, ln, sides(h, g), inverse[:, :], sides(h, g))
                    g = r - 1
                    if g.within(EG):
                        vec.wait_ge(normed, g.n + 1)
                        vec.tensor_tensor(scale[:, :], norms[:, :, 0], norms[:, :, 1], ALU.mult).then_inc(dots, 1)
                        vec.wait_ge(dots, g.n * 7 + 5)
                        vec.reciprocal(scale[:, :], scale[:, :]).then_inc(dots, 1)
                        vec.wait_ge(dots, g.n * 7 + 6)
                        if g.from_first():
                            vec.wait_ge(exped, g.n)
                        vec.tensor_tensor(score[:, :], dot[:, :], scale[:, :], ALU.mult).then_inc(dots, 1)

                rounds(vec, EG, 2, step)

            @block.scalar
            def _(act):
                def step(r):
                    g = r
                    if g.within(EG):
                        act.wait_ge(ln, g.n * 4 + 2)
                        act.activation(squares[:, :, :], sides(h, g), ACT.Square, scale=0.125).then_inc(sq_done, 1)
                    g = r - 1
                    if g.within(EG):
                        act.activation(h_squares[:, :, :], sides(h, g), ACT.Square).then_inc(h_sq_done, 1)
                    g = r
                    if g.within(EG):
                        act.wait_ge(ln, g.n * 4 + 3)
                        act.activation(roots[:, :], roots[:, :], ACT.Sqrt, bias=k.eps_col[:, 0:1]).then_inc(rooted, 1)
                    g = r - 1
                    if g.within(EG):
                        act.wait_ge(dots, g.n * 7 + 4)
                        act.activation(norms[:, :, :], norms[:, :, :], ACT.Sqrt).then_inc(normed, 1)
                    g = r - 2
                    if g.within(EG):
                        act.wait_ge(summed, g.n + 1)
                        if g.from_second():
                            act.wait_ge(added, (g - 1).n * (TG * 16))
                        act.activation(sums[:, g.buf], k.bank[0][:, 0:TG * (D + 1)].rearrange("p (t d) -> p t d", d=D + 1),
                                       ACT.Copy).then_inc(sums_out, 1)
                    g = r - 1
                    if g.within(EG):
                        act.wait_ge(dots, g.n * 7 + 7)
                        if g.from_second():
                            act.wait_ge(packed, (g - 1).n * PACK)
                        act.activation(e[:, g.buf, :], score[:, :], ACT.Exp).then_inc(exped, 1)

                rounds(act, EG, 2, step)

            @block.tensor
            def _(pe):
                def step(g):
                    pe.wait_ge(packed, g.n * PACK + 3 + TG)
                    if g.from_first():
                        pe.wait_ge(sums_out, g.n)
                    pe.sem_inc(k.pe_wait, 1)
                    for t in range(TG):
                        for u in range(TG):
                            mm = pe.matmul(k.bank[0][:, t * (D + 1):(t + 1) * (D + 1)], equal[:, u, t * P:(t + 1) * P],
                                           v[:, u, :], start=u == 0, stop=u == TG - 1)
                    mm.then_inc(summed, 1)

                rounds(pe, EG, 0, step)


def layer3(nc, k):
    with ExitStack() as ctx:
        def sb(name, shape, dt=F32):
            return k.sb(name, shape, dt, ctx)

        def sem(name):
            return k.sem(name, ctx)

        ss = sb("l3_ss", [P, 2, TG, D + 1])
        total = sb("l3_total", [P, TG])
        change = sb("l3_change", [P, TG, D])
        x3 = sb("l3_x3", [P, TG, D])
        x2 = sb("l3_x2", [NP, 2, NG, D])
        node_sums = sb("l3_node_sums", [NP, 2, NG, D + 1])
        node_total = sb("l3_node_total", [NP, NG])
        outs = sb("l3_outs", [NP, 2, NG, D])
        h = sb("l3_h", [P, 2, TG, D])
        squares = sb("l3_squares", [P, 2, TG, D])
        stats = sb("l3_stats", [P, 2, TG])
        roots = sb("l3_roots", [P, 2, TG])
        inverse = sb("l3_inverse", [P, 2, TG])
        ht = sb("l3_ht", [D, GS])
        msg = sb("l3_msg", [D, 2, GS])
        agg = sb("l3_agg", [D, 2, GS])
        deg = sb("l3_deg", [P, TG])
        mean = sb("l3_mean", [P, TG, D])
        y = sb("l3_y", [P, TG, D])
        src_ring = sb("l3_src_ring", [P, 2, TG], I32)

        gathered = k.pair_of_sems("l3_gathered", ctx)
        nodes_in, out_stored, outed = k.pair_of_sems("l3_nodes_in", ctx), k.pair_of_sems("l3_out_stored", ctx), sem("l3_outed")
        lna, lnb = sem("l3_lna"), sem("l3_lnb")
        sqa_done, sqb_done, rooted_a, rooted_b, inverted_a, inverted_b = (
            sem("l3_" + n) for n in ("sqa_done", "sqb_done", "rooted_a", "rooted_b", "inverted_a", "inverted_b"))
        turned, ht_done, m_done, msg_done = sem("l3_turned"), sem("l3_ht_done"), sem("l3_m"), sem("l3_msg_done")
        scanned, rows_done = sem("l3_scanned"), sem("l3_rows")
        idx_copied = sem("l3_idx_copied")

        def x_dst(g):
            return k.x_dst[:, bass.ds(g.n * TG, TG), :]

        def x_src(g):
            return k.x_src[:, bass.ds(g.n * TG, TG), :]

        def nodes(a, g):
            return a[0:NODES, :].rearrange("(p j) d -> p j d", p=NP)[:, bass.ds(g.n * NG, NG), :]

        with nc.Block() as block:
            @block.sync
            def _(sp):
                def step(r):
                    g = r
                    if g.within(DG):
                        if g.from_second():
                            sp.wait_ge(outed, (g - 2).n * 5 + 5)
                        sp.dma_start(x2[:, g.buf], nodes(k.x2_table, g)).then_inc(nodes_in[g.buf], 16)
                        sp.dma_start(node_sums[:, g.buf], nodes(k.sum_table, g)).then_inc(nodes_in[g.buf], 16)
                    g = r - 1
                    if g.within(DG):
                        sp.wait_ge(outed, g.n * 5 + 5)
                        sp.dma_start(nodes(k.out, g), outs[:, g.buf]).then_inc(out_stored[g.buf], 16)

                rounds(sp, DG, 1, step)
                for b in range(2):
                    sp.wait_ge(out_stored[b], (DG + 1 - b) // 2 * 16)

            @block.gpsimd
            def _(pool):
                def step(r):
                    g = r
                    if g.within(EG):
                        if g.from_second():
                            pool.wait_ge(lna, (g - 2).n * 8 + 3)
                        gather_group(pool, g, ((ss[:, g.buf], k.sum_table, k.src_idx, src_ring),),
                                     idx_copied, gathered, k.pool_wait)

                rounds(pool, EG, 0, step)

            @block.vector
            def _(vec):
                def step(r):
                    edges, of_nodes = r.within(EG), r.within(DG)
                    g = r
                    n, m = g.n * 8, g.n * 5
                    if edges:
                        vec.wait_ge(gathered[g.buf], (g.half + 1) * (TG * 16))
                        vec.tensor_scalar(total[:, :], ss[:, g.buf, :, D], TINY, None, ALU.max).then_inc(lna, 1)
                    if of_nodes:
                        vec.wait_ge(nodes_in[g.buf], (g.half + 1) * 32)
                        vec.tensor_scalar(node_total[:, :], node_sums[:, g.buf, :, D], TINY, None, ALU.max).then_inc(outed, 1)
                    if edges:
                        vec.wait_ge(lna, n + 1)
                        vec.reciprocal(total[:, :], total[:, :]).then_inc(lna, 1)
                    if of_nodes:
                        vec.wait_ge(outed, m + 1)
                        vec.reciprocal(node_total[:, :], node_total[:, :]).then_inc(outed, 1)
                    if edges:
                        vec.wait_ge(lna, n + 2)
                        vec.tensor_tensor(change[:, :, :], ss[:, g.buf, :, 0:D],
                                          total[:, :].unsqueeze(2).to_broadcast([P, TG, D]), ALU.mult).then_inc(lna, 1)
                    if of_nodes:
                        vec.wait_ge(outed, m + 2)
                        if g.from_second():
                            vec.wait_ge(out_stored[g.buf], g.half * 16)
                        vec.tensor_tensor(outs[:, g.buf], node_sums[:, g.buf, :, 0:D],
                                          node_total[:, :].unsqueeze(2).to_broadcast([NP, NG, D]), ALU.mult).then_inc(outed, 1)
                    if edges:
                        vec.wait_ge(lna, n + 3)
                        vec.tensor_tensor(x3[:, :, :], change[:, :, :], x_src(g), ALU.add).then_inc(lna, 1)
                        vec.wait_ge(lna, n + 4)
                        if g.from_second():
                            vec.wait_ge(turned, (g - 2).n + 1)
                        vec.tensor_reduce(stats[:, 0, :], x3[:, :, :], AX.X, ALU.add).then_inc(lna, 1)
                    last = r - 3
                    means, k3 = last.within(EG), last.n * 8
                    if means:
                        vec.tensor_scalar(deg[:, :], k.degree[:, bass.ds(last.n * TG, TG)], 1e-6, None, ALU.add).then_inc(lnb, 1)
                    if edges:
                        vec.wait_ge(lna, n + 5)
                        vec.scalar_tensor_tensor(out=h[:, r.buf], in0=x3[:, :, :], scalar=float(D),
                                                 in1=stats[:, 0, :].unsqueeze(2).to_broadcast([P, TG, D]),
                                                 op0=ALU.mult, op1=ALU.subtract).then_inc(lna, 1)
                    if means:
                        vec.wait_ge(lnb, k3 + 1)
                        vec.reciprocal(deg[:, :], deg[:, :]).then_inc(lnb, 1)
                    if of_nodes:
                        vec.wait_ge(outed, m + 3)
                        vec.tensor_tensor(outs[:, r.buf], outs[:, r.buf], x2[:, r.buf], ALU.add).then_inc(outed, 1)
                    if edges:
                        vec.wait_ge(sqa_done, r.n + 1)
                        vec.tensor_reduce(roots[:, 0, :], squares[:, 0], AX.X, ALU.add).then_inc(lna, 1)
                    if means:
                        vec.wait_ge(lnb, k3 + 2)
                        vec.wait_ge(rows_done, last.n + 1)
                        vec.scalar_tensor_tensor(out=mean[:, :, :], in0=k.bank[2][:, 0:TG * D].rearrange("p (t d) -> p t d", d=D),
                                                 scalar=0.0, in1=deg[:, :].unsqueeze(2).to_broadcast([P, TG, D]),
                                                 op0=ALU.max, op1=ALU.mult).then_inc(lnb, 1)
                        vec.wait_ge(lnb, k3 + 3)
                        vec.tensor_reduce(stats[:, 1, :], mean[:, :, :], AX.X, ALU.add).then_inc(lnb, 1)
                    if edges:
                        vec.wait_ge(rooted_a, r.n + 1)
                        vec.reciprocal(inverse[:, 0, :], roots[:, 0, :]).then_inc(inverted_a, 1)
                    if means:
                        vec.wait_ge(lnb, k3 + 4)
                        vec.scalar_tensor_tensor(out=y[:, :, :], in0=mean[:, :, :], scalar=float(D),
                                                 in1=stats[:, 1, :].unsqueeze(2).to_broadcast([P, TG, D]),
                                                 op0=ALU.mult, op1=ALU.subtract).then_inc(lnb, 1)
                    if edges:
                        vec.wait_ge(inverted_a, r.n + 1)
                        scale_rows(vec, lna, h[:, r.buf], inverse[:, 0, :], h[:, r.buf])
                    g = r - 2
                    if g.within(EG):
                        vec.wait_ge(msg_done, g.n + 1)
                        if g.from_second():
                            vec.wait_ge(rows_done, (g - 2).n + 1)
                        if g.from_first():
                            vec.wait_ge(scanned, g.n)
                        vec.tensor_tensor_scan(agg[:, g.buf, :], k.same[0:D, bass.ds(g.n * GS, GS)], msg[:, g.buf, :],
                                               agg[:, (g - 1).buf, GS - 1:GS] if g.from_first() else 0.0,
                                               ALU.mult, ALU.add).then_inc(scanned, 1)
                    if means:
                        vec.wait_ge(sqb_done, last.n + 1)
                        vec.tensor_reduce(roots[:, 1, :], squares[:, 1], AX.X, ALU.add).then_inc(lnb, 1)
                    if of_nodes:
                        vec.wait_ge(outed, m + 4)
                        vec.tensor_tensor(outs[:, r.buf], outs[:, r.buf],
                                          k.beta_b[0:NP, :].unsqueeze(1).to_broadcast([NP, NG, D]), ALU.add).then_inc(outed, 1)
                    if means:
                        vec.wait_ge(rooted_b, last.n + 1)
                        vec.reciprocal(inverse[:, 1, :], roots[:, 1, :]).then_inc(inverted_b, 1)
                        vec.wait_ge(inverted_b, last.n + 1)
                        scale_rows(vec, lnb, y[:, :, :], inverse[:, 1, :], y[:, :, :], relu=False)
                        vec.wait_ge(lnb, k3 + 7)
                        vec.tensor_tensor(x_dst(last), y[:, :, :], k.gamma_b[:, :].unsqueeze(1).to_broadcast([P, TG, D]),
                                          ALU.mult).then_inc(lnb, 1)

                rounds(vec, EG, 3, step)

            @block.scalar
            def _(act):
                def step(r):
                    for m, g, ln, centered, sq_done, rooted in ((0, r, lna, 6, sqa_done, rooted_a),
                                                                (1, r - 3, lnb, 5, sqb_done, rooted_b)):
                        if g.within(EG):
                            act.wait_ge(ln, g.n * 8 + centered)
                            act.activation(squares[:, m], h[:, g.buf] if m == 0 else y[:, :, :], ACT.Square,
                                           scale=0.125).then_inc(sq_done, 1)
                            act.wait_ge(ln, g.n * 8 + centered + 1)
                            act.activation(roots[:, m, :], roots[:, m, :], ACT.Sqrt, bias=k.eps_col[:, 0:1]).then_inc(rooted, 1)
                    g = r
                    if g.within(EG):
                        act.wait_ge(turned, g.n + 1)
                        if g.from_first():
                            act.wait_ge(m_done, g.n)
                        act.activation(ht[:, :], k.bank[0][0:D, :], ACT.Copy).then_inc(ht_done, 1)
                        act.wait_ge(m_done, g.n + 1)
                        if g.from_second():
                            act.wait_ge(scanned, (g - 2).n + 1)
                        act.activation(msg[:, g.buf, :], k.bank[1][0:D, :], ACT.Identity, bias=k.b3c[:, 0:1]).then_inc(msg_done, 1)

                rounds(act, EG, 3, step)

            @block.tensor
            def _(pe):
                def step(r):
                    g = r
                    if g.within(EG):
                        pe.wait_ge(lna, g.n * 8 + 8)
                        if g.from_first():
                            pe.wait_ge(ht_done, g.n)
                        pe.sem_inc(k.pe_wait, 1)
                        for t in range(TG):
                            mm = pe.transpose(k.bank[0][0:D, t * P:(t + 1) * P], h[:, g.buf, t, :], k.ident[:, :])
                        mm.then_inc(turned, 1)
                    g = r - 2
                    if g.within(EG):
                        pe.wait_ge(scanned, g.n + 1)
                        if g.from_first():
                            pe.wait_ge(lnb, g.n * 8 - 5)
                        pe.sem_inc(k.pe_wait, 1)
                        for t in range(TG):
                            mm = pe.transpose(k.bank[2][:, t * D:(t + 1) * D], agg[:, g.buf, t * P:(t + 1) * P], k.ident[0:D, 0:D])
                        mm.then_inc(rows_done, 1)
                    g = r
                    if g.within(EG):
                        pe.wait_ge(ht_done, g.n + 1)
                        if g.from_first():
                            pe.wait_ge(msg_done, g.n)
                        pe.sem_inc(k.pe_wait, 1)
                        pe.matmul(k.bank[1][0:D, :], k.w3[:, :], ht[:, :], start=True, stop=True).then_inc(m_done, 1)

                rounds(pe, EG, 2, step)


def write_last(nc, k):
    with ExitStack() as ctx:
        rows = k.sb("out_rows", [P, 2, TG, D], F32, ctx)
        last_ring = k.sb("out_last_ring", [P, 2, TG], I32, ctx)
        copied, idx_copied = k.sem("out_copied", ctx), k.sem("out_idx_copied", ctx)
        scattered = k.pair_of_sems("out_scattered", ctx)

        with nc.Block() as block:
            @block.scalar
            def _(act):
                def step(g):
                    if g.from_second():
                        act.wait_ge(scattered[g.buf], g.half * (TG * 16))
                        act.sem_inc(k.act_wait, 1)
                    act.activation(rows[:, g.buf], k.x_dst[:, bass.ds(g.n * TG, TG), :], ACT.Copy).then_inc(copied, 1)

                rounds(act, EG, 0, step)

            @block.gpsimd
            def _(pool):
                def step(g):
                    scatter_group(pool, g, rows, copied, g.n + 1, k.out, k.last_idx, last_ring, idx_copied, scattered, k.pool_wait,
                                  compute_op=ALU.add)

                rounds(pool, EG, 0, step)
                for b in range(2):
                    pool.wait_ge(scattered[b], (EG + 1 - b) // 2 * TG * 16)


_INS = ["x", "src", "dst", "edge_attr_32", "edge_type_32", "L0_gnn_w_m1", "L0_gnn_b_m1", "L0_gnn_w_m2",
        "L0_gnn_b_m2", "L0_gnn_w_u1", "L0_gnn_b_u1", "L0_gnn_w_u2", "L0_gnn_b_u2", "L1_gnn_basis",
        "L1_gnn_coeff", "L1_gnn_self_weight", "L1_gnn_bias", "L3_gnn_W", "L3_gnn_b", "L3_gnn_gamma",
        "L3_gnn_beta"]
_TURNED = ("L1_gnn_coeff", "L3_gnn_W")


def kernel(**inputs):
    import numpy as _np
    import concourse.bacc as _bacc
    from concourse import mybir as _mybir
    from concourse.bass_utils import run_bass_kernel_spmd as _run

    nc = _bacc.Bacc("TRN2", target_bir_lowering=False, num_devices=1)
    arrays, args = {}, []
    for name in _INS:
        a = _np.asarray(inputs[name])
        a = _np.ascontiguousarray(a.T if name in _TURNED else a)
        arrays[f"in_{name}_dram"] = a
        args.append(nc.dram_tensor(f"in_{name}_dram", a.shape, _mybir.dt.from_np(a.dtype), kind="ExternalInput").ap())
    out = nc.dram_tensor("out_0_dram", (NODES, D), _mybir.dt.float32, kind="ExternalOutput").ap()
    build(nc, *args, out)
    r = _run(nc, [arrays], core_ids=[0])
    return r.results[0]["out_0_dram"]
```
